# Optimizing a Trainium2 kernel written in Bass

```python
import numpy as np
import jax
import jax.numpy as jnp

def _softmax(x, axis=-1):
    return jax.nn.softmax(x, axis=axis)

def _gelu(x):
    return jax.nn.gelu(x, approximate=True)

def _silu(x):
    return jax.nn.silu(x)

def _sigmoid(x):
    return jax.nn.sigmoid(x)

def _layernorm(x, axis=-1, eps=1e-05):
    m = jnp.mean(x, axis=axis, keepdims=True)
    v = jnp.var(x, axis=axis, keepdims=True)
    return (x - m) / jnp.sqrt(v + eps)

def _scatter_add(tgt, idx, src, axis=0):
    return tgt.at[idx].add(src)

def _segment_sum(src, seg, n):
    return jax.ops.segment_sum(src, seg, n)
kernel_name = 'mk_decoder_postln_d2_seqx_r8_eea604'

def setup_inputs(seed: int=0):
    np.random.seed(seed)
    _w = jnp.asarray

    def _rec_inputs():
        import jax
        import jax.numpy as jnp
        _rk = jax.random.key(seed)
        x = 7.22e-05 + 1 * jax.random.normal(jax.random.fold_in(_rk, 1), (32, 64, 256), jnp.float32)
        _lenS = 64 - jax.random.randint(jax.random.fold_in(_rk, 7), (32,), 0, max(1, 64 // 4) + 1, jnp.int32)
        _lenS2 = 64 - jax.random.randint(jax.random.fold_in(_rk, 8), (32,), 0, max(1, 64 // 4) + 1, jnp.int32)
        _ctx_512P = jax.random.normal(jax.random.fold_in(_rk, 11), (32, 16, 64), jnp.float32)
        _ctx_512c = jax.random.dirichlet(jax.random.fold_in(_rk, 511), 0.3 * jnp.ones((16,), jnp.float32), (32, 64))
        _ctx_512t = jnp.einsum('bsk,bkd->bsd', _ctx_512c, _ctx_512P)
        _ctx_512t = _ctx_512t * jax.lax.rsqrt(jnp.mean(jnp.square(_ctx_512t)) + 1e-12) * 0.953939
        ctx_512 = -0.000514642 + 1.00011 * (_ctx_512t + 0.3 * jax.random.normal(jax.random.fold_in(_rk, 611), (32, 64, 64), jnp.float32))
        return (x, ctx_512)
    x, ctx_512 = _rec_inputs()

    def _L0_attn_setup():
        import jax, jax.numpy as jnp
        import numpy as np
        HID = 256
        HEADS = 16
        HD = HID // HEADS
        EPS = 1e-06

        def _heads(x, b, s):
            return x.reshape(b, s, HEADS, HD).transpose(0, 2, 1, 3)
        key = jax.random.key(seed)
        ks = jax.random.split(key, 9)
        s = 1.0 / np.sqrt(HID)
        return {'hidden_states': jax.random.normal(ks[0], (4, 512, HID), jnp.float32), 'q_w': jax.random.normal(ks[1], (HID, HID), jnp.float32) * s, 'q_b': jnp.zeros((HID,), jnp.float32), 'k_w': jax.random.normal(ks[2], (HID, HID), jnp.float32) * s, 'k_b': jnp.zeros((HID,), jnp.float32), 'v_w': jax.random.normal(ks[3], (HID, HID), jnp.float32) * s, 'v_b': jnp.zeros((HID,), jnp.float32), 'o_w': jax.random.normal(ks[4], (HID, HID), jnp.float32) * s, 'o_b': jnp.zeros((HID,), jnp.float32)}
    _L0_attn_all = _L0_attn_setup()
    _L0_attn_in = {k: v for k, v in _L0_attn_all.items() if k in ('q_w', 'q_b', 'k_w', 'k_b', 'v_w', 'v_b', 'o_w', 'o_b')}
    del _L0_attn_all

    def _L0_xattn_setup():
        import jax, jax.numpy as jnp
        import numpy as np
        N_HEADS = 16
        N_KV_HEADS = 4
        ROPE_THETA = 10000.0
        EPS = 1e-05

        def _rms_norm(x, w):
            var = jnp.mean(x * x, axis=-1, keepdims=True)
            return x * jax.lax.rsqrt(var + EPS) * w

        def _rope_sin_cos(T, head_dim, dtype):
            inv_freq = 1.0 / ROPE_THETA ** (jnp.arange(0, head_dim, 2, dtype=jnp.float32) / head_dim)
            t = jnp.arange(T, dtype=jnp.float32)
            freqs = jnp.outer(t, inv_freq)
            emb = jnp.concatenate([freqs, freqs], -1)
            return (jnp.sin(emb).astype(dtype)[None, None], jnp.cos(emb).astype(dtype)[None, None])

        def _rotate_half(x):
            h = x.shape[-1] // 2
            x1, x2 = (x[..., :h], x[..., h:])
            return jnp.concatenate([-x2, x1], axis=-1)
        key = jax.random.key(seed)
        ks = jax.random.split(key, 6)
        B, T, C = (2, 256, 256)
        Ckv = C // N_HEADS * N_KV_HEADS
        return {'q': jax.random.normal(ks[0], (B, T, C), jnp.float32), 'k': jax.random.normal(ks[1], (B, T, Ckv), jnp.float32), 'v': jax.random.normal(ks[2], (B, T, Ckv), jnp.float32), 'q_norm_w': jnp.ones((C,), jnp.float32), 'k_norm_w': jnp.ones((Ckv,), jnp.float32), 'w_out': jax.random.normal(ks[3], (C, C), jnp.float32) * C ** (-0.5)}
    _L0_xattn_all = _L0_xattn_setup()
    _L0_xattn_in = {k: v for k, v in _L0_xattn_all.items() if k in ('q_norm_w', 'k_norm_w', 'w_out')}
    del _L0_xattn_all

    def _L0_ffn_setup():
        import jax, jax.numpy as jnp
        import numpy as np
        B, S, HID = (2, 256, 256)
        NUM_HEADS = 16
        HEAD_DIM = HID // NUM_HEADS
        NUM_EXPERTS = 8
        TOP_K = 2
        INTER = 512
        EPS = 1e-05

        def _rmsnorm(x, w, eps=EPS):
            return x * jax.lax.rsqrt(jnp.mean(x * x, axis=-1, keepdims=True) + eps) * w

        def _moe(x_flat, Wr, Wg, Wu, Wd):
            T = x_flat.shape[0]
            logits = x_flat @ Wr.T
            top_logits, top_idx = jax.lax.top_k(logits, TOP_K)
            probs = jax.nn.softmax(top_logits, axis=-1)
            cw = jnp.zeros((T, NUM_EXPERTS), x_flat.dtype)
            cw = cw.at[jnp.arange(T)[:, None], top_idx].add(probs)
            hg = jnp.einsum('eih,th->eti', Wg, x_flat)
            hu = jnp.einsum('eih,th->eti', Wu, x_flat)
            y = jnp.einsum('ehi,eti->eth', Wd, jax.nn.silu(hg) * hu)
            return jnp.einsum('eth,te->th', y, cw)
        key = jax.random.key(seed)
        ks = jax.random.split(key, 12)
        sd_h = 1.0 / np.sqrt(HID)
        sd_i = 1.0 / np.sqrt(INTER)
        return {'x': jax.random.normal(ks[0], (B, S, HID), jnp.float32), 'Wq': jax.random.normal(ks[1], (HID, HID), jnp.float32) * sd_h, 'Wk': jax.random.normal(ks[2], (HID, HID), jnp.float32) * sd_h, 'Wv': jax.random.normal(ks[3], (HID, HID), jnp.float32) * sd_h, 'Wo': jax.random.normal(ks[4], (HID, HID), jnp.float32) * sd_h, 'w_ln1': jnp.ones((HID,), jnp.float32), 'w_ln2': jnp.ones((HID,), jnp.float32), 'Wr': jax.random.normal(ks[5], (NUM_EXPERTS, HID), jnp.float32) * sd_h, 'Wg': jax.random.normal(ks[6], (NUM_EXPERTS, INTER, HID), jnp.float32) * sd_h, 'Wu': jax.random.normal(ks[7], (NUM_EXPERTS, INTER, HID), jnp.float32) * sd_h, 'Wd': jax.random.normal(ks[8], (NUM_EXPERTS, HID, INTER), jnp.float32) * sd_i}
    _L0_ffn_all = _L0_ffn_setup()
    _L0_ffn_in = {k: v for k, v in _L0_ffn_all.items() if k in ('Wq', 'Wk', 'Wv', 'Wo', 'w_ln1', 'w_ln2', 'Wr', 'Wg', 'Wu', 'Wd')}
    del _L0_ffn_all

    def _L1_attn_setup():
        import math
        import jax, jax.numpy as jnp
        import numpy as np
        MODEL_DIM = 256
        N_HEADS = 32
        N_GROUPS = 8
        R = N_HEADS // N_GROUPS
        HEAD_DIM = MODEL_DIM // N_HEADS
        KV_DIM = MODEL_DIM // R
        B, S = (1, 256)
        key = jax.random.key(seed)
        k1, k2, k3 = jax.random.split(key, 3)
        scale = 0.02
        return {'x': jax.random.normal(k1, (B, S, MODEL_DIM), dtype=jnp.float32), 'w_qkv': jax.random.normal(k2, (MODEL_DIM + 2 * KV_DIM, MODEL_DIM), dtype=jnp.float32) * scale, 'b_qkv': jnp.zeros((MODEL_DIM + 2 * KV_DIM,), dtype=jnp.float32), 'w_out': jax.random.normal(k3, (MODEL_DIM, MODEL_DIM), dtype=jnp.float32) * scale, 'b_out': jnp.zeros((MODEL_DIM,), dtype=jnp.float32)}
    _L1_attn_all = _L1_attn_setup()
    _L1_attn_in = {k: v for k, v in _L1_attn_all.items() if k in ('w_qkv', 'b_qkv', 'w_out', 'b_out')}
    del _L1_attn_all

    def _L1_xattn_setup():
        import jax, jax.numpy as jnp
        import numpy as np
        B, S, L = (2, 128, 128)
        DIM_Q, H, K, D_C, D_CQ, R = (256, 16, 128, 64, 192, 64)

        def _rope_tables(length, dim):
            inv = 1.0 / 10000.0 ** (jnp.arange(0, dim, 2, dtype=jnp.float32) / dim)
            f = jnp.arange(length, dtype=jnp.float32)[:, None] * inv[None, :]
            sin = jnp.repeat(jnp.sin(f), 2, axis=-1)
            cos = jnp.repeat(jnp.cos(f), 2, axis=-1)
            return (sin, cos)

        def _rotate_half(x):
            half = x.shape[-1] // 2
            return jnp.concatenate([-x[..., half:], x[..., :half]], axis=-1)

        def _apply_rope(x, sin, cos):
            return x * cos + _rotate_half(x) * sin
        key = jax.random.key(seed)
        ks = jax.random.split(key, 8)
        return {'hidden_q': jax.random.normal(ks[0], (B, S, DIM_Q), jnp.float32), 'kv_c': jax.random.normal(ks[1], (B, L, D_C), jnp.float32), 'Wq': jax.random.normal(ks[2], (H * K, DIM_Q), jnp.float32) / np.sqrt(DIM_Q).astype(np.float32), 'w_kc_q': jax.random.normal(ks[3], (H, K, D_CQ), jnp.float32) / np.sqrt(K).astype(np.float32), 'w_kc_kv': jax.random.normal(ks[4], (H, K, D_C), jnp.float32) / np.sqrt(K).astype(np.float32), 'W_qr': jax.random.normal(ks[5], (H, D_CQ, R), jnp.float32) / np.float32(np.sqrt(D_CQ) * np.sqrt(R)), 'W_kr': jax.random.normal(ks[6], (H, D_C, R), jnp.float32) / np.sqrt(D_C).astype(np.float32), 'Wo': jax.random.normal(ks[7], (DIM_Q, H * K), jnp.float32) / np.sqrt(H * K).astype(np.float32)}
    _L1_xattn_all = _L1_xattn_setup()
    _L1_xattn_in = {k: v for k, v in _L1_xattn_all.items() if k in ('Wq', 'w_kc_q', 'w_kc_kv', 'W_qr', 'W_kr', 'Wo')}
    del _L1_xattn_all

    def _L1_ffn_setup():
        import jax, jax.numpy as jnp
        import numpy as np
        EPS_NORM = 1e-06
        EPS_Q = 1e-08
        QB = 127.0

        def _ternary_quantize(w):
            scale = jnp.maximum(jnp.mean(jnp.abs(w)), EPS_Q)
            w_q = jnp.clip(jnp.round(w / scale), -1.0, 1.0)
            return (w_q, scale)

        def _activation_quant(x):
            gamma = jnp.maximum(jnp.max(jnp.abs(x), axis=-1, keepdims=True), EPS_Q)
            x_q = jnp.clip(jnp.round(x * QB / gamma), -QB, QB)
            return (x_q, gamma / QB)

        def _rmsnorm(x, weight):
            out = x * jax.lax.rsqrt(jnp.mean(x * x, axis=-1, keepdims=True) + EPS_NORM)
            return out * weight
        key = jax.random.key(seed)
        dim, expansion = (256, 4)
        hidden = dim * expansion
        B, S = (4, 512)
        k1, k2, k3 = jax.random.split(key, 3)
        x = jax.random.normal(k1, (B, S, dim), dtype=jnp.float32)
        weight_up = jax.random.normal(k2, (hidden, dim), dtype=jnp.float32) * 0.02
        weight_down = jax.random.normal(k3, (dim, hidden), dtype=jnp.float32) * 0.02
        norm_weight = jnp.ones((dim,), dtype=jnp.float32)
        gamma = jnp.full((dim,), 1e-05, dtype=jnp.float32)
        return {'x': x, 'weight_up': weight_up, 'weight_down': weight_down, 'norm_weight': norm_weight, 'gamma': gamma}
    _L1_ffn_all = _L1_ffn_setup()
    _L1_ffn_in = {k: v for k, v in _L1_ffn_all.items() if k in ('weight_up', 'weight_down', 'norm_weight', 'gamma')}
    del _L1_ffn_all
    return {'x': x, 'ctx_512': ctx_512, 'L0_attn_q_w': _L0_attn_in['q_w'], 'L0_attn_q_b': _L0_attn_in['q_b'], 'L0_attn_k_w': _L0_attn_in['k_w'], 'L0_attn_k_b': _L0_attn_in['k_b'], 'L0_attn_v_w': _L0_attn_in['v_w'], 'L0_attn_v_b': _L0_attn_in['v_b'], 'L0_attn_o_w': _L0_attn_in['o_w'], 'L0_attn_o_b': _L0_attn_in['o_b'], 'L0_xattn_q_norm_w': _L0_xattn_in['q_norm_w'], 'L0_xattn_k_norm_w': _L0_xattn_in['k_norm_w'], 'L0_xattn_w_out': _L0_xattn_in['w_out'], 'L0_ffn_Wq': _L0_ffn_in['Wq'], 'L0_ffn_Wk': _L0_ffn_in['Wk'], 'L0_ffn_Wv': _L0_ffn_in['Wv'], 'L0_ffn_Wo': _L0_ffn_in['Wo'], 'L0_ffn_w_ln1': _L0_ffn_in['w_ln1'], 'L0_ffn_w_ln2': _L0_ffn_in['w_ln2'], 'L0_ffn_Wr': _L0_ffn_in['Wr'], 'L0_ffn_Wg': _L0_ffn_in['Wg'], 'L0_ffn_Wu': _L0_ffn_in['Wu'], 'L0_ffn_Wd': _L0_ffn_in['Wd'], 'L1_attn_w_qkv': _L1_attn_in['w_qkv'], 'L1_attn_b_qkv': _L1_attn_in['b_qkv'], 'L1_attn_w_out': _L1_attn_in['w_out'], 'L1_attn_b_out': _L1_attn_in['b_out'], 'L1_xattn_Wq': _L1_xattn_in['Wq'], 'L1_xattn_w_kc_q': _L1_xattn_in['w_kc_q'], 'L1_xattn_w_kc_kv': _L1_xattn_in['w_kc_kv'], 'L1_xattn_W_qr': _L1_xattn_in['W_qr'], 'L1_xattn_W_kr': _L1_xattn_in['W_kr'], 'L1_xattn_Wo': _L1_xattn_in['Wo'], 'L1_ffn_weight_up': _L1_ffn_in['weight_up'], 'L1_ffn_weight_down': _L1_ffn_in['weight_down'], 'L1_ffn_norm_weight': _L1_ffn_in['norm_weight'], 'L1_ffn_gamma': _L1_ffn_in['gamma']}

def reference(x, ctx_512, L0_attn_q_w, L0_attn_q_b, L0_attn_k_w, L0_attn_k_b, L0_attn_v_w, L0_attn_v_b, L0_attn_o_w, L0_attn_o_b, L0_xattn_q_norm_w, L0_xattn_k_norm_w, L0_xattn_w_out, L0_ffn_Wq, L0_ffn_Wk, L0_ffn_Wv, L0_ffn_Wo, L0_ffn_w_ln1, L0_ffn_w_ln2, L0_ffn_Wr, L0_ffn_Wg, L0_ffn_Wu, L0_ffn_Wd, L1_attn_w_qkv, L1_attn_b_qkv, L1_attn_w_out, L1_attn_b_out, L1_xattn_Wq, L1_xattn_w_kc_q, L1_xattn_w_kc_kv, L1_xattn_W_qr, L1_xattn_W_kr, L1_xattn_Wo, L1_ffn_weight_up, L1_ffn_weight_down, L1_ffn_norm_weight, L1_ffn_gamma):
    import jax
    import jax.numpy as jnp

    def _L0_attn_ref(hidden_states, q_w, q_b, k_w, k_b, v_w, v_b, o_w, o_b):
        import jax, jax.numpy as jnp
        import numpy as np
        HID = 256
        HEADS = 16
        HD = HID // HEADS
        EPS = 1e-06

        def _heads(x, b, s):
            return x.reshape(b, s, HEADS, HD).transpose(0, 2, 1, 3)
        b, s, _ = hidden_states.shape
        q = _heads(hidden_states @ q_w.T + q_b, b, s)
        k = _heads(hidden_states @ k_w.T + k_b, b, s)
        v = _heads(hidden_states @ v_w.T + v_b, b, s)
        qp = jax.nn.elu(q) + 1.0
        kp = jax.nn.elu(k) + 1.0
        kv = jnp.einsum('bhsd,bhse->bhde', kp, v)
        z = jnp.einsum('bhsd,bhd->bhs', qp, kp.sum(axis=2))[..., None]
        attn = jnp.einsum('bhsd,bhde->bhse', qp, kv) / (z + EPS)
        out = attn.transpose(0, 2, 1, 3).reshape(b, s, HID)
        return out @ o_w.T + o_b

    def _L0_xattn_ref(q, k, v, q_norm_w, k_norm_w, w_out):
        import jax, jax.numpy as jnp
        import numpy as np
        N_HEADS = 16
        N_KV_HEADS = 4
        ROPE_THETA = 10000.0
        EPS = 1e-05

        def _rms_norm(x, w):
            var = jnp.mean(x * x, axis=-1, keepdims=True)
            return x * jax.lax.rsqrt(var + EPS) * w

        def _rope_sin_cos(T, head_dim, dtype):
            inv_freq = 1.0 / ROPE_THETA ** (jnp.arange(0, head_dim, 2, dtype=jnp.float32) / head_dim)
            t = jnp.arange(T, dtype=jnp.float32)
            freqs = jnp.outer(t, inv_freq)
            emb = jnp.concatenate([freqs, freqs], -1)
            return (jnp.sin(emb).astype(dtype)[None, None], jnp.cos(emb).astype(dtype)[None, None])

        def _rotate_half(x):
            h = x.shape[-1] // 2
            x1, x2 = (x[..., :h], x[..., h:])
            return jnp.concatenate([-x2, x1], axis=-1)
        B, T, C = q.shape
        hd = C // N_HEADS
        g = N_HEADS // N_KV_HEADS
        q = _rms_norm(q, q_norm_w)
        k = _rms_norm(k, k_norm_w)
        q = q.reshape(B, T, N_HEADS, hd).transpose(0, 2, 1, 3)
        k = k.reshape(B, T, N_KV_HEADS, hd).transpose(0, 2, 1, 3)
        v = v.reshape(B, T, N_KV_HEADS, hd).transpose(0, 2, 1, 3)
        sin, cos = _rope_sin_cos(T, hd, q.dtype)
        q = q * cos + _rotate_half(q) * sin
        k = k * cos + _rotate_half(k) * sin
        qg = q.reshape(B, N_KV_HEADS, g, T, hd)
        scale = 1.0 / jnp.sqrt(jnp.asarray(hd, q.dtype))
        scores = jnp.einsum('bgnqd,bgkd->bgnqk', qg, k) * scale
        causal = jnp.tril(jnp.ones((T, T), bool))
        scores = jnp.where(causal, scores, jnp.asarray(-1e+30, scores.dtype))
        attn = jax.nn.softmax(scores, axis=-1)
        out = jnp.einsum('bgnqk,bgkd->bgnqd', attn, v)
        out = out.reshape(B, N_HEADS, T, hd).transpose(0, 2, 1, 3).reshape(B, T, C)
        return out @ w_out.T

    def _L0_ffn_ref(x, Wq, Wk, Wv, Wo, w_ln1, w_ln2, Wr, Wg, Wu, Wd):
        import jax, jax.numpy as jnp
        import numpy as np
        B, S, HID = (2, 256, 256)
        NUM_HEADS = 16
        HEAD_DIM = HID // NUM_HEADS
        NUM_EXPERTS = 8
        TOP_K = 2
        INTER = 512
        EPS = 1e-05

        def _rmsnorm(x, w, eps=EPS):
            return x * jax.lax.rsqrt(jnp.mean(x * x, axis=-1, keepdims=True) + eps) * w

        def _moe(x_flat, Wr, Wg, Wu, Wd):
            T = x_flat.shape[0]
            logits = x_flat @ Wr.T
            top_logits, top_idx = jax.lax.top_k(logits, TOP_K)
            probs = jax.nn.softmax(top_logits, axis=-1)
            cw = jnp.zeros((T, NUM_EXPERTS), x_flat.dtype)
            cw = cw.at[jnp.arange(T)[:, None], top_idx].add(probs)
            hg = jnp.einsum('eih,th->eti', Wg, x_flat)
            hu = jnp.einsum('eih,th->eti', Wu, x_flat)
            y = jnp.einsum('ehi,eti->eth', Wd, jax.nn.silu(hg) * hu)
            return jnp.einsum('eth,te->th', y, cw)
        b, s, hid = x.shape
        residual = x
        xn = _rmsnorm(x, w_ln1)
        q = (xn @ Wq.T).reshape(b, s, NUM_HEADS, HEAD_DIM)
        k = (xn @ Wk.T).reshape(b, s, NUM_HEADS, HEAD_DIM)
        v = (xn @ Wv.T).reshape(b, s, NUM_HEADS, HEAD_DIM)
        scale = 1.0 / np.sqrt(HEAD_DIM)
        attn = jnp.einsum('bqhd,bkhd->bhqk', q, k) * scale
        causal = jnp.tril(jnp.ones((s, s), bool))
        attn = jnp.where(causal[None, None], attn, -jnp.inf)
        attn = jax.nn.softmax(attn, axis=-1)
        h = jnp.einsum('bhqk,bkhd->bqhd', attn, v).reshape(b, s, hid)
        x = residual + h @ Wo.T
        residual = x
        xn = _rmsnorm(x, w_ln2)
        moe_out = _moe(xn.reshape(-1, hid), Wr, Wg, Wu, Wd).reshape(b, s, hid)
        return residual + moe_out

    def _L1_attn_ref(x, w_qkv, b_qkv, w_out, b_out):
        import math
        import jax, jax.numpy as jnp
        import numpy as np
        MODEL_DIM = 256
        N_HEADS = 32
        N_GROUPS = 8
        R = N_HEADS // N_GROUPS
        HEAD_DIM = MODEL_DIM // N_HEADS
        KV_DIM = MODEL_DIM // R
        B, S = (1, 256)
        Bx, Sx, _ = x.shape
        fused = x @ w_qkv.T + b_qkv
        q = fused[..., :MODEL_DIM]
        k = fused[..., MODEL_DIM:MODEL_DIM + KV_DIM]
        v = fused[..., MODEL_DIM + KV_DIM:]
        q = q.reshape(Bx, Sx, N_GROUPS, R, HEAD_DIM).transpose(0, 2, 3, 1, 4)
        k = k.reshape(Bx, Sx, N_GROUPS, HEAD_DIM).transpose(0, 2, 1, 3)
        v = v.reshape(Bx, Sx, N_GROUPS, HEAD_DIM).transpose(0, 2, 1, 3)
        sim = jnp.einsum('bgrsd,bgtd->bgrst', q, k) / math.sqrt(HEAD_DIM)
        attn = jax.nn.softmax(sim, axis=-1)
        out = jnp.einsum('bgrst,bgtd->bgrsd', attn, v)
        out = out.transpose(0, 3, 1, 2, 4).reshape(Bx, Sx, MODEL_DIM)
        return out @ w_out.T + b_out

    def _L1_xattn_ref(hidden_q, kv_c, Wq, w_kc_q, w_kc_kv, W_qr, W_kr, Wo):
        import jax, jax.numpy as jnp
        import numpy as np
        B, S, L = (2, 128, 128)
        DIM_Q, H, K, D_C, D_CQ, R = (256, 16, 128, 64, 192, 64)

        def _rope_tables(length, dim):
            inv = 1.0 / 10000.0 ** (jnp.arange(0, dim, 2, dtype=jnp.float32) / dim)
            f = jnp.arange(length, dtype=jnp.float32)[:, None] * inv[None, :]
            sin = jnp.repeat(jnp.sin(f), 2, axis=-1)
            cos = jnp.repeat(jnp.cos(f), 2, axis=-1)
            return (sin, cos)

        def _rotate_half(x):
            half = x.shape[-1] // 2
            return jnp.concatenate([-x[..., half:], x[..., :half]], axis=-1)

        def _apply_rope(x, sin, cos):
            return x * cos + _rotate_half(x) * sin
        Bv, Sv, _ = hidden_q.shape
        _, Lv, _ = kv_c.shape
        q_hk = (hidden_q @ Wq.T).reshape(Bv, Sv, H, K)
        q_big = jnp.einsum('bshk,hkq->bshq', q_hk, w_kc_q)
        sin_q, cos_q = _rope_tables(Sv, D_CQ)
        q_big = _apply_rope(q_big, sin_q[None, :, None, :], cos_q[None, :, None, :])
        sin_k, cos_k = _rope_tables(Lv, D_C)
        kv_r = _apply_rope(kv_c, sin_k[None], cos_k[None])
        q_r = jnp.einsum('bshq,hqr->bhsr', q_big, W_qr)
        k_r = jnp.einsum('bld,hdr->bhlr', kv_r, W_kr)
        scores = jnp.einsum('bhsr,bhlr->bhsl', q_r, k_r)
        attn = jax.nn.softmax(scores, axis=-1)
        ctx_c = jnp.einsum('bhsl,bld->bhsd', attn, kv_r)
        ctx_lat = jnp.einsum('bhsd,hkd->bhsk', ctx_c, w_kc_kv)
        ctx = ctx_lat.transpose(0, 2, 1, 3).reshape(Bv, Sv, H * K)
        return ctx @ Wo.T

    def _L1_ffn_ref(x, weight_up, weight_down, norm_weight, gamma):
        import jax, jax.numpy as jnp
        import numpy as np
        EPS_NORM = 1e-06
        EPS_Q = 1e-08
        QB = 127.0

        def _ternary_quantize(w):
            scale = jnp.maximum(jnp.mean(jnp.abs(w)), EPS_Q)
            w_q = jnp.clip(jnp.round(w / scale), -1.0, 1.0)
            return (w_q, scale)

        def _activation_quant(x):
            gamma = jnp.maximum(jnp.max(jnp.abs(x), axis=-1, keepdims=True), EPS_Q)
            x_q = jnp.clip(jnp.round(x * QB / gamma), -QB, QB)
            return (x_q, gamma / QB)

        def _rmsnorm(x, weight):
            out = x * jax.lax.rsqrt(jnp.mean(x * x, axis=-1, keepdims=True) + EPS_NORM)
            return out * weight
        residual = x
        xn = _rmsnorm(x, norm_weight)
        w_up_q, s_up = _ternary_quantize(weight_up)
        w_down_q, s_down = _ternary_quantize(weight_down)
        x_q, s_x = _activation_quant(xn)
        h = jnp.einsum('bsd,hd->bsh', x_q * s_x, w_up_q * s_up)
        h = jax.nn.silu(h)
        out = jnp.einsum('bsh,dh->bsd', h, w_down_q * s_down)
        return residual + out * gamma
    x = _layernorm(x + _L0_attn_ref(x, L0_attn_q_w, L0_attn_q_b, L0_attn_k_w, L0_attn_k_b, L0_attn_v_w, L0_attn_v_b, L0_attn_o_w, L0_attn_o_b), axis=-1)
    x = _layernorm(x + _L0_xattn_ref(x, ctx_512, ctx_512, L0_xattn_q_norm_w, L0_xattn_k_norm_w, L0_xattn_w_out), axis=-1)
    x = _layernorm(x + _L0_ffn_ref(x, L0_ffn_Wq, L0_ffn_Wk, L0_ffn_Wv, L0_ffn_Wo, L0_ffn_w_ln1, L0_ffn_w_ln2, L0_ffn_Wr, L0_ffn_Wg, L0_ffn_Wu, L0_ffn_Wd), axis=-1)
    x = _layernorm(x + _L1_attn_ref(x, L1_attn_w_qkv, L1_attn_b_qkv, L1_attn_w_out, L1_attn_b_out), axis=-1)
    x = _layernorm(x + _L1_xattn_ref(x, ctx_512, L1_xattn_Wq, L1_xattn_w_kc_q, L1_xattn_w_kc_kv, L1_xattn_W_qr, L1_xattn_W_kr, L1_xattn_Wo), axis=-1)
    x = _layernorm(x + _L1_ffn_ref(x, L1_ffn_weight_up, L1_ffn_weight_down, L1_ffn_norm_weight, L1_ffn_gamma), axis=-1)
    return x

_drawn_inputs = setup_inputs


def setup_inputs(seed=0):
    import zlib

    import numpy as np

    out = dict(_drawn_inputs(seed))
    spreads = {'L0_attn_q_b': (0.0, 2.0),
     'L0_attn_k_b': (0.0, 2.0),
     'L0_attn_v_b': (0.0, 0.1),
     'L0_attn_o_b': (0.0, 0.1),
     'L0_xattn_q_norm_w': (1.0, 0.2),
     'L0_xattn_k_norm_w': (1.0, 0.2),
     'L0_ffn_w_ln1': (1.0, 0.2),
     'L0_ffn_w_ln2': (1.0, 0.2),
     'L1_attn_b_qkv': (0.0, 0.272),
     'L1_attn_b_out': (0.0, 0.1),
     'L1_ffn_norm_weight': (1.0, 0.6),
     'L1_ffn_gamma': (9.999999747378752e-06, 0.6)}
    factors = {'L1_ffn_weight_up': 200.0, 'L1_ffn_weight_down': 200.0, 'L0_attn_q_w': 3.004}
    for name, (base, spread) in spreads.items():
        noise = np.random.default_rng([zlib.crc32(name.encode()), seed]).standard_normal(out[name].shape)
        drawn = base * np.exp(spread * noise) if base else spread * noise
        out[name] = jnp.asarray(drawn.astype(out[name].dtype))
    for name, factor in factors.items():
        out[name] = (out[name] * factor).astype(out[name].dtype)
    return out
```

```python
from collections import namedtuple
from contextlib import ExitStack

import numpy as np

import concourse.bass as bass
from concourse import mybir

ALU = mybir.AluOpType
ACT = mybir.ActivationFunctionType
AX = mybir.AxisListType
F32 = mybir.dt.float32
BF16 = mybir.dt.bfloat16
F32R = mybir.dt.float32r
U32 = mybir.dt.uint32

B, S, D = 32, 64, 256
DC = 64
P = 128
PAIRS = B // 2
TOK = B * S
KC = D // P
E, I = 8, 512
GT = 512
H1, QC, KV = 16, 192, 64
QH = QC // 2
HID = 1024
LN_EPS = 1e-5
ROUND = 1.5 * 2.0 ** 23


def named(**fields):
    return namedtuple("Named", fields)(**fields)



def pieces(widths):
    at, out = 0, {}
    for name, width in widths:
        out[name] = (at, at + width)
        at += width
    return out, at


TABLES = [("ident", 128), ("kvz_mask", 136), ("cos16", 16), ("sin16", 16), ("mask_g4", 4), ("mask_g8", 8),
          ("rope_q", 12 * 64), ("cos64", 64), ("sin64", 64), ("mask_fold", 8), ("iota8", 8), ("negsq", 1)]
SMALL = [("l0_qb", 2), ("l0_kvb", 512), ("l0_ob", 256), ("x_qnw", 256), ("x_knw", 64), ("ln1", 2), ("ln2", 2),
         ("l1_qb", 2), ("l1_kb", 1), ("l1_vb", 64), ("l1_ob", 256), ("f_nw", 256), ("f_gamma", 256)]
EARLY = [("l0_q", 512), ("l0_kv", 1024), ("l0_o", 512), ("x_o", 512),
         ("f_q", 512), ("f_k", 512), ("f_v", 512), ("f_o", 512), ("f_r", 16)]
L1A = [("a_q", 512), ("a_k", 256), ("a_v", 128), ("a_o", 1024)]
LATENT = [("wq", H1 * D), ("wkcq", H1 * QC), ("wqr", H1 * QC), ("wkr", H1 * KV), ("wkckv", H1 * KV), ("wo", H1 * D)]
FFN = [("up", KC * HID), ("down", HID // P * D)]
EXPERT = [("gate", KC * I), ("up", KC * I), ("down", I // P * D)]


def rope_tables(length, dim, spread):
    inv = (np.float32(1.0) / np.float32(10000.0) ** (np.arange(0, dim, 2, dtype=np.float32) / np.float32(dim))).astype(np.float32)
    f = np.arange(length, dtype=np.float32)[:, None] * inv[None, :]
    f = np.repeat(f, 2, axis=-1) if spread else np.concatenate([f, f], -1)
    return np.sin(f).astype(np.float32), np.cos(f).astype(np.float32)


def shape_tables():
    out = {}
    r = np.arange(P)
    out["ident"] = np.eye(P)
    col = np.arange(P)
    out["kvz_mask"] = np.concatenate([r[:, None] // 16 == col[None, :] // 16, r[:, None] // 16 == np.arange(8)[None, :]], 1)
    sin, cos = rope_tables(S, 16, False)
    sign = np.where(np.arange(16) < 8, -1.0, 1.0)
    out["cos16"], out["sin16"] = np.tile(cos, (2, 1)), np.tile(sin * sign, (2, 1))
    out["mask_g4"] = (r[:, None] % 64) // 16 == np.arange(4)
    out["mask_g8"] = (r[:, None] % 64) // 8 == np.arange(8)
    sin, cos = rope_tables(S, QC, True)
    rows = (np.arange(3)[None, :] * P + r[:, None]) % QH
    kinds = [cos[:, :QH], sin[:, :QH], cos[:, QH:], sin[:, QH:]]
    out["rope_q"] = np.stack([k.T[rows] for k in kinds], 1).reshape(P, -1)
    sin, cos = rope_tables(S, KV, True)
    sign = np.where(np.arange(KV) < KV // 2, -1.0, 1.0)
    out["cos64"], out["sin64"] = np.tile(cos, (2, 1)), np.tile(sin * sign, (2, 1))
    fold = [(0, 0), (1, 0), (1, 1), (2, 1)]
    out["mask_fold"] = np.stack([(t * P + r) // QH == 2 * p + h for t, p in fold for h in range(2)], 1)
    out["iota8"] = np.tile(np.arange(8), (P, 1))
    out["negsq"] = np.full((P, 1), -0.5)
    return np.concatenate([np.asarray(out[n], np.float32).reshape(P, w) for n, w in TABLES], 1)


def causal_table():
    q = np.arange(P) % S
    return np.tile(np.where(np.arange(S)[None, :] > q[:, None], -1e30, 0.0), (1, 8)).astype(np.float32)


class Signal:

    def __init__(self, sem, base=0):
        self.sem, self.base = sem, base



def pipelined(eng, groups, per, stages, margin=2):
    deepest = max(lag for _, lag in stages)
    first = min(groups, -(-(deepest + margin) // per))
    for unit in range(first * per):
        for stage, lag in stages:
            if unit >= lag:
                stage((unit - lag) // per, (unit - lag) % per)
    if first < groups:
        with eng.Fori(first, groups) as i:
            for u in range(per):
                for stage, lag in stages:
                    stage(i + (u - lag) // per, (u - lag) % per)
    for unit in range(groups * per, groups * per + deepest):
        for stage, lag in stages:
            if unit - lag < groups * per:
                stage((unit - lag) // per, (unit - lag) % per)


def wait_done(eng, sem, unit, times=1):
    eng.wait_ge(sem.sem, sem.base + (unit + 1) * times)


def wait_freed(eng, sem, unit, back, times=1):
    if isinstance(unit, int) and unit < back:
        return
    eng.wait_ge(sem.sem, sem.base + (unit + 1 - back) * times)


def least(value, limit):
    return min(value, limit) if isinstance(value, int) else value


def decoder(nc, dram, out):
    with ExitStack() as ctx:
        def sbuf(name, shape, dt=F32):
            return ctx.enter_context(nc.sbuf_tensor(name, shape, dt))

        def signals_of(prefix, names):
            return {n: Signal(ctx.enter_context(nc.semaphore(f"{prefix}_{n}"))) for n in names.split()}

        def sems(prefix, names):
            return named(**signals_of(prefix, names))

        def part(tensor, widths, at=0):
            where, _ = pieces(widths)
            return named(**{n: tensor[:, at + a:at + b] for n, (a, b) in where.items()})

        X = sbuf("X", [P, PAIRS, D])
        XT = sbuf("XT", [P, KC, TOK])
        ctx_tok = sbuf("ctx_tok", [P, PAIRS, DC])
        with nc.sbuf_tensor("big_r", [P, 16384], F32R) as big_r, nc.sbuf_tensor("mid_r", [P, 12288], F32R) as mid_r:
            pass
        big = sbuf("big", [P, 16384])
        mid = sbuf("mid", [P, 12288])
        work = sbuf("work", [P, 9728])
        tables = sbuf("tables", [P, sum(w for _, w in TABLES)])
        small = sbuf("small", [P, sum(w for _, w in SMALL)])
        causal = sbuf("causal", [P, 512], BF16)
        ident_bf = sbuf("ident_bf", [P, P], BF16)
        ones = sbuf("ones", [P, P])
        stat = sbuf("stat", [P, 256])
        scores_max = sbuf("scores_max", [P, 2, 16])
        scores_sum = sbuf("scores_sum", [P, 2, 16])
        scores_inv = sbuf("scores_inv", [P, 2, 16])
        ps = ctx.enter_context(nc.psum_tensor("ps", [P, 8, 512], F32))

        T, SM = part(tables, TABLES), part(small, SMALL)
        early = part(big, EARLY)
        l1a_w = part(mid, L1A)
        x_parts = big_r[:, 8192:16384].rearrange("p (n k t) -> p n k t", n=2, k=KC)

        def two(view, cols, n=2):
            return view.rearrange("p (b c) -> p b c", b=n)

        wk = part(work, [("xts", 512), ("qT", 512), ("kT", 512), ("kbd", 2048), ("vbd", 1024), ("sd", 2048),
                         ("pT", 1024), ("avT", 512), ("xn", 512), ("xo", 512), ("xe", 512)])
        xts = wk.xts.rearrange("p (b k t) -> p b k t", b=2, k=KC)
        qT = wk.qT.rearrange("p (b a t) -> p b a t", b=2, a=2)
        kT = wk.kT.rearrange("p (b a t) -> p b a t", b=2, a=2)
        kbd = wk.kbd.rearrange("p (b n) -> p b n", b=2)
        vbd = wk.vbd.rearrange("p (b n) -> p b n", b=2)
        sd = wk.sd.rearrange("p (b n) -> p b n", b=2)
        pT = wk.pT.rearrange("p (n t) -> p n t", n=8)
        avT = wk.avT.rearrange("p (b a t) -> p b a t", b=2, a=2)
        xn = wk.xn.rearrange("p (b c) -> p b c", b=2)
        xo = wk.xo.rearrange("p (b c) -> p b c", b=2)
        xe = wk.xe.rearrange("p (b k t) -> p b k t", b=2, k=KC)

        ld = sems("ld", "x xt ctx tables causal small early l1a latent ffn expert0 expert1")
        setup = sems("setup", "ones causal ident")
        stored = sems("out", "y")

        POST = "y stats aggr eps rstd xn x_stored ss ms rr xo xtr xe xt_stored"

        def stat_cols(slot, j, n=1):
            return stat[:, slot * 64 + j:slot * 64 + j + n]

        def dve_add_residual(L, i, slot, unit, pair, acc, out_ready, acc_times=1):
            wait_done(nc.vector, out_ready, unit, acc_times)
            if L.bias_x:
                wait_done(nc.vector, L.s.xb, unit)
            if L.norm:
                wait_freed(nc.vector, L.s.x_stored, unit, 2)
            else:
                wait_freed(nc.vector, L.s.x_stored, unit, 2)
            if L.rms:
                wait_freed(nc.vector, L.s.ss, unit, 2)
            nc.vector.tensor_tensor(xn[:, slot], acc, X[:, pair, :], ALU.add).then_inc(L.s.y.sem, 1)

        def dve_norm_stats(L, unit, slot):
            wait_done(nc.vector, L.s.y, unit)
            nc.vector.bn_stats(stat_cols(slot, 0, 6), xn[:, slot]).then_inc(L.s.stats.sem, 1)
            nc.vector.wait_ge(ld.tables.sem, 16)
            wait_done(nc.vector, L.s.stats, unit)
            nc.vector.bn_aggr(stat_cols(slot, 8, 2), stat_cols(slot, 0, 6)).then_inc(L.s.aggr.sem, 1)
            wait_done(nc.vector, L.s.aggr, unit)
            nc.vector.tensor_scalar(stat_cols(slot, 10), stat_cols(slot, 9), LN_EPS, None, ALU.add).then_inc(L.s.eps.sem, 1)

        def pool_rstd(L, unit, slot):
            wait_done(nc.gpsimd, L.s.eps, unit)
            nc.gpsimd.tensor_tensor(stat_cols(slot, 11), stat_cols(slot, 10), T.negsq, ALU.pow).then_inc(L.s.rstd.sem, 1)

        def dve_norm(L, unit, slot):
            wait_done(nc.vector, L.s.rstd, unit)
            nc.vector.tensor_scalar(xn[:, slot], xn[:, slot], stat_cols(slot, 8), stat_cols(slot, 11),
                                    ALU.subtract, ALU.mult).then_inc(L.s.xn.sem, 1)

        def pool_store_x(L, unit, slot, pair):
            wait_done(nc.gpsimd, L.s.xn if L.norm else L.s.y, unit)
            if L.twice:
                nc.gpsimd.tensor_tensor(X[:, pair, :], X[:, pair, :], xn[:, slot], ALU.add).then_inc(L.s.x_stored.sem, 1)
            else:
                nc.gpsimd.tensor_copy(X[:, pair, :], xn[:, slot]).then_inc(L.s.x_stored.sem, 1)

        def act_square(L, unit, slot):
            wait_done(nc.scalar, L.s.xn if L.norm else L.s.y, unit)
            wait_freed(nc.scalar, L.s.xtr if L.transposes else L.s.xo, unit, 2)
            nc.scalar.activation(xo[:, slot], xn[:, slot], ACT.Square, accum_out=stat_cols(slot, 12)).then_inc(L.s.ss.sem, 1)

        def dve_mean_square(L, unit, slot):
            wait_done(nc.vector, L.s.ss, unit)
            nc.vector.tensor_scalar(stat_cols(slot, 13), stat_cols(slot, 12), 1.0 / D, L.rms, ALU.mult,
                                    ALU.add).then_inc(L.s.ms.sem, 1)

        def pool_rms(L, unit, slot):
            wait_done(nc.gpsimd, L.s.ms, unit)
            nc.gpsimd.tensor_tensor(stat_cols(slot, 14), stat_cols(slot, 13), T.negsq, ALU.pow).then_inc(L.s.rr.sem, 1)

        def dve_scale_rms(L, unit, slot):
            wait_done(nc.vector, L.s.rr, unit)
            nc.vector.tensor_scalar(xo[:, slot], xn[:, slot], stat_cols(slot, 14), None, ALU.mult).then_inc(L.s.xo.sem, 1)

        def pe_transpose_x(L, unit, slot):
            wait_done(nc.tensor, L.s.xo if L.rms else L.s.xn, unit)
            wait_freed(nc.tensor, L.s.xe, unit, 1)
            if L.v_ahead is not None:
                nc.tensor.wait_ge(L.s.vbd.sem, L.s.vbd.base + least(unit + 1 + L.v_ahead, PAIRS))
            if L.router:
                wait_freed(nc.tensor, L.s.lg, unit, 1)
            src = xo if L.rms else xn
            for kc in range(KC):
                mm = nc.tensor.transpose(ps[:, 5, kc * P:(kc + 1) * P], src[:, slot, kc * P:(kc + 1) * P], T.ident)
            mm.then_inc(L.s.xtr.sem, 1)

        def act_copy_xt(L, unit, slot):
            wait_done(nc.scalar, L.s.xtr, unit)
            wait_freed(nc.scalar, L.s.xt_stored, unit, 2)
            if L.router:
                wait_freed(nc.scalar, L.s.routed, unit, 2)
            for kc in range(KC):
                scale = L.xt_scale[:, kc:kc + 1] if L.xt_scale is not None else 1.0
                a = nc.scalar.activation(xe[:, slot, kc, :], ps[:, 5, kc * P:(kc + 1) * P], ACT.Copy, scale=scale)
            a.then_inc(L.s.xe.sem, 1)

        def pool_store_xt(L, unit, slot, pair):
            wait_done(nc.gpsimd, L.s.xe, unit)
            if L.router:
                high = x_parts[:, 0, :, bass.ds(pair * P, P)]
                nc.gpsimd.tensor_copy(high, xe[:, slot]).then_inc(L.s.x_high.sem, 1)
                wait_done(nc.gpsimd, L.s.x_high, unit)
                nc.gpsimd.tensor_tensor(x_parts[:, 1, :, bass.ds(pair * P, P)], xe[:, slot], high.bitcast(F32),
                                        ALU.subtract).then_inc(L.s.xt_stored.sem, 1)
                return
            nc.gpsimd.tensor_copy(XT[:, :, bass.ds(pair * P, P)], xe[:, slot]).then_inc(L.s.xt_stored.sem, 1)

        def wait_sublayer(eng, L):
            eng.wait_ge(L.s.x_stored.sem, L.s.x_stored.base + PAIRS)
            if L.router:
                wait_done(eng, L.s.lg, PAIRS - 1)
            if L.transposes:
                wait_done(eng, L.s.xt_stored, PAIRS - 1)
            elif L.rms:
                wait_done(eng, L.s.xo, PAIRS - 1)


        lin = named(bias_x=True, norm=True, rms=1e-5, transposes=False, router=False, xt_scale=None, twice=False,
                              s=sems("lin", POST + " ready xts q_psum kv_psum qb kb vb low ex qk kvz kvz_masked att "
                                     "den rden an atr anT o xb vones"))
        qk = wk.kbd[:, 0:1024].rearrange("p (b n) -> p b n", b=2)
        qk_exp = wk.pT.rearrange("p (b n) -> p b n", b=2)
        v_one = wk.sd[:, 0:544].rearrange("p (b h n) -> p b h n", b=2, h=2)
        kvz = wk.sd[:, 544:1632].rearrange("p (b q n) -> p b q n", b=2, q=4)
        an = wk.qT.rearrange("p (b n) -> p b n", b=2)
        lin_rec = scores_inv

        def lin_pool():
            s = lin.s
            pool = nc.gpsimd
            pool.memset(v_one[:, :, :, 128:136], 1.0).then_inc(s.vones.sem, 1)
            pool.wait_ge(ld.xt.sem, ld.xt.base + 16)
            pool.wait_ge(ld.x.sem, ld.x.base + 16)
            pool.wait_ge(ld.small.sem, ld.small.base + 16)
            pool.wait_ge(ld.tables.sem, ld.tables.base + 16)

            def load(i, k):
                u = 2 * i + k
                wait_freed(pool, s.kv_psum, u, 2)
                pool.tensor_copy(xts[:, k], XT[:, :, bass.ds(u * P, P)]).then_inc(s.xts.sem, 1)
                pool.tensor_tensor(X[:, u, :], X[:, u, :], SM.l0_ob, ALU.add).then_inc(s.xb.sem, 1)

            pipelined(pool, PAIRS // 2, 2, [
                (load, 0),
                (lambda i, k: pool_rstd(lin, 2 * i + k, k), 3),
                (lambda i, k: pool_store_x(lin, 2 * i + k, k, 2 * i + k), 3),
                (lambda i, k: pool_rms(lin, 2 * i + k, k), 3)])

        def lin_pe():
            s = lin.s
            pe = nc.tensor
            pe.wait_ge(ld.early.sem, ld.early.base + 16)
            pe.wait_ge(ld.tables.sem, ld.tables.base + 16)

            def project(i, k):
                u = 2 * i + k
                wait_done(pe, s.xts, u)
                wait_freed(pe, s.anT, u, 2)
                for m in range(2):
                    for kc in range(KC):
                        mm = pe.matmul(ps[:, 2 + k, m * P:(m + 1) * P], early.l0_q[:, kc * D + m * P:kc * D + (m + 1) * P],
                                       xts[:, k, kc], start=kc == 0, stop=kc == 1)
                mm.then_inc(s.q_psum.sem, 1)
                wait_freed(pe, s.kb, u, 2)
                wait_freed(pe, s.vb, u, 2)
                for kc in range(KC):
                    mm = pe.matmul(ps[:, k, :], xts[:, k, kc], early.l0_kv[:, kc * 512:(kc + 1) * 512],
                                   start=kc == 0, stop=kc == 1)
                mm.then_inc(s.kv_psum.sem, 1)

            def sums(i, k):
                u = 2 * i + k
                wait_done(pe, s.qk, u)
                wait_done(pe, s.vb, u)
                pe.wait_ge(s.vones.sem, s.vones.base + 1)
                wait_freed(pe, s.kvz_masked, u, 1)
                for b in range(2):
                    for h in range(2):
                        r = slice(64 * b, 64 * b + 64)
                        mm = pe.matmul(ps[:, 4 + b, h * 136:(h + 1) * 136], qk[r, k, 256 + h * P:256 + (h + 1) * P],
                                       v_one[r, k, h, :], start=True, stop=True)
                mm.then_inc(s.kvz.sem, 1)

            def attend(i, k):
                u = 2 * i + k
                wait_done(pe, s.kvz_masked, u)
                wait_freed(pe, s.an, u, 1)
                for b in range(2):
                    for h in range(2):
                        mm = pe.matmul(ps[64 * b:64 * b + 64, 6, h * 136:(h + 1) * 136],
                                       qk[:, k, h * P + 64 * b:h * P + 64 * b + 64], kvz[:, k, 2 * b + h, :],
                                       start=True, stop=True)
                mm.then_inc(s.att.sem, 1)

            def turn(i, k):
                u = 2 * i + k
                wait_done(pe, s.an, u)
                for h in range(2):
                    mm = pe.transpose(ps[:, 2 + k, 256 + h * P:256 + (h + 1) * P], an[:, k, h * P:(h + 1) * P], T.ident)
                mm.then_inc(s.atr.sem, 1)

            def project_out(i, k):
                u = 2 * i + k
                wait_done(pe, s.anT, u)
                wait_freed(pe, s.y, u, 1)
                for h in range(2):
                    mm = pe.matmul(ps[:, 7, 0:D], avT[:, k, h], early.l0_o[:, h * D:(h + 1) * D], start=h == 0, stop=h == 1)
                mm.then_inc(s.o.sem, 1)

            pipelined(pe, PAIRS // 2, 2, [(project, 0), (attend, 1), (project_out, 2), (sums, 0), (turn, 1)])

        def lin_act():
            s = lin.s
            act = nc.scalar
            act.wait_ge(ld.small.sem, ld.small.base + 16)
            act.wait_ge(ld.causal.sem, ld.causal.base + 16)
            act.activation(causal[:, :], big[:, 12288:12800], ACT.Copy).then_inc(setup.causal.sem, 1)
            act.wait_ge(ld.tables.sem, ld.tables.base + 16)
            act.activation(ident_bf[:, :], T.ident, ACT.Copy).then_inc(setup.ident.sem, 1)

            def bias_q(i, k):
                u = 2 * i + k
                wait_done(act, s.q_psum, u)
                wait_freed(act, s.att, u, 2)
                for m in range(2):
                    a = act.activation(qk[:, k, m * P:(m + 1) * P], ps[:, 2 + k, m * P:(m + 1) * P], ACT.Identity,
                                       bias=SM.l0_qb[:, m:m + 1])
                a.then_inc(s.qb.sem, 1)

            def exponent(i, k):
                u = 2 * i + k
                wait_done(act, s.low, u)
                act.activation(qk_exp[:, k], qk_exp[:, k], ACT.Exp).then_inc(s.ex.sem, 1)

            def copy_att(i, k):
                u = 2 * i + k
                wait_done(act, s.atr, u)
                wait_freed(act, s.o, u, 2)
                act.activation(avT[:, k], ps[:, 2 + k, 256:512].rearrange("p (a t) -> p a t", a=2), ACT.Copy).then_inc(s.anT.sem, 1)

            pipelined(act, PAIRS // 2, 2, [(bias_q, 0), (exponent, 0), (copy_att, 1),
                                            (lambda i, k: act_square(lin, 2 * i + k, k), 2)])

        def lin_dve():
            s = lin.s
            dve = nc.vector
            dve.wait_ge(ld.small.sem, ld.small.base + 16)
            dve.wait_ge(ld.tables.sem, ld.tables.base + 16)
            dve.wait_ge(ld.x.sem, ld.x.base + 16)

            def bias_kv(i, k):
                u = 2 * i + k
                wait_done(dve, s.kv_psum, u)
                wait_freed(dve, s.kvz, u, 2)
                dve.tensor_tensor(qk[:, k, 256:512], ps[:, k, 0:256], SM.l0_kvb[:, 0:256], ALU.add).then_inc(s.kb.sem, 1)
                dve.tensor_tensor(v_one[:, k, :, 0:P], ps[:, k, 256:512].rearrange("p (h n) -> p h n", h=2),
                                  SM.l0_kvb[:, 256:512].rearrange("p (h n) -> p h n", h=2), ALU.add).then_inc(s.vb.sem, 1)

            def low(i, k):
                u = 2 * i + k
                wait_done(dve, s.qb, u)
                wait_done(dve, s.kb, u)
                wait_freed(dve, s.qk, u, 2)
                dve.tensor_scalar(qk_exp[:, k], qk[:, k], 0.0, None, ALU.min).then_inc(s.low.sem, 1)

            def elu(i, k):
                u = 2 * i + k
                wait_done(dve, s.ex, u)
                dve.scalar_tensor_tensor(out=qk[:, k], in0=qk[:, k], scalar=0.0, in1=qk_exp[:, k], op0=ALU.max,
                                         op1=ALU.add).then_inc(s.qk.sem, 1)

            def keep_heads(i, k):
                u = 2 * i + k
                wait_done(dve, s.kvz, u)
                wait_freed(dve, s.att, u, 2)
                mask = T.kvz_mask[:, None, :].broadcast_to([P, 2, 136])
                for b in range(2):
                    ins = dve.tensor_tensor(kvz[:, k, 2 * b:2 * b + 2, :], ps[:, 4 + b, 0:272].rearrange("p (h n) -> p h n", h=2),
                                            mask, ALU.mult)
                ins.then_inc(s.kvz_masked.sem, 1)

            def divide(i, k):
                u = 2 * i + k
                wait_done(dve, s.att, u)
                both = ps[:, 6, 0:272].rearrange("p (h n) -> p h n", h=2)
                den = scores_sum[:, k, :]
                dve.tensor_scalar(den.rearrange("p (h n) -> p h n", h=2), both[:, :, 128:136], 1e-6, None,
                                  ALU.add).then_inc(s.den.sem, 1)
                wait_done(dve, s.den, u)
                dve.reciprocal(lin_rec[:, k, :], den).then_inc(s.rden.sem, 1)
                wait_done(dve, s.rden, u)
                wait_freed(dve, s.atr, u, 2)
                for h in range(2):
                    rec = lin_rec[:, k, 8 * h:8 * h + 8, None].broadcast_to([P, 8, 16])
                    ins = dve.tensor_tensor(an[:, k, h * P:(h + 1) * P].rearrange("p (n e) -> p n e", n=8),
                                            both[:, h, 0:P].rearrange("p (n e) -> p n e", n=8), rec, ALU.mult)
                ins.then_inc(s.an.sem, 1)

            def post1(i, k):
                u = 2 * i + k
                dve_add_residual(lin, i, k, u, u, ps[:, 7, 0:D], s.o)
                dve_norm_stats(lin, u, k)

            def post3(i, k):
                u = 2 * i + k
                wait_freed(dve, lin.s.xo, u, 1)
                dve_mean_square(lin, u, k)

            def post4(i, k):
                u = 2 * i + k
                wait_done(dve, s.rr, u)
                dve.tensor_scalar(XT[:, :, bass.ds(u * P, P)], xn[:, k].rearrange("p (a c) -> p a c", a=2),
                                  stat_cols(k, 14), None, ALU.mult).then_inc(s.xo.sem, 1)

            pipelined(dve, PAIRS // 2, 2, [
                (bias_kv, 0), (low, 0), (divide, 1), (elu, 0), (post1, 2), (keep_heads, 0),
                (lambda i, k: dve_norm(lin, 2 * i + k, k), 2), (post3, 2), (post4, 2)])

        SOFT = ("rope qk_t xts xq kst qk_psum v_psum q k kbd vbd scored maxed subbed exped summed inv normed pt0 pt1 ptc0 ptc1 "
                "av avT avT1 o xb routed lg zero xw amax gam inv_gam q1 q2 part down own_y x_high")

        UNIT_STEPS = "scored maxed subbed exped summed inv normed pt0 pt1 ptc0 ptc1 av avT".split()
        soft_sems = signals_of("soft", SOFT + " " + POST)
        counted = {n: 0 for n in (SOFT + " " + POST).split()}

        def soft(kind, drop, **k):
            signals = {}
            for n in counted:
                if n in drop.split():
                    continue
                signals[n] = Signal(soft_sems[n].sem, counted[n])
                times = k.get("upp", 1) if n in UNIT_STEPS else 1
                times *= {"rope": 4, "av": 2 if kind == "latent" else 1}.get(n, 1)
                counted[n] += 1 if n == "zero" else PAIRS * times
            if kind == "self0":
                signals["y"] = Signal(soft_sems["own_y"].sem)
            n = 1 if kind == "latent" else 2
            turn_x = n + 5 if k.get("rms") else n + 4
            lags = named(scores=n, values_in=n + 1, turn=n + 2, out=n + 3, turn_x=turn_x, route=turn_x + 1)
            return named(**{**dict(lags=lags, kind=kind, upp=1, bias_x=False, norm=True, rms=None, transposes=True, router=False,
                                   xt_scale=None, v_ahead=3, masked=False, twice=False, s=named(**signals)), **k})

        QUANT = "xw amax gam inv_gam q1 q2 part down own_y"

        def only(names):
            return " ".join(n for n in counted if n not in names.split())

        cross = soft("cross", QUANT + " x_high xts qk_psum v_psum xb avT1 routed lg", scale=0.25, rms=1e-5, xt_scale=SM.ln1, masked=True, v_ahead=None)
        causal_self = soft("self0", QUANT + " y rope qk_t xq kst xb avT1 stats aggr eps rstd xn", scale=0.25, norm=False, rms=1e-5,
                           xt_scale=SM.ln2, router=True, masked=True, twice=True)
        moe_norm = soft("moe_norm", only("y stats aggr eps rstd xn x_stored xtr xe xt_stored"), v_ahead=None)
        grouped = soft("self1", QUANT + " x_high rope qk_t xq kst avT1 ss ms rr xo routed lg", scale=8.0 ** -0.5, bias_x=True, upp=2, v_ahead=1)
        latent = soft("latent", "x_high rope xq xts kbd qk_psum v_psum xb ss ms rr xo routed lg xtr xe xt_stored " + QUANT, scale=1.0,
                      v_ahead=None, transposes=False)
        ffn = soft("ffn", only("ss ms rr xw amax gam inv_gam q1 q2 xo xtr xe scored exped pt0 pt1 ptc0 ptc1 part down o y stats aggr "
                               "eps rstd xn x_stored"), transposes=False)

        xq = wk.xts.rearrange("p (b n) -> p b n", b=2)
        kst = kT[:, :, 1, :]
        k_rope = mid[:, 0:1024].rearrange("p (t n) -> p t n", t=PAIRS)
        rope_w = mid[:, 1024:1536].rearrange("p (b n) -> p b n", b=2)
        k_tmp = mid[:, 1536:4608].rearrange("p (b t n) -> p b t n", b=3, t=PAIRS)
        qts = wk.kbd.rearrange("p (b h t) -> p b h t", b=2, h=8)
        q_lat = big[:, :].rearrange("p (h t) -> p h t", h=8)
        fold_o = mid[:, 10240:12288].rearrange("p (n c) -> p n c", n=8)
        cT = work[:, 0:1024].rearrange("p (n t) -> p n t", n=8)
        logits = sbuf("logits", [P, PAIRS, E])

        def at(L, i, k):
            return 2 * L.upp * i + k, k % 2, 2 * i + k // L.upp, k // L.upp, k % L.upp

        def run(eng, L, stages):
            pipelined(eng, PAIRS // 2, 2 * L.upp, stages, margin=2 * L.upp)

        def soft_pe(L):
            s, pe = L.s, nc.tensor

            def project(i, k):
                u, us, p, slot, a = at(L, i, k)
                if a:
                    return
                if L.kind in ("cross", "latent"):
                    if L.kind == "cross":
                        wait_done(pe, s.xq, p)
                        wait_freed(pe, s.q, p, 1)
                    wait_done(pe, s.kst, p)
                    wait_freed(pe, s.k, p, 1)
                    if L.kind == "cross":
                        for m in range(2):
                            pe.transpose(ps[:, 6, m * P:(m + 1) * P], xq[:, slot, m * P:(m + 1) * P], T.ident)
                    pe.transpose(ps[:, 6, 256:384] if L.kind == "cross" else ps[:, 5, 256:384], kst[:, slot], T.ident).then_inc(s.qk_t.sem, 1)
                    return
                wait_freed(pe, s.k, p, 1)
                wq, wkk, nk = (early.f_q, early.f_k, 2) if L.kind == "self0" else (l1a_w.a_q, l1a_w.a_k, 1)
                for w, n, at0 in ((wq, 2, 0), (wkk, nk, 256)):
                    for m in range(n):
                        for kc in range(KC):
                            mm = pe.matmul(ps[:, 6, at0 + m * P:at0 + (m + 1) * P], w[:, (kc * n + m) * P:(kc * n + m + 1) * P],
                                           XT[:, kc, bass.ds(p * P, P)], start=kc == 0, stop=kc == 1)
                mm.then_inc(s.qk_psum.sem, 1)

            def project_values(i, k):
                u, us, p, slot, a = at(L, i, k)
                if a:
                    return
                wait_done(pe, s.xts, p)
                wv, nv = (early.f_v, D) if L.kind == "self0" else (l1a_w.a_v, 64)
                wait_freed(pe, s.vbd, p, 1)
                wait_freed(pe, s.xe, p, L.v_ahead + 1)
                if L.router:
                    wait_freed(pe, s.lg, p, L.v_ahead + 2)
                for kc in range(KC):
                    mm = pe.matmul(ps[:, 5, 256:256 + nv], xts[:, slot, kc], wv[:, kc * nv:(kc + 1) * nv],
                                   start=kc == 0, stop=kc == 1)
                mm.then_inc(s.v_psum.sem, 1)

            def scores(i, k):
                u, us, p, slot, a_unit = at(L, i, k)
                wait_done(pe, s.q, p)
                wait_done(pe, s.k if L.kind == "latent" else s.kbd, p)
                wait_freed(pe, s.subbed, u, 1)
                if not L.masked:
                    pe.matmul(ps[:, 0, 0:2], ident_bf[:, :], ident_bf[:, 0:2], start=True, stop=True)
                if L.masked:
                    for c in range(2):
                        pe.matmul(ps[:, c, :], ident_bf[:, :], causal[:, :], start=True, stop=True)
                for b in range(2):
                    rb = slice(64 * b, 64 * b + 64)
                    for c in range(2):
                        rc = slice(64 * c, 64 * c + 64)
                        if L.kind == "self1":
                            mm = pe.matmul(ps[rb, c, :], qT[rc, slot, a_unit, rb], kbd[rc, slot, b * 512:(b + 1) * 512],
                                           start=True, stop=True)
                        elif L.kind == "latent":
                            for h in range(8):
                                mm = pe.matmul(ps[rb, c, h * 64:(h + 1) * 64], qts[rc, slot, h, rb], kT[rc, slot, 0, rb],
                                               start=True, stop=True)
                        else:
                            for a in range(2):
                                n = b if L.kind == "cross" else 2 * a + b
                                mm = pe.matmul(ps[rb, c, a * 256:(a + 1) * 256], qT[rc, slot, a, rb],
                                               kbd[rc, slot, n * 256:(n + 1) * 256], start=False, stop=True,
                                               skip_group_check=True)
                mm.then_inc(s.scored.sem, 1)

            def turn(i, k):
                u, us, p, slot, a = at(L, i, k)
                wait_done(pe, s.normed, u)
                for half, copied, full in ((0, s.ptc0, s.pt0), (1, s.ptc1, s.pt1)):
                    wait_freed(pe, copied, u, 1)
                    for n in range(4):
                        mm = pe.transpose(ps[:, 2 + half, n * P:(n + 1) * P], sd[:, us, (4 * half + n) * P:(4 * half + n + 1) * P],
                                          T.ident)
                    mm.then_inc(full.sem, 1)

            def values(i, k):
                u, us, p, slot, a_unit = at(L, i, k)
                wait_done(pe, s.ptc0, u)
                wait_done(pe, s.vbd, p)
                wait_freed(pe, s.avT, u, 1)
                chunks = pT[:, :, :].rearrange("p (c a g) t -> p c a g t", c=2, a=2)
                bank = ps[:, 4, 0:256].rearrange("p (a b t) -> p a b t", a=2, b=2)
                for c in range(2):
                    if c == 1:
                        wait_done(pe, s.ptc1, u)
                    if L.kind == "latent":
                        if c == 1:
                            wait_freed(pe, s.avT1, u, 1)
                        wide = ps[:, 4 if c == 0 else 6, :].rearrange("p (n b t) -> p n b t", n=4, b=2)
                        for b in range(2):
                            mm = pe.matmul(wide[:, :, b, :], vbd[:, slot, b * P:(b + 1) * P], pT[:, 4 * c:4 * c + 4, 64 * b:64 * b + 64],
                                           start=True, stop=True)
                        mm.then_inc(s.av.sem, 1)
                        continue
                    for b in range(2):
                        rb = slice(64 * b, 64 * b + 64)
                        if L.kind == "self1":
                            for g in range(4):
                                mm = pe.matmul(bank[32 * g:32 * g + 32, c, b, :], vbd[:, slot, b * P + 32 * g:b * P + 32 * g + 32],
                                               pT[:, 4 * c + g, rb], start=True, stop=True)
                            continue
                        for g in range(2):
                            rows = slice(32 * (2 * c + g), 32 * (2 * c + g) + 32)
                            if L.kind == "cross":
                                mm = pe.matmul(bank[rows, :, b, :], vbd[:, slot, b * 64 + 32 * g:b * 64 + 32 * g + 32],
                                               chunks[:, c, :, g, rb], start=True, stop=True)
                            else:
                                for a in range(2):
                                    n = 4 * c + 2 * a + g
                                    mm = pe.matmul(bank[rows, a, b, :], vbd[:, slot, b * 256 + 32 * n:b * 256 + 32 * n + 32],
                                                   pT[:, n, rb], start=True, stop=True)
                if L.kind != "latent":
                    mm.then_inc(s.av.sem, 1)

            def project_out(i, k):
                u, us, p, slot, a_unit = at(L, i, k)
                if a_unit != L.upp - 1:
                    return
                wait_done(pe, s.avT, u)
                if L.kind == "latent":
                    wait_done(pe, s.avT1, u)
                wait_freed(pe, s.y, p, 1)
                pairs = {"cross": [(avT[:, us, a], early.x_o, a) for a in range(2)],
                         "self0": [(avT[:, us, a], early.f_o, a) for a in range(2)],
                         "self1": [(avT[:, a, c], l1a_w.a_o, 2 * a + c) for a in range(2) for c in range(2)],
                         "latent": [(cT[:, n], None, n) for n in range(8)]}[L.kind]
                for n, (lhs, w, at0) in enumerate(pairs):
                    rhs = fold_o[:, at0] if w is None else w[:, at0 * D:(at0 + 1) * D]
                    mm = pe.matmul(ps[:, 7, 0:D], lhs, rhs, start=n == 0, stop=n == len(pairs) - 1)
                mm.then_inc(s.o.sem, 1)

            def turn_x(i, k):
                u, us, p, slot, a = at(L, i, k)
                if a == L.upp - 1:
                    pe_transpose_x(L, p, slot)

            def route(i, k):
                u, us, p, slot, a = at(L, i, k)
                wait_done(pe, s.xe, p)
                pe.wait_ge(s.vbd.sem, s.vbd.base + least(p + 2 + L.v_ahead, PAIRS))
                for kc in range(KC):
                    mm = pe.matmul(ps[:, 5, 0:E], xe[:, slot, kc], early.f_r[:, kc * E:(kc + 1) * E], start=kc == 0, stop=kc == 1)
                mm.then_inc(s.routed.sem, 1)

            g = L.lags
            stages = [(turn, g.turn), (scores, g.scores)] + ([(route, g.route)] if L.router else []) + [(project_out, g.out)]
            stages += ([(turn_x, g.turn_x)] if L.transposes else []) + [(project, 0)]
            run(pe, L, stages + ([(project_values, g.values_in)] if L.kind in ("self0", "self1") else []) + [(values, g.turn)])

        def soft_act(L):
            s, act = L.s, nc.scalar

            def copy_xt(i, k):
                u, us, p, slot, a = at(L, i, k)
                if a == L.upp - 1:
                    act_copy_xt(L, p, slot)

            def copy_qkv(i, k):
                u, us, p, slot, a = at(L, i, k)
                if a:
                    return
                wait_done(act, s.qk_t if L.kind in ("cross", "latent") else s.qk_psum, p)
                wait_freed(act, s.scored, p, 2, L.upp)
                if L.kind == "cross":
                    act.activation(qT[:, slot], ps[:, 6, 0:256].rearrange("p (a t) -> p a t", a=2), ACT.Copy).then_inc(s.q.sem, 1)
                    act.activation(kT[:, slot, 0], ps[:, 6, 256:384], ACT.Copy).then_inc(s.k.sem, 1)
                elif L.kind == "latent":
                    act.activation(kT[:, slot, 0], ps[:, 5, 256:384], ACT.Copy).then_inc(s.k.sem, 1)
                elif L.kind == "self0":
                    act.activation(qT[:, slot], ps[:, 6, 0:256].rearrange("p (a t) -> p a t", a=2), ACT.Copy).then_inc(s.q.sem, 1)
                    wait_freed(act, s.kbd, p, 2)
                    act.activation(kT[:, slot], ps[:, 6, 256:512].rearrange("p (a t) -> p a t", a=2), ACT.Copy).then_inc(s.k.sem, 1)
                else:
                    for m in range(2):
                        ins = act.activation(qT[:, slot, m], ps[:, 6, m * P:(m + 1) * P], ACT.Identity, bias=SM.l1_qb[:, m:m + 1])
                    ins.then_inc(s.q.sem, 1)
                    wait_freed(act, s.kbd, p, 2)
                    act.activation(kT[:, slot, 0], ps[:, 6, 256:384], ACT.Identity, bias=SM.l1_kb).then_inc(s.k.sem, 1)

            def spread_v(i, k):
                u, us, p, slot, a = at(L, i, k)
                if L.kind == "self1":
                    return
                wait_freed(act, s.av, p, 2, 2 if L.kind == "latent" else 1)
                if L.kind == "self0":
                    wait_done(act, s.v_psum, p)
                act.wait_ge(s.zero.sem, s.zero.base + 1)
                for b in range(2):
                    rb = slice(64 * b, 64 * b + 64)
                    for x in range(2):
                        rx = slice(64 * x, 64 * x + 64)
                        if L.kind == "cross":
                            dst = vbd[rx, slot, 64 * b:64 * b + 64].rearrange("p (g x d) -> p g x d", g=2, x=2)[:, :, x, :]
                            src = ctx_tok[rb, p, :].rearrange("p (g x d) -> p g x d", g=2, x=2)[:, :, x, :]
                        elif L.kind == "latent":
                            dst = vbd[rx, slot, b * P + 64 * x:b * P + 64 * x + 64]
                            src = ctx_tok[rb, p, :]
                        else:
                            dst = vbd[rx, slot, 256 * b:256 * b + 256].rearrange("p (n x d) -> p n x d", n=8, x=2)
                            dst = dst.rearrange("p (c a g) x d -> p c a g x d", c=2, a=2)
                            src = ps[rb, 5, 256:512].rearrange("p (a c g x d) -> p a c g x d", a=2, c=2, g=2, x=2)
                            for c in range(2):
                                ins = act.activation(dst[:, c, :, :, x, :], src[:, :, c, :, x, :], ACT.Copy)
                            continue
                        ins = act.activation(dst, src, ACT.Copy)
                ins.then_inc(s.vbd.sem, 1)

            def exponent(i, k):
                u, us, p, slot, a = at(L, i, k)
                wait_done(act, s.subbed, u)
                act.activation(sd[:, us], sd[:, us], ACT.Exp, scale=L.scale).then_inc(s.exped.sem, 1)

            def square(i, k):
                u, us, p, slot, a = at(L, i, k)
                act_square(L, p, slot)

            def copy_pt(i, k):
                u, us, p, slot, a = at(L, i, k)
                wait_done(act, s.pt0, u)
                wait_freed(act, s.av, u, 1, 2 if L.kind == "latent" else 1)
                act.activation(pT[:, 0:4], ps[:, 2, :].rearrange("p (n t) -> p n t", n=4), ACT.Copy).then_inc(s.ptc0.sem, 1)

            def copy_av(i, k):
                u, us, p, slot, a = at(L, i, k)
                if L.kind == "latent":
                    wait_freed(act, s.o, p, 1)
                    act.wait_ge(s.av.sem, s.av.base + 2 * u + 1)
                    act.activation(cT[:, 0:4], ps[:, 4, :].rearrange("p (n t) -> p n t", n=4), ACT.Copy).then_inc(s.avT.sem, 1)
                    wait_done(act, s.av, u, 2)
                    act.activation(cT[:, 4:8], ps[:, 6, :].rearrange("p (n t) -> p n t", n=4), ACT.Copy).then_inc(s.avT1.sem, 1)
                    return
                wait_done(act, s.av, u)
                if L.upp == 2:
                    wait_freed(act, s.o, p, 1)
                else:
                    wait_freed(act, s.o, p, 2)
                act.activation(avT[:, us], ps[:, 4, 0:256].rearrange("p (a t) -> p a t", a=2), ACT.Copy).then_inc(s.avT.sem, 1)

            def copy_logits(i, k):
                u, us, p, slot, a = at(L, i, k)
                wait_done(act, s.routed, p)
                act.activation(logits[:, p, :], ps[:, 5, 0:E], ACT.Copy).then_inc(s.lg.sem, 1)

            g = L.lags
            stages = [(copy_pt, g.turn)] + ([(copy_logits, g.route)] if L.router else [])
            stages += [(copy_xt, g.turn_x)] if L.transposes else []
            stages += [(exponent, g.scores), (copy_qkv, 0)] + ([(square, g.out)] if L.rms else [])
            stages += [(copy_av, g.turn), (spread_v, g.values_in)]
            run(act, L, stages)

        def soft_dve(L):
            s, dve = L.s, nc.vector

            def bank(us):
                return ps[:, 0:2, :].rearrange("p c (n t) -> p (c n) t", t=64)

            def top(i, k):
                u, us, p, slot, a = at(L, i, k)
                wait_done(dve, s.scored, u)
                dve.tensor_reduce(scores_max[:, us], bank(us), AX.X, ALU.max).then_inc(s.maxed.sem, 1)

            def below_top(i, k):
                u, us, p, slot, a = at(L, i, k)
                wait_done(dve, s.maxed, u)
                wait_freed(dve, s.pt1, u, 2)
                dve.tensor_tensor(sd[:, us].rearrange("p (n t) -> p n t", t=64), bank(us),
                                  scores_max[:, us, :, None].broadcast_to([P, 16, 64]), ALU.subtract).then_inc(s.subbed.sem, 1)

            def inverse_sum(i, k):
                u, us, p, slot, a = at(L, i, k)
                wait_done(dve, s.exped, u)
                dve.tensor_reduce(scores_sum[:, us], sd[:, us].rearrange("p (n t) -> p n t", t=64), AX.X,
                                  ALU.add).then_inc(s.summed.sem, 1)
                wait_done(dve, s.summed, u)
                wait_freed(dve, s.normed, u, 2)
                dve.reciprocal(scores_inv[:, us], scores_sum[:, us]).then_inc(s.inv.sem, 1)

            def copy_pt(i, k):
                u, us, p, slot, a = at(L, i, k)
                wait_done(dve, s.pt1, u)
                wait_freed(dve, s.av, u, 1, 2 if L.kind == "latent" else 1)
                dve.tensor_copy(pT[:, 4:8], ps[:, 3, :].rearrange("p (n t) -> p n t", n=4)).then_inc(s.ptc1.sem, 1)

            def spread_v(i, k):
                u, us, p, slot, a = at(L, i, k)
                if a:
                    return
                wait_done(dve, s.v_psum, p)
                dve.wait_ge(s.zero.sem, s.zero.base + 1)
                wait_freed(dve, s.av, p, 2, 2)
                for b in range(2):
                    rb = slice(64 * b, 64 * b + 64)
                    for x in range(2):
                        rx = slice(64 * x, 64 * x + 64)
                        dst = vbd[rx, slot, b * P:(b + 1) * P].rearrange("p (g n) -> p g n", g=4)[:, :, 8 * x:8 * x + 8]
                        src = ps[rb, 5, 256:320].rearrange("p (g x d) -> p g x d", g=4, x=2)[:, :, x, :]
                        bias = SM.l1_vb[rb].rearrange("p (g x d) -> p g x d", g=4, x=2)[:, :, x, :]
                        ins = dve.tensor_tensor(dst, src, bias, ALU.add)
                ins.then_inc(s.vbd.sem, 1)

            def post(step):
                def stage(i, k):
                    u, us, p, slot, a = at(L, i, k)
                    if a == L.upp - 1:
                        step(p, slot)
                return stage

            def add(p, slot):
                dve_add_residual(L, None, slot, p, p, ps[:, 7, 0:D], s.o)
                if L.norm:
                    dve_norm_stats(L, p, slot)

            g = L.lags
            stages = [(copy_pt, g.turn)] + ([(post(lambda p, slot: dve_scale_rms(L, p, slot)), g.out + 1)] if L.rms else [])
            stages += [(top, g.scores), (below_top, g.scores), (post(add), g.out), (inverse_sum, g.scores)]
            if L.norm:
                stages += [(post(lambda p, slot: dve_norm(L, p, slot)), g.out)]
            if L.kind == "self1":
                stages += [(spread_v, g.values_in)]
            if L.rms:
                stages += [(post(lambda p, slot: dve_mean_square(L, p, slot)), g.out)]
            run(dve, L, stages)

        def soft_pool(L):
            s, pool = L.s, nc.gpsimd
            pool.memset(wk.vbd, 0.0).then_inc(s.zero.sem, 1)

            def load(i, k):
                u, us, p, slot, a = at(L, i, k)
                if a:
                    return
                if L.kind in ("cross", "latent"):
                    wait_freed(pool, s.qk_t, p, 2)
                    both = ctx_tok if L.kind == "latent" else k_rope
                    pool.tensor_copy(kst[:, slot].rearrange("p (x d) -> p x d", x=2),
                                     both[:, bass.ds(p, 1), :].broadcast_to([P, 2, 64])).then_inc(s.kst.sem, 1)
                    if L.kind == "latent":
                        wait_freed(pool, s.scored, p, 2)
                        pool.tensor_copy(qts[:, slot], q_lat[:, :, bass.ds(p * P, P)]).then_inc(s.q.sem, 1)
                        return
                    xr, part2 = kbd[:, slot, 512:768], kbd[:, slot, 768:1024]
                    pool.tensor_copy(xr.rearrange("p (a c) -> p a c", a=2), XT[:, :, bass.ds(p * P, P)]).then_inc(s.rope.sem, 1)
                    pool.wait_ge(s.rope.sem, s.rope.base + 4 * p + 1)
                    hv = lambda t: t.rearrange("p (n x d) -> p n x d", x=2, d=8)
                    for x in range(2):
                        ins = pool.tensor_tensor(hv(part2)[:, :, x], hv(xr)[:, :, 1 - x], hv(rope_w[:, 1])[:, :, x], ALU.mult)
                        ins.then_inc(s.rope.sem, 1)
                    pool.wait_ge(s.rope.sem, s.rope.base + 4 * p + 3)
                    pool.tensor_tensor(xr, xr, rope_w[:, 0], ALU.mult).then_inc(s.rope.sem, 1)
                    pool.wait_ge(s.rope.sem, s.rope.base + 4 * p + 4)
                    by_tile = lambda t: t.rearrange("p (g c a d) -> p a c g d", g=4, c=2, a=2)
                    for m in range(2):
                        ins = pool.tensor_tensor(xq[:, slot, m * P:(m + 1) * P].rearrange("p (c g d) -> p c g d", c=2, g=4),
                                                 by_tile(xr)[:, m], by_tile(part2)[:, m], ALU.add)
                    ins.then_inc(s.xq.sem, 1)
                    return
                wait_freed(pool, s.v_psum, p, 2)
                pool.tensor_copy(xts[:, slot], XT[:, :, bass.ds(p * P, P)]).then_inc(s.xts.sem, 1)
                if L.bias_x:
                    pool.tensor_tensor(X[:, p, :], X[:, p, :], SM.l1_ob, ALU.add).then_inc(s.xb.sem, 1)

            def spread_k(i, k):
                u, us, p, slot, a = at(L, i, k)
                if a or L.kind == "latent":
                    return
                wait_done(pool, s.k, p)
                wait_freed(pool, s.scored, p, 2, L.upp)
                heads, mask = (8, T.mask_g8) if L.kind == "self1" else (4, T.mask_g4)
                for m in range(2 if L.kind == "self0" else 1):
                    n = 2 * heads * 64
                    dst = kbd[:, slot, m * n:(m + 1) * n].rearrange("p (b g t) -> p b g t", b=2, g=heads)
                    keys = kT[:, slot, m].rearrange("p (b t) -> p b t", b=2)[:, :, None, :].broadcast_to([P, 2, heads, 64])
                    ins = pool.tensor_tensor(dst, keys, mask[:, None, :, None].broadcast_to([P, 2, heads, 64]), ALU.mult)
                ins.then_inc(s.kbd.sem, 1)

            def divide(i, k):
                u, us, p, slot, a = at(L, i, k)
                wait_done(pool, s.inv, u)
                pr = sd[:, us].rearrange("p (n t) -> p n t", t=64)
                pool.tensor_tensor(pr, pr, scores_inv[:, us, :, None].broadcast_to([P, 16, 64]), ALU.mult).then_inc(s.normed.sem, 1)

            def post(step):
                def stage(i, k):
                    u, us, p, slot, a = at(L, i, k)
                    if a == L.upp - 1:
                        step(p, slot)
                return stage

            g = L.lags
            stages = [(load, g.scores if L.kind in ("self0", "self1") else 0)]
            if L.norm:
                stages += [(post(lambda p, slot: pool_rstd(L, p, slot)), g.out)]
            stages += [(divide, g.scores), (post(lambda p, slot: pool_store_x(L, p, slot, p)), g.out), (spread_k, 0)]
            if L.rms:
                stages += [(post(lambda p, slot: pool_rms(L, p, slot)), g.out)]
            if L.transposes:
                stages += [(post(lambda p, slot: pool_store_xt(L, p, slot, p)), g.turn_x)]
            run(pool, L, stages)

        def cross_keys_dve():
            s, dve = prep.s, nc.vector
            sq, kw, part2 = k_tmp[:, 0], k_tmp[:, 1], k_tmp[:, 2]
            dve.wait_ge(ld.ctx.sem, ld.ctx.base + 16)
            dve.wait_ge(ld.small.sem, ld.small.base + 16)
            dve.wait_ge(ld.tables.sem, ld.tables.base + 16)
            n = [0]

            def step(ins):
                n[0] += 1
                ins.then_inc(s.dve_keys.sem, 1)
                dve.wait_ge(s.dve_keys.sem, s.dve_keys.base + n[0])

            ss, r = scores_sum[:, 0, :], scores_sum[:, 1, :]
            step(dve.tensor_tensor(sq, ctx_tok[:, :, :], ctx_tok[:, :, :], ALU.mult))
            step(dve.tensor_reduce(ss, sq, AX.X, ALU.add))
            dve.tensor_scalar(ss, ss, 1.0 / DC, 1e-5, ALU.mult, ALU.add).then_inc(s.key_ms.sem, 1)
            dve.wait_ge(s.key_rms.sem, s.key_rms.base + 1)
            step(dve.tensor_tensor(kw, ctx_tok[:, :, :], r[:, :, None].broadcast_to([P, PAIRS, DC]), ALU.mult))
            step(dve.tensor_tensor(kw, kw, SM.x_knw[:, None, :].broadcast_to([P, PAIRS, DC]), ALU.mult))
            v = lambda t: t.rearrange("p t (n x d) -> p (t n) x d", x=2, d=8)
            for x in range(2):
                table = T.sin16[:, None, 8 * x:8 * x + 8].broadcast_to([P, 64, 8])
                step(dve.tensor_tensor(v(part2)[:, :, x], v(kw)[:, :, 1 - x], table, ALU.mult))
            w = lambda t: t.rearrange("p t (n d) -> p (t n) d", d=16)
            step(dve.tensor_tensor(w(sq), w(kw), T.cos16[:, None, :].broadcast_to([P, 64, 16]), ALU.mult))
            dve.tensor_tensor(k_rope, sq, part2, ALU.add).then_inc(s.keys.sem, 1)
            wn = SM.x_qnw.rearrange("p (n d) -> p n d", d=16)
            dve.tensor_tensor(rope_w[:, 0].rearrange("p (n d) -> p n d", d=16), wn, T.cos16[:, None, :].broadcast_to([P, 16, 16]),
                              ALU.mult).then_inc(s.rope_w.sem, 1)
            h = lambda t: t.rearrange("p (n x d) -> p n x d", x=2, d=8)
            for x in range(2):
                dve.tensor_tensor(h(rope_w[:, 1])[:, :, x], h(SM.x_qnw)[:, :, 1 - x],
                                  T.sin16[:, None, 8 * x:8 * x + 8].broadcast_to([P, 16, 8]), ALU.mult).then_inc(s.rope_w.sem, 1)

        def cross_keys_pool():
            nc.gpsimd.wait_ge(prep.s.key_ms.sem, prep.s.key_ms.base + 1)
            nc.gpsimd.tensor_tensor(scores_sum[:, 1, :], scores_sum[:, 0, :], T.negsq.broadcast_to([P, 16]), ALU.pow).then_inc(prep.s.key_rms.sem, 1)

        prep = named(s=sems("prep", "dve_keys key_ms key_rms keys rope_w"))

        moe = sems("moe", "top idx gap ex one p1 p2 idxf hot hot1 hot2 cw cwe gu silu h h_high h_low w_high w_low down acc")
        best = sbuf("best", [P, PAIRS, 8])
        best_at = sbuf("best_at", [P, PAIRS, 8], U32)
        best_f = sbuf("best_f", [P, PAIRS, 8])
        hot = sbuf("hot", [P, 2, PAIRS, E])
        share = sbuf("share", [P, 4, PAIRS])
        cw = sbuf("cw", [P, E, PAIRS])
        cwe = sbuf("cwe", [P, 2, PAIRS])
        raw = [mid[:, (1 - n) * 6144 + 3072:(1 - n) * 6144 + 6144] for n in range(2)]
        w_parts = [mid_r[:, (1 - n) * 6144:(1 - n) * 6144 + 6144].rearrange("p (n w) -> p n w", n=2) for n in range(2)]
        expert = [[part(w_parts[n][:, x], EXPERT) for x in range(2)] for n in range(2)]
        hidden = big_r[:, 0:8192].rearrange("p (b n m t) -> p b n m t", b=2, n=2, m=4)
        PRODUCTS = ((0, 0), (0, 1), (1, 0))
        h_full = wk.kbd[:, 0:1024].rearrange("p (b n) -> p b n", b=2)
        silu = wk.sd.rearrange("p (b n) -> p b n", b=2)[:, :, 0:512]
        CHUNKS, MT = TOK // GT, I // P

        def route_dve():
            dve = nc.vector
            for p in range(PAIRS):
                dve.max(best[:, p], logits[:, p]).then_inc(moe.top.sem, 1)
            for p in range(PAIRS):
                dve.wait_ge(moe.top.sem, p + 1)
                dve.max_index(best_at[:, p], best[:, p], logits[:, p]).then_inc(moe.idx.sem, 1)
            dve.tensor_tensor(share[:, 0], best[:, :, 1], best[:, :, 0], ALU.subtract).then_inc(moe.gap.sem, 1)
            dve.wait_ge(moe.idx.sem, PAIRS)
            dve.tensor_copy(best_f[:, :, :], best_at[:, :, :]).then_inc(moe.idxf.sem, 1)
            dve.wait_ge(moe.ex.sem, 1)
            dve.tensor_scalar(share[:, 1], share[:, 0], 1.0, None, ALU.add).then_inc(moe.one.sem, 1)
            dve.wait_ge(moe.one.sem, 1)
            dve.reciprocal(share[:, 2], share[:, 1]).then_inc(moe.p1.sem, 1)
            dve.wait_ge(moe.p1.sem, 1)
            dve.tensor_tensor(share[:, 3], share[:, 0], share[:, 2], ALU.mult).then_inc(moe.p2.sem, 1)
            dve.wait_ge(moe.idxf.sem, 1)
            dve.wait_ge(moe.p2.sem, 1)
            iota = T.iota8[:, None, :].broadcast_to([P, PAIRS, E])
            for n in range(2):
                dve.tensor_tensor(hot[:, n], iota, best_f[:, :, n:n + 1].broadcast_to([P, PAIRS, E]),
                                  ALU.is_equal).then_inc(moe.hot.sem, 1)
            for n in range(2):
                dve.wait_ge(moe.hot.sem, n + 1)
                dve.tensor_tensor(hot[:, n], hot[:, n], share[:, 2 + n, :, None].broadcast_to([P, PAIRS, E]),
                                  ALU.mult).then_inc(moe.hot1.sem, 1)
            dve.wait_ge(moe.hot1.sem, 2)
            dve.tensor_tensor(cw[:, :, :].rearrange("p e t -> p t e"), hot[:, 0], hot[:, 1], ALU.add).then_inc(moe.cw.sem, 1)

        def route_act():
            nc.scalar.wait_ge(moe.gap.sem, 1)
            nc.scalar.activation(share[:, 0], share[:, 0], ACT.Exp).then_inc(moe.ex.sem, 1)

        def moe_place(i, k):
            return 2 * CHUNKS * i + k, k % 2, 2 * i + k // CHUNKS, k // CHUNKS, k % CHUNKS

        def moe_pe():
            pe = nc.tensor

            def gate_up(i, k):
                u, us, e, slot, c = moe_place(i, k)
                if c == 0:
                    pe.wait_ge(moe.w_low.sem, e + 1)
                for m in range(MT):
                    j = MT * u + m
                    wait_freed(pe, moe.h, j, 2)
                    for n, name in enumerate(("gate", "up")):
                        for y, (a, b) in enumerate(PRODUCTS):
                            w = (expert[slot][a].gate, expert[slot][a].up)[n]
                            for kc in range(KC):
                                mm = pe.matmul(ps[:, 2 * n + m % 2, :], w[:, kc * I + m * P:kc * I + (m + 1) * P],
                                               x_parts[:, b, kc, c * GT:(c + 1) * GT], start=y + kc == 0, stop=y + kc == 3)
                    mm.then_inc(moe.gu.sem, 1)

            def down(i, k):
                u, us, e, slot, c = moe_place(i, k)
                for t in range(4):
                    j = 4 * u + t
                    wait_freed(pe, moe.acc, j, 4)
                    for m in range(MT):
                        if t == 0:
                            pe.wait_ge(moe.h_low.sem, MT * u + m + 1)
                        for y, (a, b) in enumerate(PRODUCTS):
                            mm = pe.matmul(ps[:, 4 + t, 0:D], hidden[:, us, a, m, t * P:(t + 1) * P],
                                           expert[slot][b].down[:, m * D:(m + 1) * D], start=m + y == 0, stop=m + y == MT + 1)
                    mm.then_inc(moe.down.sem, 1)

            pipelined(pe, E // 2, 2 * CHUNKS, [(gate_up, 0), (down, 1)])

        def moe_act():
            act = nc.scalar

            def gate(i, k):
                u, us, e, slot, c = moe_place(i, k)
                for m in range(MT + 1):
                    if m < MT:
                        j = MT * u + m
                        wait_done(act, moe.gu, j)
                        wait_freed(act, moe.h, j, 2)
                        act.activation(silu[:, m % 2], ps[:, m % 2, :], ACT.Silu).then_inc(moe.silu.sem, 1)
                    if m == 0:
                        wait_freed(act, moe.down, u, 2, 4)
                    else:
                        wait_done(act, moe.h, MT * u + m - 1)
                        act.activation(hidden[:, us, 0, m - 1], h_full[:, (m - 1) % 2], ACT.Copy).then_inc(moe.h_high.sem, 1)

            pipelined(act, E // 2, 2 * CHUNKS, [(gate, 0)])

        def moe_dve():
            dve = nc.vector

            def gated(i, k):
                u, us, e, slot, c = moe_place(i, k)
                wait_freed(dve, moe.down, u, 2, 4)
                for m in range(MT + 1):
                    if m < MT:
                        wait_done(dve, moe.silu, MT * u + m)
                        wait_freed(dve, moe.h_low, MT * u + m, 2)
                        dve.tensor_tensor(h_full[:, m % 2], silu[:, m % 2], ps[:, 2 + m % 2, :], ALU.mult).then_inc(moe.h.sem, 1)
                    if m:
                        wait_done(dve, moe.h_high, MT * u + m - 1)
                        dve.tensor_tensor(hidden[:, us, 1, m - 1], h_full[:, (m - 1) % 2], hidden[:, us, 0, m - 1].bitcast(F32),
                                          ALU.subtract).then_inc(moe.h_low.sem, 1)

            def accumulate(i, k):
                u, us, e, slot, c = moe_place(i, k)
                if c == 0:
                    dve.wait_ge(moe.cwe.sem, e + 1)
                for t in range(4):
                    wait_done(dve, moe.down, 4 * u + t)
                    if not (isinstance(u, int) and u < CHUNKS):
                        dve.wait_ge(moe.acc.sem, 4 * u + t + 1 - 4 * CHUNKS)
                    q = 4 * c + t
                    dve.scalar_tensor_tensor(out=X[:, q], in0=ps[:, 4 + t, 0:D], scalar=cwe[:, slot, q:q + 1], in1=X[:, q],
                                             op0=ALU.mult, op1=ALU.add).then_inc(moe.acc.sem, 1)

            pipelined(dve, E // 2, 2 * CHUNKS, [(gated, 0), (accumulate, 1)])

        def split_expert(e):
            pool = nc.gpsimd
            pool.wait_ge((ld.expert0, ld.expert1)[e % 2].sem, 16 * (e // 2) + 16)
            pool.tensor_copy(w_parts[e % 2][:, 0], raw[e % 2]).then_inc(moe.w_high.sem, 1)
            pool.wait_ge(moe.w_high.sem, e + 1)
            pool.tensor_tensor(w_parts[e % 2][:, 1], raw[e % 2], w_parts[e % 2][:, 0].bitcast(F32), ALU.subtract).then_inc(moe.w_low.sem, 1)

        def moe_pool():
            pool = nc.gpsimd
            pool.wait_ge(moe.cw.sem, 1)
            for e in range(E):
                if e >= 2:
                    pool.wait_ge(moe.acc.sem, 4 * CHUNKS * (e - 1))
                pool.tensor_copy(cwe[:, e % 2], cw[:, e]).then_inc(moe.cwe.sem, 1)
                if e + 1 < E:
                    split_expert(e + 1)

        def each(step):
            def stage(i, k):
                step(2 * i + k, k)
            return stage

        def norm_dve(L):
            def copy(p, slot):
                wait_freed(nc.vector, L.s.x_stored, p, 2)
                wait_freed(nc.vector, L.s.xtr, p, 2)
                nc.vector.tensor_copy(xn[:, slot], X[:, p, :]).then_inc(L.s.y.sem, 1)
                dve_norm_stats(L, p, slot)
            run(nc.vector, L, [(each(copy), 0), (each(lambda p, slot: dve_norm(L, p, slot)), 1)])

        def norm_pool(L):
            run(nc.gpsimd, L, [(each(lambda p, slot: pool_rstd(L, p, slot)), 0),
                               (each(lambda p, slot: pool_store_x(L, p, slot, p)), 1),
                               (each(lambda p, slot: pool_store_xt(L, p, slot, p)), 2)])

        fold = sems("fold", "psum act dve kv")
        lw = part(big, LATENT)
        fold_q = mid[:, 0:6144].rearrange("p (k n) -> p k n", k=KC)
        fold_s = mid[:, 6144:10240].rearrange("p (g x n c) -> p g x n c", g=4, x=2, n=4)
        TILE_PAIRS = [(0, 0), (1, 0), (1, 1), (2, 1)]
        steps = [("q", h, "act" if h % 2 else "dve") for h in range(H1)]
        steps += [("s", n, "dve") for n in range(8)] + [("o", n, "act") for n in range(8)]

        def copied_through(n):
            who = steps[n][2]
            return (fold.act if who == "act" else fold.dve), sum(s[2] == who for s in steps[:n + 1])

        def fold_pe():
            pe = nc.tensor
            pe.wait_ge(ld.latent.sem, 16)
            for n, (kind, at0, who) in enumerate(steps):
                if n >= 8:
                    sem, count = copied_through(n - 8)
                    pe.wait_ge(sem.sem, count)
                bank = ps[:, n % 8, :]
                if kind == "q":
                    for kc in range(KC):
                        mm = pe.matmul(bank[:, kc * QC:(kc + 1) * QC], lw.wq[:, at0 * D + kc * P:at0 * D + (kc + 1) * P],
                                       lw.wkcq[:, at0 * QC:(at0 + 1) * QC], start=True, stop=True)
                elif kind == "s":
                    g, x = at0 // 2, at0 % 2
                    for m, (t, pair) in enumerate(TILE_PAIRS):
                        row = x * H1 * QH + (3 * g + t) * P
                        mm = pe.matmul(bank[:, m * P:(m + 1) * P], lw.wqr[0:KV, row:row + P],
                                       lw.wkr[0:KV, (4 * g + 2 * pair) * KV:(4 * g + 2 * pair + 2) * KV], start=True, stop=True)
                else:
                    c, hp = at0 // 4, at0 % 4
                    for x in range(2):
                        h = 2 * (2 * hp + x) + c
                        mm = pe.matmul(bank[64 * x:64 * x + 64, 0:D], lw.wkckv[:, h * KV:(h + 1) * KV], lw.wo[:, h * D:(h + 1) * D],
                                       start=True, stop=True)
                mm.then_inc(fold.psum.sem, 1)

        def fold_copies(eng, who):
            for n, (kind, at0, by) in enumerate(steps):
                if by != who:
                    continue
                eng.wait_ge(fold.psum.sem, n + 1)
                bank = ps[:, n % 8, :]
                if kind == "q":
                    dst = mid[:, 0:6144].rearrange("p (k x n) -> p k x n", k=KC, x=2)[:, :, :, at0 * QH:(at0 + 1) * QH]
                    src = bank[:, 0:KC * QC].rearrange("p (k x n) -> p k x n", k=KC, x=2)
                    if who == "act":
                        eng.activation(dst, src, ACT.Copy).then_inc(fold.act.sem, 1)
                    else:
                        eng.tensor_copy(dst, src).then_inc(fold.dve.sem, 1)
                elif kind == "s":
                    eng.tensor_tensor(fold_s[:, at0 // 2, at0 % 2].rearrange("p n (x c) -> p (n x) c", x=2),
                                      bank.rearrange("p (m c) -> p m c", m=8), T.mask_fold[:, :, None].broadcast_to([P, 8, KV]),
                                      ALU.mult).then_inc(fold.dve.sem, 1)
                else:
                    eng.activation(fold_o[:, at0], bank[:, 0:D], ACT.Copy).then_inc(fold.act.sem, 1)

        def rotate_kv_dve():
            dve = nc.vector
            t1 = work[:, 0:1024].rearrange("p (t n) -> p t n", t=PAIRS)
            t2 = work[:, 1024:2048].rearrange("p (t n) -> p t n", t=PAIRS)
            dve.tensor_tensor(t1, ctx_tok[:, :, :], T.cos64[:, None, :].broadcast_to([P, PAIRS, KV]), ALU.mult).then_inc(fold.kv.sem, 1)
            for x in range(2):
                dst, src = slice(32 * x, 32 * x + 32), slice(32 - 32 * x, 64 - 32 * x)
                dve.tensor_tensor(t2[:, :, dst], ctx_tok[:, :, src], T.sin64[:, None, dst].broadcast_to([P, PAIRS, 32]),
                                  ALU.mult).then_inc(fold.kv.sem, 1)
            dve.wait_ge(fold.kv.sem, 3)
            dve.tensor_tensor(ctx_tok[:, :, :], t1, t2, ALU.add).then_inc(fold.kv.sem, 1)

        qry = sems("qry", "q mult sub add t out")
        turned = work[:, 0:4096].rearrange("p (b n t) -> p b n t", b=2, n=4)
        rotated = work[:, 4096:7168].rearrange("p (n x t) -> p n x t", n=3, x=2)
        rope_q = T.rope_q.rearrange("p (n t s) -> p n t s", n=4, t=3)

        def query_pe():
            pe = nc.tensor

            def make(i, k):
                u = 4 * i + k
                for t in range(3):
                    j = 3 * u + t
                    wait_freed(pe, qry.mult, j, 3)
                    for x in range(2):
                        for kc in range(KC):
                            at0 = x * H1 * QH + (3 * k + t) * P
                            mm = pe.matmul(ps[:, 2 * t + x, :], fold_q[:, kc, at0:at0 + P], XT[:, kc, bass.ds(i * GT, GT)],
                                           start=kc == 0, stop=kc == 1)
                    mm.then_inc(qry.q.sem, 1)

            def to_keys(i, k):
                u = 4 * i + k
                wait_done(pe, qry.add, u, 3)
                wait_freed(pe, qry.out, u, 1, 2)
                for pair in range(2):
                    terms = [(x, m, t) for m, (t, q) in enumerate(TILE_PAIRS) if q == pair for x in range(2)]
                    for n, (x, m, t) in enumerate(terms):
                        mm = pe.matmul(ps[:, 6 + pair, :], fold_s[:, k, x, m], rotated[:, t, x], start=n == 0, stop=n == 3)
                    mm.then_inc(qry.t.sem, 1)

            pipelined(pe, TOK // GT, 4, [(make, 0), (to_keys, 1)])

        def query_dve():
            dve = nc.vector

            def mult(i, k):
                u = 4 * i + k
                for t in range(3):
                    j = 3 * u + t
                    b = (3 * k + t) % 2
                    wait_done(dve, qry.q, j)
                    wait_freed(dve, qry.add, j, 2)
                    for n, x in enumerate((0, 1, 1, 0)):
                        table = rope_q[:, (0, 1, 2, 3)[n], t, None, :].broadcast_to([P, GT // S, S])
                        ins = dve.tensor_tensor(turned[:, b, n].rearrange("p (b s) -> p b s", s=S),
                                                ps[:, 2 * t + x, :].rearrange("p (b s) -> p b s", s=S), table, ALU.mult)
                    ins.then_inc(qry.mult.sem, 1)

            pipelined(dve, TOK // GT, 4, [(mult, 0)])

        def query_pool():
            pool = nc.gpsimd

            def combine(i, k):
                u = 4 * i + k
                wait_freed(pool, qry.t, u, 1, 2)
                for t in range(3):
                    j = 3 * u + t
                    b = (3 * k + t) % 2
                    wait_done(pool, qry.mult, j)
                    pool.tensor_tensor(rotated[:, t, 0], turned[:, b, 0], turned[:, b, 1], ALU.subtract)
                    pool.tensor_tensor(rotated[:, t, 1], turned[:, b, 2], turned[:, b, 3], ALU.add).then_inc(qry.add.sem, 1)

            pipelined(pool, TOK // GT, 4, [(combine, 0)])

        def query_act():
            act = nc.scalar

            def copy(i, k):
                u = 4 * i + k
                for pair in range(2):
                    wait_done(act, qry.t, 2 * u + pair)
                    act.activation(q_lat[:, 2 * k + pair, bass.ds(i * GT, GT)], ps[:, 6 + pair, :], ACT.Copy).then_inc(qry.out.sem, 1)

            pipelined(act, TOK // GT, 4, [(copy, 0)])

        tern = sems("tern", "sums total mean inv scaled rounded up down gs")
        fw = part(mid, FFN)
        up_q = XT[:, 0, 0:KC * HID // 2].bitcast(BF16)
        tst = sbuf("tst", [P, 8])
        xq_t = sbuf("xq_t", [P, 2, KC, P], BF16)
        gs = small[:, pieces(SMALL)[0]["f_gamma"][0]:pieces(SMALL)[0]["f_gamma"][1]]

        def ternary_dve():
            dve = nc.vector
            dve.wait_ge(ld.ffn.sem, 16)
            for n, w in enumerate((fw.up, fw.down)):
                dve.tensor_reduce(tst[:, n:n + 1], w, AX.X, ALU.add, apply_absolute_value=True).then_inc(tern.sums.sem, 1)
            dve.wait_ge(tern.total.sem, 1)
            dve.tensor_scalar(tst[:, 2:4], ps[:, 0, 0:2], 1.0 / (D * HID), 1e-8, ALU.mult, ALU.max).then_inc(tern.mean.sem, 1)
            dve.wait_ge(tern.mean.sem, 1)
            dve.reciprocal(tst[:, 4:6], tst[:, 2:4]).then_inc(tern.inv.sem, 1)
            dve.wait_ge(tern.inv.sem, 1)
            for n, w in enumerate((fw.up, fw.down)):
                dve.tensor_scalar(w, w, tst[:, 4 + n:5 + n], ROUND, ALU.mult, ALU.add).then_inc(tern.scaled.sem, 1)
                dve.wait_ge(tern.scaled.sem, n + 1)
                dve.tensor_scalar(w, w, ROUND, 1.0, ALU.subtract, ALU.min).then_inc(tern.rounded.sem, 1)
                dve.wait_ge(tern.rounded.sem, n + 1)
                dve.tensor_scalar((up_q, w)[n], w, -1.0, None, ALU.max).then_inc((tern.up, tern.down)[n].sem, 1)
            dve.tensor_scalar(gs, SM.f_gamma, tst[:, 3:4], None, ALU.mult).then_inc(tern.gs.sem, 1)

        def ternary_pe():
            nc.tensor.wait_ge(tern.sums.sem, 2)
            nc.tensor.matmul(ps[:, 0, 0:2], ones[:, :], tst[:, 0:2], start=True, stop=True).then_inc(tern.total.sem, 1)

        def ffn_act():
            s, act = ffn.s, nc.scalar

            def square(p, slot):
                wait_freed(act, s.xo, p, 2)
                act.activation(xo[:, slot], X[:, p, :], ACT.Square, accum_out=stat_cols(slot, 12)).then_inc(s.ss.sem, 1)

            def copy_x(p, slot):
                wait_done(act, s.xtr, p)
                wait_freed(act, s.scored, p, 2)
                act.activation(xq_t[:, slot], ps[:, 5, 0:256].rearrange("p (k t) -> p k t", k=KC), ACT.Copy).then_inc(s.xe.sem, 1)

            def gate(p, slot):
                wait_done(act, s.scored, p)
                wait_done(act, s.part, p)
                wait_freed(act, s.pt1, p, 2)
                for n in range(2):
                    ins = act.activation(sd[:, slot, n * 512:(n + 1) * 512], ps[:, n, :], ACT.Silu, scale=stat_cols(slot, 20))
                ins.then_inc(s.exped.sem, 1)

            def copy_pt(p, slot):
                wait_done(act, s.pt0, p)
                wait_freed(act, s.o, p, 1)
                act.activation(pT[:, 0:4], ps[:, 2, :].rearrange("p (n t) -> p n t", n=4), ACT.Copy).then_inc(s.ptc0.sem, 1)

            run(act, ffn, [(each(square), 0), (each(copy_x), 1), (each(gate), 1), (each(copy_pt), 2)])

        def ffn_pool():
            run(nc.gpsimd, ffn, [(each(lambda p, slot: pool_rms(ffn, p, slot)), 0),
                                 (each(lambda p, slot: pool_rstd(ffn, p, slot)), 3),
                                 (each(lambda p, slot: pool_store_x(ffn, p, slot, p)), 3)])

        def ffn_dve():
            s, dve = ffn.s, nc.vector
            xw = wk.xe.rearrange("p (b n) -> p b n", b=2)

            def quantize(p, slot):
                dve_mean_square(named(s=s, rms=1e-6), p, slot)
                wait_done(dve, s.rr, p)
                wait_freed(dve, s.q1, p, 2)
                dve.scalar_tensor_tensor(out=xw[:, slot], in0=X[:, p, :], scalar=stat_cols(slot, 14), in1=SM.f_nw, op0=ALU.mult,
                                         op1=ALU.mult).then_inc(s.xw.sem, 1)
                wait_done(dve, s.xw, p)
                dve.tensor_reduce(stat_cols(slot, 16), xw[:, slot], AX.X, ALU.max, apply_absolute_value=True).then_inc(s.amax.sem, 1)
                wait_done(dve, s.amax, p)
                dve.tensor_scalar(stat_cols(slot, 17), stat_cols(slot, 16), 1e-8, None, ALU.max).then_inc(s.gam.sem, 1)
                wait_done(dve, s.gam, p)
                wait_freed(dve, s.exped, p, 2)
                dve.reciprocal(stat_cols(slot, 18), stat_cols(slot, 17)).then_inc(s.inv_gam.sem, 1)
                dve.tensor_scalar(stat_cols(slot, 20), stat_cols(slot, 17), 1.0 / 127.0, tst[:, 2:3], ALU.mult,
                                  ALU.mult).then_inc(s.part.sem, 1)
                wait_done(dve, s.inv_gam, p)
                dve.tensor_scalar(xw[:, slot], xw[:, slot], 127.0, stat_cols(slot, 18), ALU.mult, ALU.mult).then_inc(s.q1.sem, 1)
                wait_done(dve, s.q1, p)
                dve.tensor_scalar(xw[:, slot], xw[:, slot], ROUND, ROUND, ALU.add, ALU.subtract).then_inc(s.q2.sem, 1)
                wait_done(dve, s.q2, p)
                wait_freed(dve, s.xtr, p, 2)
                dve.tensor_scalar(xo[:, slot], xw[:, slot], 127.0, -127.0, ALU.min, ALU.max).then_inc(s.xo.sem, 1)

            def copy_pt(p, slot):
                wait_done(dve, s.pt1, p)
                wait_freed(dve, s.o, p, 1)
                dve.tensor_copy(pT[:, 4:8], ps[:, 3, :].rearrange("p (n t) -> p n t", n=4)).then_inc(s.ptc1.sem, 1)

            def add(p, slot):
                wait_done(dve, s.o, p)
                wait_freed(dve, s.x_stored, p, 2)
                dve.tensor_tensor(xn[:, slot], ps[:, 7, 0:D], gs, ALU.mult).then_inc(s.down.sem, 1)
                wait_done(dve, s.down, p)
                dve.scalar_tensor_tensor(out=xn[:, slot], in0=X[:, p, :], scalar=2.0, in1=xn[:, slot], op0=ALU.mult,
                                         op1=ALU.add).then_inc(s.y.sem, 1)
                dve_norm_stats(ffn, p, slot)

            run(dve, ffn, [(each(quantize), 0), (each(add), 3), (each(copy_pt), 2), (each(lambda p, slot: dve_norm(ffn, p, slot)), 3)])

        def ffn_pe():
            s, pe = ffn.s, nc.tensor
            pe.wait_ge(tern.up.sem, 1)
            pe.wait_ge(tern.down.sem, 1)

            def turn_x(p, slot):
                wait_done(pe, s.xo, p)
                wait_freed(pe, s.xe, p, 1)
                for kc in range(KC):
                    mm = pe.transpose(ps[:, 5, kc * P:(kc + 1) * P], xo[:, slot, kc * P:(kc + 1) * P], T.ident)
                mm.then_inc(s.xtr.sem, 1)

            def up(p, slot):
                wait_done(pe, s.xe, p)
                wait_freed(pe, s.exped, p, 1)
                for n in range(2):
                    for kc in range(KC):
                        mm = pe.matmul(ps[:, n, :], xq_t[:, slot, kc], up_q[:, kc * HID + n * 512:kc * HID + (n + 1) * 512],
                                       start=kc == 0, stop=kc == 1)
                mm.then_inc(s.scored.sem, 1)

            def turn(p, slot):
                wait_done(pe, s.exped, p)
                for half, copied, full in ((0, s.ptc0, s.pt0), (1, s.ptc1, s.pt1)):
                    wait_freed(pe, copied, p, 1)
                    for n in range(4):
                        mm = pe.transpose(ps[:, 2 + half, n * P:(n + 1) * P], sd[:, slot, (4 * half + n) * P:(4 * half + n + 1) * P],
                                          T.ident)
                    mm.then_inc(full.sem, 1)

            def down(p, slot):
                wait_done(pe, s.ptc0, p)
                wait_done(pe, s.ptc1, p)
                wait_freed(pe, s.y, p, 1)
                for n in range(8):
                    mm = pe.matmul(ps[:, 7, 0:D], pT[:, n], fw.down[:, n * D:(n + 1) * D], start=n == 0, stop=n == 7)
                mm.then_inc(s.o.sem, 1)

            run(pe, ffn, [(each(turn_x), 0), (each(down), 3), (each(up), 1), (each(turn), 2)])

        block = ctx.enter_context(nc.Block())

        @block.sync
        def _(sp):
            sp.dma_start(XT[:, :, :], dram["x_t"].rearrange("p (k t) -> p k t", k=KC)).then_inc(ld.xt.sem, 16)
            sp.dma_start(X[:, :, :], dram["x"].rearrange("(t p) c -> p t c", p=P)).then_inc(ld.x.sem, 16)
            sp.dma_start(tables[:, :], dram["tables"]).then_inc(ld.tables.sem, 16)
            sp.dma_start(small[:, :], dram["small"]).then_inc(ld.small.sem, 16)
            sp.dma_start(big[:, 0:4624], dram["early"]).then_inc(ld.early.sem, 16)
            sp.dma_start(big[:, 12288:12800], dram["causal"]).then_inc(ld.causal.sem, 16)
            sp.dma_start(ctx_tok[:, :, :], dram["ctx"].rearrange("(t p) c -> p t c", p=P)).then_inc(ld.ctx.sem, 16)
            sp.dma_start(raw[0], dram["experts"][0]).then_inc(ld.expert0.sem, 16)
            wait_sublayer(sp, cross)
            for e in range(1, E):
                if e >= 2:
                    sp.wait_ge(moe.down.sem, 4 * CHUNKS * (e - 1))
                sp.dma_start(raw[e % 2], dram["experts"][e]).then_inc((ld.expert0, ld.expert1)[e % 2].sem, 16)
            sp.wait_ge(moe.down.sem, 4 * CHUNKS * E)
            sp.dma_start(mid[:, 0:1920], dram["l1a"]).then_inc(ld.l1a.sem, 16)
            sp.dma_start(big[:, :], dram["latent"]).then_inc(ld.latent.sem, 16)
            sp.wait_ge(qry.out.sem, TOK // GT * 8)
            sp.dma_start(mid[:, 0:4096], dram["ffn"]).then_inc(ld.ffn.sem, 16)
            y = out.rearrange("(t p) c -> p t c", p=P)
            for q in range(4):
                wait_done(sp, ffn.s.x_stored, 4 * q + 3)
                sp.dma_start(y[:, 4 * q:4 * q + 4], X[:, 4 * q:4 * q + 4, :]).then_inc(stored.y.sem, 16)
            sp.wait_ge(stored.y.sem, 64)

        @block.gpsimd
        def _(pool):
            pool.memset(ones[:, :], 1.0).then_inc(setup.ones.sem, 1)
            lin_pool()
            wait_sublayer(pool, lin)
            cross_keys_pool()
            split_expert(0)
            pool.wait_ge(prep.s.keys.sem, 1)
            pool.wait_ge(prep.s.rope_w.sem, 3)
            soft_pool(cross)
            wait_sublayer(pool, cross)
            soft_pool(causal_self)
            wait_sublayer(pool, causal_self)
            moe_pool()
            pool.wait_ge(moe.acc.sem, 16 * E)
            norm_pool(moe_norm)
            wait_sublayer(pool, moe_norm)
            soft_pool(grouped)
            wait_sublayer(pool, grouped)
            pool.wait_ge(fold.kv.sem, 4)
            query_pool()
            pool.wait_ge(qry.out.sem, TOK // GT * 8)
            soft_pool(latent)
            wait_sublayer(pool, latent)
            ffn_pool()

        @block.tensor
        def _(pe):
            lin_pe()
            wait_sublayer(pe, lin)
            pe.wait_ge(setup.causal.sem, 1)
            pe.wait_ge(setup.ident.sem, 1)
            soft_pe(cross)
            wait_sublayer(pe, cross)
            soft_pe(causal_self)
            wait_sublayer(pe, causal_self)
            moe_pe()
            pe.wait_ge(moe.acc.sem, 16 * E)
            run(pe, moe_norm, [(each(lambda p, slot: pe_transpose_x(moe_norm, p, slot)), 0)])
            wait_sublayer(pe, moe_norm)
            pe.wait_ge(ld.l1a.sem, 16)
            soft_pe(grouped)
            wait_sublayer(pe, grouped)
            fold_pe()
            for n in (23, 31):
                sem, count = copied_through(n)
                pe.wait_ge(sem.sem, count)
            query_pe()
            pe.wait_ge(qry.out.sem, TOK // GT * 8)
            soft_pe(latent)
            wait_sublayer(pe, latent)
            pe.wait_ge(setup.ones.sem, 1)
            ternary_pe()
            ffn_pe()

        @block.scalar
        def _(act):
            lin_act()
            wait_sublayer(act, lin)
            soft_act(cross)
            wait_sublayer(act, cross)
            soft_act(causal_self)
            wait_sublayer(act, causal_self)
            route_act()
            moe_act()
            act.wait_ge(moe.acc.sem, 16 * E)
            run(act, moe_norm, [(each(lambda p, slot: act_copy_xt(moe_norm, p, slot)), 0)])
            wait_sublayer(act, moe_norm)
            soft_act(grouped)
            wait_sublayer(act, grouped)
            fold_copies(act, "act")
            query_act()
            act.wait_ge(fold.kv.sem, 4)
            soft_act(latent)
            wait_sublayer(act, latent)
            ffn_act()

        @block.vector
        def _(dve):
            lin_dve()
            wait_sublayer(dve, lin)
            cross_keys_dve()
            soft_dve(cross)
            wait_sublayer(dve, cross)
            soft_dve(causal_self)
            wait_sublayer(dve, causal_self)
            route_dve()
            dve.wait_ge(moe.cw.sem, 1)
            moe_dve()
            dve.wait_ge(moe.acc.sem, 16 * E)
            norm_dve(moe_norm)
            wait_sublayer(dve, moe_norm)
            soft_dve(grouped)
            wait_sublayer(dve, grouped)
            rotate_kv_dve()
            fold_copies(dve, "dve")
            dve.wait_ge(fold.kv.sem, 4)
            query_dve()
            dve.wait_ge(qry.out.sem, TOK // GT * 8)
            soft_dve(latent)
            wait_sublayer(dve, latent)
            ternary_dve()
            dve.wait_ge(tern.gs.sem, 1)
            ffn_dve()



def halves(w):
    return w.reshape(-1, P, w.shape[1]).transpose(1, 0, 2).reshape(P, -1)


def columns(v):
    return v.reshape(-1, P).T


def rows(v):
    return np.broadcast_to(v[None, :], (P, v.shape[0]))


def pack(parts, widths):
    return np.ascontiguousarray(np.concatenate([parts[n].reshape(P, w) for n, w in widths], 1))


def top64(a):
    return np.concatenate([a, np.zeros_like(a)], 0)


def layouts(i):
    x = i["x"].reshape(TOK, D)
    small = {
        "l0_qb": columns(i["L0_attn_q_b"]), "l0_kvb": rows(np.concatenate([i["L0_attn_k_b"], i["L0_attn_v_b"]])),
        "l0_ob": rows(i["L0_attn_o_b"]), "x_qnw": rows(i["L0_xattn_q_norm_w"]), "x_knw": rows(i["L0_xattn_k_norm_w"]),
        "ln1": columns(i["L0_ffn_w_ln1"]), "ln2": columns(i["L0_ffn_w_ln2"]),
        "l1_ob": rows(i["L1_attn_b_out"]), "f_nw": rows(i["L1_ffn_norm_weight"]), "f_gamma": rows(i["L1_ffn_gamma"]),
    }
    w_qkv, b_qkv = i["L1_attn_w_qkv"], i["L1_attn_b_qkv"]
    acgd = np.arange(D).reshape(8, 2, 2, 8).transpose(1, 2, 0, 3).reshape(-1)
    small["l1_qb"] = columns(b_qkv[:D][acgd])
    small["l1_kb"] = np.concatenate([b_qkv[D:D + 64]] * 2)[:, None]
    small["l1_vb"] = rows(b_qkv[D + 64:])
    xo = i["L0_xattn_w_out"].T.reshape(4, 2, 2, 16, D).transpose(2, 1, 0, 3, 4).reshape(D, D)
    early = {
        "l0_q": halves(i["L0_attn_q_w"].T), "l0_kv": halves(np.concatenate([i["L0_attn_k_w"].T, i["L0_attn_v_w"].T], 1)),
        "l0_o": halves(i["L0_attn_o_w"].T), "x_o": halves(xo), "f_q": halves(i["L0_ffn_Wq"].T), "f_k": halves(i["L0_ffn_Wk"].T),
        "f_v": halves(i["L0_ffn_Wv"].T), "f_o": halves(i["L0_ffn_Wo"].T), "f_r": halves(i["L0_ffn_Wr"].T),
    }
    wo = i["L1_attn_w_out"].T.reshape(4, 2, 2, 2, 8, D).transpose(2, 3, 0, 1, 4, 5)
    wo = np.concatenate([wo.reshape(4, 4, 16, D), np.zeros((4, 4, 16, D), wo.dtype)], 2).reshape(4 * P, D)
    l1a = {"a_q": halves(w_qkv[:D][acgd].T), "a_k": halves(np.concatenate([w_qkv[D:D + 64]] * 2, 0).T),
           "a_v": halves(w_qkv[D + 64:].T), "a_o": halves(wo)}
    wqr = i["L1_xattn_W_qr"].reshape(H1, 2, QH, KV).transpose(3, 1, 0, 2).reshape(KV, -1)
    latent = {"wq": i["L1_xattn_Wq"].reshape(H1, P, D).transpose(1, 0, 2), "wkcq": i["L1_xattn_w_kc_q"].transpose(1, 0, 2),
              "wqr": top64(wqr), "wkr": top64(i["L1_xattn_W_kr"].transpose(2, 0, 1).reshape(KV, -1)),
              "wkckv": i["L1_xattn_w_kc_kv"].transpose(1, 0, 2), "wo": halves(i["L1_xattn_Wo"].T)}
    ffn = {"up": halves(i["L1_ffn_weight_up"].T), "down": halves(i["L1_ffn_weight_down"].T)}
    experts = [pack({"gate": halves(i["L0_ffn_Wg"][e].T), "up": halves(i["L0_ffn_Wu"][e].T),
                     "down": halves(i["L0_ffn_Wd"][e].T)}, EXPERT) for e in range(E)]
    return {
        "x": np.ascontiguousarray(x), "x_t": halves(np.ascontiguousarray(x.T)), "ctx": i["ctx_512"].reshape(TOK, DC),
        "tables": shape_tables(), "causal": causal_table(), "small": pack(small, SMALL), "early": pack(early, EARLY),
        "l1a": pack(l1a, L1A), "latent": pack(latent, LATENT), "ffn": pack(ffn, FFN), "experts": np.stack(experts, 0),
    }


def kernel(**inputs):
    import concourse.bacc as _bacc
    from concourse.bass_utils import run_bass_kernel_spmd as _run

    nc = _bacc.Bacc("TRN2", target_bir_lowering=False, num_devices=1)
    arrays = layouts({n: np.asarray(a) for n, a in inputs.items()})
    arrays = {n: np.ascontiguousarray(a) for n, a in arrays.items()}
    dram = {n: nc.dram_tensor(f"in_{n}", a.shape, mybir.dt.from_np(a.dtype), kind="ExternalInput").ap() for n, a in arrays.items()}
    out = nc.dram_tensor("out_x", (TOK, D), F32, kind="ExternalOutput").ap()
    decoder(nc, dram, out)
    r = _run(nc, [{f"in_{n}": a for n, a in arrays.items()}], core_ids=[0])
    return r.results[0]["out_x"].reshape(B, S, D)
```

```python
from collections import namedtuple
from contextlib import ExitStack

import numpy as np

import concourse.bass as bass
from concourse import mybir

ALU = mybir.AluOpType
ACT = mybir.ActivationFunctionType
AX = mybir.AxisListType
F32 = mybir.dt.float32
BF16 = mybir.dt.bfloat16
F32R = mybir.dt.float32r
U32 = mybir.dt.uint32

B, S, D = 32, 64, 256
DC = 64
P = 128
PAIRS = B // 2
TOK = B * S
KC = D // P
E, I = 8, 512
GT = 512
H1, QC, KV = 16, 192, 64
QH = QC // 2
FIRST = 4
HID = 1024
LN_EPS = 1e-5
ROUND = 1.5 * 2.0 ** 23


def named(**fields):
    return namedtuple("Named", fields)(**fields)



def pieces(widths):
    at, out = 0, {}
    for name, width in widths:
        out[name] = (at, at + width)
        at += width
    return out, at


TABLES = [("ident", 128), ("kvz_mask", 136), ("cos16", 16), ("sin16", 16), ("mask_g4", 4), ("mask_g8", 8),
          ("rope_q", 12 * 64), ("cos64", 64), ("sin64", 64), ("mask_fold", 8), ("iota8", 8), ("negsq", 1)]
SMALL = [("l0_qb", 2), ("l0_kvb", 512), ("l0_ob", 256), ("x_qnw", 256), ("x_knw", 64), ("ln1", 2), ("ln2", 2),
         ("l1_qb", 2), ("l1_kb", 1), ("l1_vb", 64), ("l1_ob", 256), ("f_nw", 256), ("f_gamma", 256)]
EARLY = [("l0_q", 512), ("l0_kv", 1024), ("l0_o", 512), ("x_o", 512),
         ("f_q", 512), ("f_k", 512), ("f_v", 512), ("f_o", 512), ("f_r", 16)]
L1A = [("a_q", 512), ("a_k", 256), ("a_v", 128), ("a_o", 1024)]
LATENT = [("wq", H1 * D), ("wkcq", H1 * QC), ("wkckv", H1 * KV), ("wo", H1 * D), ("wqr", H1 * QC), ("wkr", H1 * KV)]
FFN = [("up", KC * HID), ("down", HID // P * D)]
EXPERT = [("gate", KC * I), ("up", KC * I), ("down", I // P * D)]


def rope_tables(length, dim, spread):
    inv = (np.float32(1.0) / np.float32(10000.0) ** (np.arange(0, dim, 2, dtype=np.float32) / np.float32(dim))).astype(np.float32)
    f = np.arange(length, dtype=np.float32)[:, None] * inv[None, :]
    f = np.repeat(f, 2, axis=-1) if spread else np.concatenate([f, f], -1)
    return np.sin(f).astype(np.float32), np.cos(f).astype(np.float32)


def shape_tables():
    out = {}
    r = np.arange(P)
    out["ident"] = np.eye(P)
    col = np.arange(P)
    out["kvz_mask"] = np.concatenate([r[:, None] // 16 == col[None, :] // 16, r[:, None] // 16 == np.arange(8)[None, :]], 1)
    sin, cos = rope_tables(S, 16, False)
    sign = np.where(np.arange(16) < 8, -1.0, 1.0)
    out["cos16"], out["sin16"] = np.tile(cos, (2, 1)), np.tile(sin * sign, (2, 1))
    out["mask_g4"] = (r[:, None] % 64) // 16 == np.arange(4)
    out["mask_g8"] = (r[:, None] % 64) // 8 == np.arange(8)
    sin, cos = rope_tables(S, QC, True)
    rows = (np.arange(3)[None, :] * P + r[:, None]) % QH
    kinds = [cos[:, :QH], sin[:, :QH], cos[:, QH:], sin[:, QH:]]
    out["rope_q"] = np.stack([k.T[rows] for k in kinds], 1).reshape(P, -1)
    sin, cos = rope_tables(S, KV, True)
    sign = np.where(np.arange(KV) < KV // 2, -1.0, 1.0)
    out["cos64"], out["sin64"] = np.tile(cos, (2, 1)), np.tile(sin * sign, (2, 1))
    fold = [(0, 0), (1, 0), (1, 1), (2, 1)]
    out["mask_fold"] = np.stack([(t * P + r) // QH == 2 * p + h for t, p in fold for h in range(2)], 1)
    out["iota8"] = np.tile(np.arange(8), (P, 1))
    out["negsq"] = np.full((P, 1), -0.5)
    return np.concatenate([np.asarray(out[n], np.float32).reshape(P, w) for n, w in TABLES], 1)


def causal_table():
    q = np.arange(P) % S
    return np.tile(np.where(np.arange(S)[None, :] > q[:, None], -1e30, 0.0), (1, 8)).astype(np.float32)


class Signal:

    def __init__(self, sem, base=0):
        self.sem, self.base = sem, base



def pipelined(eng, groups, per, stages, margin=2):
    deepest = max(lag for _, lag in stages)
    first = min(groups, -(-(deepest + margin) // per))
    for unit in range(first * per):
        for stage, lag in stages:
            if unit >= lag:
                stage((unit - lag) // per, (unit - lag) % per)
    if first < groups:
        with eng.Fori(first, groups) as i:
            for u in range(per):
                for stage, lag in stages:
                    stage(i + (u - lag) // per, (u - lag) % per)
    for unit in range(groups * per, groups * per + deepest):
        for stage, lag in stages:
            if unit - lag < groups * per:
                stage((unit - lag) // per, (unit - lag) % per)


def wait_done(eng, sem, unit, times=1):
    eng.wait_ge(sem.sem, sem.base + (unit + 1) * times)


def wait_freed(eng, sem, unit, back, times=1):
    if isinstance(unit, int) and unit < back:
        return
    eng.wait_ge(sem.sem, sem.base + (unit + 1 - back) * times)


def least(value, limit):
    return min(value, limit) if isinstance(value, int) else value


def decoder(nc, dram, out):
    with ExitStack() as ctx:
        def sbuf(name, shape, dt=F32):
            return ctx.enter_context(nc.sbuf_tensor(name, shape, dt))

        def signals_of(prefix, names):
            return {n: Signal(ctx.enter_context(nc.semaphore(f"{prefix}_{n}"))) for n in names.split()}

        def sems(prefix, names):
            return named(**signals_of(prefix, names))

        def part(tensor, widths, at=0):
            where, _ = pieces(widths)
            return named(**{n: tensor[:, at + a:at + b] for n, (a, b) in where.items()})

        X = sbuf("X", [P, PAIRS, D])
        with nc.sbuf_tensor("XT_r", [P, KC, TOK], F32R) as XT_r:
            pass
        XT = sbuf("XT", [P, KC, TOK])
        ctx_tok = sbuf("ctx_tok", [P, PAIRS, DC])
        with nc.sbuf_tensor("big_r", [P, 16384], F32R) as big_r, nc.sbuf_tensor("mid_r", [P, 12288], F32R) as mid_r:
            with nc.sbuf_tensor("work_r", [P, 9728], F32R) as work_r:
                pass
        big = sbuf("big", [P, 16384])
        mid = sbuf("mid", [P, 12288])
        work = sbuf("work", [P, 9728])
        tables = sbuf("tables", [P, sum(w for _, w in TABLES)])
        small = sbuf("small", [P, sum(w for _, w in SMALL)])
        causal = sbuf("causal", [P, 512], BF16)
        ident_bf = sbuf("ident_bf", [P, P], BF16)
        ones = sbuf("ones", [P, P])
        stat = sbuf("stat", [P, 256])
        scores_max = sbuf("scores_max", [P, 2, 16])
        scores_sum = sbuf("scores_sum", [P, 2, 16])
        scores_inv = sbuf("scores_inv", [P, 2, 16])
        ps = ctx.enter_context(nc.psum_tensor("ps", [P, 8, 512], F32))

        T, SM = part(tables, TABLES), part(small, SMALL)
        early = part(big, EARLY)
        l1a_w = part(mid, L1A)
        x_parts = big_r[:, 8192:16384].rearrange("p (n k t) -> p n k t", n=2, k=KC)

        def two(view, cols, n=2):
            return view.rearrange("p (b c) -> p b c", b=n)

        wk = part(work, [("xts", 512), ("qT", 512), ("kT", 512), ("kbd", 2048), ("vbd", 1024), ("sd", 2048),
                         ("pT", 1024), ("avT", 512), ("xn", 512), ("xo", 512), ("xe", 512)])
        xts = wk.xts.rearrange("p (b k t) -> p b k t", b=2, k=KC)
        qT = wk.qT.rearrange("p (b a t) -> p b a t", b=2, a=2)
        kT = wk.kT.rearrange("p (b a t) -> p b a t", b=2, a=2)
        kbd = wk.kbd.rearrange("p (b n) -> p b n", b=2)
        vbd = wk.vbd.rearrange("p (b n) -> p b n", b=2)
        sd = wk.sd.rearrange("p (b n) -> p b n", b=2)
        pT = wk.pT.rearrange("p (n t) -> p n t", n=8)
        avT = wk.avT.rearrange("p (b a t) -> p b a t", b=2, a=2)
        xn = wk.xn.rearrange("p (b c) -> p b c", b=2)
        xo = wk.xo.rearrange("p (b c) -> p b c", b=2)
        xe = wk.xe.rearrange("p (b k t) -> p b k t", b=2, k=KC)

        q_lat = nc.dram_tensor("latent_queries", (P, H1 // 2, TOK), F32, kind="Internal").ap()

        ld = sems("ld", "x0 xt0 early0 x xt ctx tables causal small early l1a latent ffn expert0 expert1")
        setup = sems("setup", "ones causal ident")
        stored = sems("out", "y")

        POST = "y stats aggr eps rstd xn x_stored ss ms rr xo xtr xe xt_stored"

        def stat_cols(slot, j, n=1):
            return stat[:, slot * 64 + j:slot * 64 + j + n]

        def dve_add_residual(L, i, slot, unit, pair, acc, out_ready, acc_times=1):
            wait_done(nc.vector, out_ready, unit, acc_times)
            if L.bias_x:
                wait_done(nc.vector, L.s.xb, unit)
            wait_freed(nc.vector, L.s.x_stored, unit, 2)
            if L.rms:
                wait_freed(nc.vector, L.s.xo, unit, 2)
            nc.vector.tensor_tensor(xn[:, slot], acc, X[:, pair, :], ALU.add).then_inc(L.s.y.sem, 1)

        def dve_norm_stats(L, unit, slot):
            wait_done(nc.vector, L.s.y, unit)
            nc.vector.bn_stats(stat_cols(slot, 0, 6), xn[:, slot]).then_inc(L.s.stats.sem, 1)
            nc.vector.wait_ge(ld.tables.sem, 16)
            wait_done(nc.vector, L.s.stats, unit)
            nc.vector.bn_aggr(stat_cols(slot, 8, 2), stat_cols(slot, 0, 6)).then_inc(L.s.aggr.sem, 1)
            wait_done(nc.vector, L.s.aggr, unit)
            nc.vector.tensor_scalar(stat_cols(slot, 10), stat_cols(slot, 9), LN_EPS, None, ALU.add).then_inc(L.s.eps.sem, 1)

        def pool_rstd(L, unit, slot):
            wait_done(nc.gpsimd, L.s.eps, unit)
            nc.gpsimd.tensor_tensor(stat_cols(slot, 11), stat_cols(slot, 10), T.negsq, ALU.pow).then_inc(L.s.rstd.sem, 1)

        def dve_norm(L, unit, slot):
            wait_done(nc.vector, L.s.rstd, unit)
            nc.vector.tensor_scalar(xn[:, slot], xn[:, slot], stat_cols(slot, 8), stat_cols(slot, 11),
                                    ALU.subtract, ALU.mult).then_inc(L.s.xn.sem, 1)

        def pool_store_x(L, unit, slot, pair):
            wait_done(nc.gpsimd, L.s.xn if L.norm else L.s.y, unit)
            if L.twice:
                nc.gpsimd.tensor_tensor(X[:, pair, :], X[:, pair, :], xn[:, slot], ALU.add).then_inc(L.s.x_stored.sem, 1)
            else:
                nc.gpsimd.tensor_copy(X[:, pair, :], xn[:, slot]).then_inc(L.s.x_stored.sem, 1)

        def act_square(L, unit, slot):
            wait_done(nc.scalar, L.s.xn if L.norm else L.s.y, unit)
            wait_freed(nc.scalar, L.s.xtr if L.transposes else L.s.xo, unit, 2)
            nc.scalar.activation(xo[:, slot], xn[:, slot], ACT.Square, accum_out=stat_cols(slot, 12)).then_inc(L.s.ss.sem, 1)

        def dve_mean_square(L, unit, slot):
            wait_done(nc.vector, L.s.ss, unit)
            nc.vector.tensor_scalar(stat_cols(slot, 13), stat_cols(slot, 12), 1.0 / D, L.rms, ALU.mult,
                                    ALU.add).then_inc(L.s.ms.sem, 1)

        def pool_rms(L, unit, slot):
            wait_done(nc.gpsimd, L.s.ms, unit)
            nc.gpsimd.tensor_tensor(stat_cols(slot, 14), stat_cols(slot, 13), T.negsq, ALU.pow).then_inc(L.s.rr.sem, 1)

        def dve_scale_rms(L, unit, slot):
            wait_done(nc.vector, L.s.rr, unit)
            nc.vector.tensor_scalar(xo[:, slot], xn[:, slot], stat_cols(slot, 14), None, ALU.mult).then_inc(L.s.xo.sem, 1)

        def pe_transpose_x(L, unit, slot):
            wait_done(nc.tensor, L.s.xo if L.rms else L.s.xn, unit)
            wait_freed(nc.tensor, L.s.xe, unit, 1)
            if L.v_ahead is not None:
                nc.tensor.wait_ge(L.s.vbd.sem, L.s.vbd.base + least(unit + 1 + L.v_ahead, PAIRS))
            if L.router:
                wait_freed(nc.tensor, L.s.lg, unit, 1)
            src = xo if L.rms else xn
            for kc in range(KC):
                mm = nc.tensor.transpose(ps[:, 5, kc * P:(kc + 1) * P], src[:, slot, kc * P:(kc + 1) * P], T.ident)
            mm.then_inc(L.s.xtr.sem, 1)

        def act_copy_xt(L, unit, slot):
            wait_done(nc.scalar, L.s.xtr, unit)
            if L.router:
                wait_freed(nc.scalar, L.s.xt_stored, unit, 2)
                wait_freed(nc.scalar, L.s.routed, unit, 2)
            for kc in range(KC):
                scale = L.xt_scale[:, kc:kc + 1] if L.xt_scale is not None else 1.0
                dst = xe[:, slot, kc, :] if L.router else XT[:, kc, bass.ds(unit * P, P)]
                a = nc.scalar.activation(dst, ps[:, 5, kc * P:(kc + 1) * P], ACT.Copy, scale=scale)
            a.then_inc(L.s.xe.sem, 1)

        def pool_store_xt(L, unit, slot, pair):
            wait_done(nc.gpsimd, L.s.xe, unit)
            high = x_parts[:, 0, :, bass.ds(pair * P, P)]
            nc.gpsimd.tensor_copy(high, xe[:, slot]).then_inc(L.s.x_high.sem, 1)
            wait_done(nc.gpsimd, L.s.x_high, unit)
            nc.gpsimd.tensor_tensor(x_parts[:, 1, :, bass.ds(pair * P, P)], xe[:, slot], high.bitcast(F32),
                                    ALU.subtract).then_inc(L.s.xt_stored.sem, 1)

        def wait_sublayer(eng, L):
            eng.wait_ge(L.s.x_stored.sem, L.s.x_stored.base + PAIRS)
            if L.router:
                wait_done(eng, L.s.lg, PAIRS - 1)
            if L.transposes:
                wait_done(eng, L.s.xt_stored if L.router else L.s.xe, PAIRS - 1)
            elif L.rms:
                wait_done(eng, L.s.xo, PAIRS - 1)


        lin = named(bias_x=True, norm=True, rms=1e-5, transposes=False, router=False, xt_scale=None, twice=False,
                              s=sems("lin", POST + " ready xts q_psum kv_psum qb kb vb low ex qk kvz kvz_masked att "
                                     "den rden an atr anT o xb vones"))
        qk = wk.kbd[:, 0:1024].rearrange("p (b n) -> p b n", b=2)
        qk_exp = wk.pT.rearrange("p (b n) -> p b n", b=2)
        v_one = wk.sd[:, 0:544].rearrange("p (b h n) -> p b h n", b=2, h=2)
        kvz = wk.sd[:, 544:1632].rearrange("p (b q n) -> p b q n", b=2, q=4)
        an = wk.qT.rearrange("p (b n) -> p b n", b=2)
        lin_rec = scores_inv

        def lin_pool():
            s = lin.s
            pool = nc.gpsimd
            pool.memset(v_one[:, :, :, 128:136], 1.0).then_inc(s.vones.sem, 1)
            cross_keys_pool()
            pool.wait_ge(ld.xt0.sem, ld.xt0.base + 16)
            pool.wait_ge(ld.x0.sem, ld.x0.base + 16)
            pool.wait_ge(ld.small.sem, ld.small.base + 16)
            pool.wait_ge(ld.tables.sem, ld.tables.base + 16)

            def load(i, k):
                u = 2 * i + k
                if isinstance(u, int) and u == FIRST:
                    pool.wait_ge(ld.xt.sem, ld.xt.base + 16)
                    pool.wait_ge(ld.x.sem, ld.x.base + 16)
                wait_freed(pool, s.kv_psum, u, 2)
                pool.tensor_copy(xts[:, k], XT[:, :, bass.ds(u * P, P)]).then_inc(s.xts.sem, 1)
                pool.tensor_tensor(X[:, u, :], X[:, u, :], SM.l0_ob, ALU.add).then_inc(s.xb.sem, 1)

            pipelined(pool, PAIRS // 2, 2, [
                (load, 0),
                (lambda i, k: pool_rms(lin, 2 * i + k, k), 5),
                (lambda i, k: pool_rstd(lin, 2 * i + k, k), 4),
                (lambda i, k: pool_store_x(lin, 2 * i + k, k, 2 * i + k), 4)])

        def lin_pe():
            s = lin.s
            pe = nc.tensor
            pe.wait_ge(ld.early0.sem, ld.early0.base + 16)
            pe.wait_ge(ld.tables.sem, ld.tables.base + 16)

            def project(i, k):
                u = 2 * i + k
                wait_done(pe, s.xts, u)
                wait_freed(pe, s.qb, u, 2)
                for m in range(2):
                    for kc in range(KC):
                        mm = pe.matmul(ps[:, 2 + k, m * P:(m + 1) * P], early.l0_q[:, kc * D + m * P:kc * D + (m + 1) * P],
                                       xts[:, k, kc], start=kc == 0, stop=kc == 1)
                mm.then_inc(s.q_psum.sem, 1)
                wait_freed(pe, s.kb, u, 2)
                wait_freed(pe, s.vb, u, 2)
                for kc in range(KC):
                    mm = pe.matmul(ps[:, k, :], xts[:, k, kc], early.l0_kv[:, kc * 512:(kc + 1) * 512],
                                   start=kc == 0, stop=kc == 1)
                mm.then_inc(s.kv_psum.sem, 1)

            def sums(i, k):
                u = 2 * i + k
                wait_done(pe, s.qk, u)
                wait_done(pe, s.vb, u)
                pe.wait_ge(s.vones.sem, s.vones.base + 1)
                wait_freed(pe, s.kvz_masked, u, 1)
                for b in range(2):
                    for h in range(2):
                        r = slice(64 * b, 64 * b + 64)
                        mm = pe.matmul(ps[:, 4 + b, h * 136:(h + 1) * 136], qk[r, k, 256 + h * P:256 + (h + 1) * P],
                                       v_one[r, k, h, :], start=True, stop=True)
                mm.then_inc(s.kvz.sem, 1)

            def attend(i, k):
                u = 2 * i + k
                wait_done(pe, s.kvz_masked, u)
                wait_freed(pe, s.an, u, 1)
                for b in range(2):
                    for h in range(2):
                        mm = pe.matmul(ps[64 * b:64 * b + 64, 6, h * 136:(h + 1) * 136],
                                       qk[:, k, h * P + 64 * b:h * P + 64 * b + 64], kvz[:, k, 2 * b + h, :],
                                       start=True, stop=True)
                mm.then_inc(s.att.sem, 1)

            def turn(i, k):
                u = 2 * i + k
                wait_done(pe, s.an, u)
                wait_freed(pe, s.y, u, 1)
                for h in range(2):
                    mm = pe.transpose(ps[:, 7, 256 + h * P:256 + (h + 1) * P], an[:, k, h * P:(h + 1) * P], T.ident)
                mm.then_inc(s.atr.sem, 1)

            def project_out(i, k):
                u = 2 * i + k
                wait_done(pe, s.anT, u)
                wait_freed(pe, s.y, u, 1)
                for h in range(2):
                    mm = pe.matmul(ps[:, 7, 0:D], avT[:, k, h], early.l0_o[:, h * D:(h + 1) * D], start=h == 0, stop=h == 1)
                mm.then_inc(s.o.sem, 1)

            pipelined(pe, PAIRS // 2, 2, [(attend, 2), (project, 0), (sums, 1), (project_out, 3), (turn, 2)])

        def lin_act():
            s = lin.s
            act = nc.scalar
            act.wait_ge(ld.small.sem, ld.small.base + 16)
            act.wait_ge(ld.tables.sem, ld.tables.base + 16)
            act.activation(ident_bf[:, :], T.ident, ACT.Copy).then_inc(setup.ident.sem, 1)

            def bias_q(i, k):
                u = 2 * i + k
                wait_done(act, s.q_psum, u)
                wait_freed(act, s.att, u, 2)
                for m in range(2):
                    a = act.activation(qk[:, k, m * P:(m + 1) * P], ps[:, 2 + k, m * P:(m + 1) * P], ACT.Identity,
                                       bias=SM.l0_qb[:, m:m + 1])
                a.then_inc(s.qb.sem, 1)

            def exponent(i, k):
                u = 2 * i + k
                wait_done(act, s.low, u)
                act.activation(qk_exp[:, k], qk_exp[:, k], ACT.Exp).then_inc(s.ex.sem, 1)

            def copy_att(i, k):
                u = 2 * i + k
                wait_done(act, s.atr, u)
                wait_freed(act, s.o, u, 2)
                act.activation(avT[:, k], ps[:, 7, 256:512].rearrange("p (a t) -> p a t", a=2), ACT.Copy).then_inc(s.anT.sem, 1)

            pipelined(act, PAIRS // 2, 2, [(lambda i, k: act_square(lin, 2 * i + k, k), 4), (bias_q, 0), (exponent, 0),
                                            (copy_att, 2)])

        def lin_dve():
            s = lin.s
            dve = nc.vector
            dve.wait_ge(ld.small.sem, ld.small.base + 16)
            dve.wait_ge(ld.tables.sem, ld.tables.base + 16)

            def bias_kv(i, k):
                u = 2 * i + k
                wait_done(dve, s.kv_psum, u)
                wait_freed(dve, s.kvz, u, 2)
                dve.tensor_tensor(qk[:, k, 256:512], ps[:, k, 0:256], SM.l0_kvb[:, 0:256], ALU.add).then_inc(s.kb.sem, 1)
                dve.tensor_tensor(v_one[:, k, :, 0:P], ps[:, k, 256:512].rearrange("p (h n) -> p h n", h=2),
                                  SM.l0_kvb[:, 256:512].rearrange("p (h n) -> p h n", h=2), ALU.add).then_inc(s.vb.sem, 1)

            def low(i, k):
                u = 2 * i + k
                wait_done(dve, s.qb, u)
                wait_done(dve, s.kb, u)
                wait_freed(dve, s.qk, u, 2)
                dve.tensor_scalar(qk_exp[:, k], qk[:, k], 0.0, None, ALU.min).then_inc(s.low.sem, 1)

            def elu(i, k):
                u = 2 * i + k
                wait_done(dve, s.ex, u)
                dve.scalar_tensor_tensor(out=qk[:, k], in0=qk[:, k], scalar=0.0, in1=qk_exp[:, k], op0=ALU.max,
                                         op1=ALU.add).then_inc(s.qk.sem, 1)

            def keep_heads(i, k):
                u = 2 * i + k
                wait_done(dve, s.kvz, u)
                wait_freed(dve, s.att, u, 2)
                mask = T.kvz_mask[:, None, :].broadcast_to([P, 2, 136])
                for b in range(2):
                    ins = dve.tensor_tensor(kvz[:, k, 2 * b:2 * b + 2, :], ps[:, 4 + b, 0:272].rearrange("p (h n) -> p h n", h=2),
                                            mask, ALU.mult)
                ins.then_inc(s.kvz_masked.sem, 1)

            def divide(i, k):
                u = 2 * i + k
                wait_done(dve, s.att, u)
                both = ps[:, 6, 0:272].rearrange("p (h n) -> p h n", h=2)
                den = scores_sum[:, k, :]
                dve.tensor_scalar(den.rearrange("p (h n) -> p h n", h=2), both[:, :, 128:136], 1e-6, None,
                                  ALU.add).then_inc(s.den.sem, 1)
                wait_done(dve, s.den, u)
                dve.reciprocal(lin_rec[:, k, :], den).then_inc(s.rden.sem, 1)
                wait_done(dve, s.rden, u)
                wait_freed(dve, s.atr, u, 2)
                for h in range(2):
                    rec = lin_rec[:, k, 8 * h:8 * h + 8, None].broadcast_to([P, 8, 16])
                    ins = dve.tensor_tensor(an[:, k, h * P:(h + 1) * P].rearrange("p (n e) -> p n e", n=8),
                                            both[:, h, 0:P].rearrange("p (n e) -> p n e", n=8), rec, ALU.mult)
                ins.then_inc(s.an.sem, 1)

            def post1(i, k):
                u = 2 * i + k
                dve_add_residual(lin, i, k, u, u, ps[:, 7, 0:D], s.o)
                dve_norm_stats(lin, u, k)

            def post3(i, k):
                u = 2 * i + k
                wait_freed(dve, lin.s.xo, u, 1)
                dve_mean_square(lin, u, k)

            def post4(i, k):
                u = 2 * i + k
                wait_done(dve, s.rr, u)
                dve.tensor_scalar(XT[:, :, bass.ds(u * P, P)], xn[:, k].rearrange("p (a c) -> p a c", a=2),
                                  stat_cols(k, 14), None, ALU.mult).then_inc(s.xo.sem, 1)

            pipelined(dve, PAIRS // 2, 2, [
                (post4, 5), (divide, 2), (bias_kv, 0), (low, 0), (post3, 4), (keep_heads, 1), (post1, 3), (elu, 0),
                (lambda i, k: dve_norm(lin, 2 * i + k, k), 3)])

        SOFT = ("rope qk_t xts xq kst qk_psum v_psum q k kbd vbd scored maxed subbed exped summed inv normed pt0 pt1 ptc0 ptc1 "
                "av avT avT1 o xb routed lg zero xw amax gam inv_gam q1 q2 part down own_y x_high")

        UNIT_STEPS = "scored maxed subbed exped summed inv normed pt0 pt1 ptc0 ptc1 av avT".split()
        soft_sems = signals_of("soft", SOFT + " " + POST)
        counted = {n: 0 for n in (SOFT + " " + POST).split()}

        def soft(kind, drop, **k):
            signals = {}
            for n in counted:
                if n in drop.split():
                    continue
                signals[n] = Signal(soft_sems[n].sem, counted[n])
                times = k.get("upp", 1) if n in UNIT_STEPS else 1
                times *= {"rope": 3, "av": 2 if kind == "latent" else 1}.get(n, 1)
                counted[n] += 1 if n == "zero" else PAIRS * times
            if kind == "self0":
                signals["y"] = Signal(soft_sems["own_y"].sem)
            project = 1 if kind == "cross" else 0
            n = project + (1 if kind == "latent" else 2)
            turn_x = n + 5
            lags = named(project=project, scores=n, values_in=n + 1, turn=n + 2, out=n + 3, turn_x=turn_x, route=turn_x + 1)
            return named(**{**dict(lags=lags, kind=kind, upp=1, bias_x=False, norm=True, rms=None, transposes=True, router=False,
                                   xt_scale=None, v_ahead=3, masked=False, twice=False, s=named(**signals)), **k})

        QUANT = "xw amax gam inv_gam q1 q2 part down own_y"

        def only(names):
            return " ".join(n for n in counted if n not in names.split())

        cross = soft("cross", QUANT + " xt_stored x_high xts qk_psum v_psum xb avT1 routed lg", scale=0.25, rms=1e-5, xt_scale=SM.ln1, masked=True, v_ahead=None)
        causal_self = soft("self0", QUANT + " y rope qk_t xq kst xb avT1 stats aggr eps rstd xn", scale=0.25, norm=False, rms=1e-5,
                           xt_scale=SM.ln2, router=True, masked=True, twice=True)
        grouped = soft("self1", QUANT + " xt_stored x_high rope qk_t xq kst avT1 ss ms rr xo routed lg", scale=8.0 ** -0.5, bias_x=True, upp=2, v_ahead=2)
        latent = soft("latent", "x_high rope xq xts kbd qk_psum v_psum xb ss ms rr xo routed lg xtr xe xt_stored " + QUANT, scale=1.0,
                      v_ahead=None, transposes=False)
        ffn = soft("ffn", only("ss ms rr xw amax gam inv_gam q1 q2 xo xtr xe scored exped pt0 pt1 ptc0 ptc1 part down o y stats aggr "
                               "eps rstd xn x_stored"), transposes=False)

        qry = named(**signals_of("qry", "q mult add t out"), high=Signal(lin.s.ex.sem, PAIRS), low=Signal(lin.s.qk.sem, PAIRS),
                    sent=[Signal(ld.x0.sem, 16), Signal(ld.xt0.sem, 16)],
                    back=[Signal(ld.expert0.sem, 16 * E // 2), Signal(ld.expert1.sem, 16 * E // 2)])

        xq = wk.xts.rearrange("p (b n) -> p b n", b=2)
        kst = kT[:, :, 1, :]
        k_rope = mid[:, 0:1024].rearrange("p (t n) -> p t n", t=PAIRS)
        rope_w = mid[:, 1024:1536].rearrange("p (b n) -> p b n", b=2)
        k_tmp = mid[:, 1536:4608].rearrange("p (b t n) -> p b t n", b=3, t=PAIRS)
        qts = wk.kbd.rearrange("p (b h t) -> p b h t", b=2, h=8)
        fold_o = big[:, 4096:6144].rearrange("p (n c) -> p n c", n=8)
        c_parts = big_r[:, 10240:12288].rearrange("p (a n t) -> p a n t", a=2, n=8)
        o_parts = mid_r[:, 6144:10240].rearrange("p (a n c) -> p a n c", a=2, n=8)
        c_low, o_split = Signal(lin.s.kvz.sem, PAIRS), Signal(lin.s.den.sem, PAIRS)
        logits = sbuf("logits", [P, PAIRS, E])

        def at(L, i, k):
            return 2 * L.upp * i + k, k % 2, 2 * i + k // L.upp, k // L.upp, k % L.upp

        def run(eng, L, stages):
            pipelined(eng, PAIRS // 2, 2 * L.upp, stages, margin=2 * L.upp)

        def soft_pe(L):
            s, pe = L.s, nc.tensor

            def project(i, k):
                u, us, p, slot, a = at(L, i, k)
                if a:
                    return
                if L.kind in ("cross", "latent"):
                    if L.kind == "cross":
                        wait_done(pe, s.xq, p)
                        wait_freed(pe, s.q, p, 1)
                    wait_done(pe, s.kst, p)
                    if L.kind == "latent" and isinstance(p, int) and p == SUMS_AT + 2:
                        pe.wait_ge(tern.mean.sem, 1)
                    wait_freed(pe, s.k, p, 1)
                    if L.kind == "cross":
                        for m in range(2):
                            pe.transpose(ps[:, 6, m * P:(m + 1) * P], xq[:, slot, m * P:(m + 1) * P], T.ident)
                    pe.transpose(ps[:, 6, 256:384] if L.kind == "cross" else ps[:, 5, 256:384], kst[:, slot], T.ident).then_inc(s.qk_t.sem, 1)
                    return
                wait_freed(pe, s.k, p, 1)
                wq, wkk, nk = (early.f_q, early.f_k, 2) if L.kind == "self0" else (l1a_w.a_q, l1a_w.a_k, 1)
                for w, n, at0 in ((wq, 2, 0), (wkk, nk, 256)):
                    for m in range(n):
                        for kc in range(KC):
                            mm = pe.matmul(ps[:, 6, at0 + m * P:at0 + (m + 1) * P], w[:, (kc * n + m) * P:(kc * n + m + 1) * P],
                                           XT[:, kc, bass.ds(p * P, P)], start=kc == 0, stop=kc == 1)
                mm.then_inc(s.qk_psum.sem, 1)

            def project_values(i, k):
                u, us, p, slot, a = at(L, i, k)
                if a:
                    return
                wait_done(pe, s.xts, p)
                wv, nv = (early.f_v, D) if L.kind == "self0" else (l1a_w.a_v, 64)
                wait_freed(pe, s.vbd, p, 1)
                wait_freed(pe, s.xe, p, L.v_ahead + 1)
                if L.router:
                    wait_freed(pe, s.lg, p, L.v_ahead + 2)
                for kc in range(KC):
                    mm = pe.matmul(ps[:, 5, 256:256 + nv], xts[:, slot, kc], wv[:, kc * nv:(kc + 1) * nv],
                                   start=kc == 0, stop=kc == 1)
                mm.then_inc(s.v_psum.sem, 1)

            def scores(i, k):
                u, us, p, slot, a_unit = at(L, i, k)
                if L.kind == "latent":
                    wait_done(pe, qry.back[slot], i, 16)
                else:
                    wait_done(pe, s.q, p)
                wait_done(pe, s.k if L.kind == "latent" else s.kbd, p)
                wait_freed(pe, s.subbed, u, 1)
                if not L.masked:
                    pe.matmul(ps[:, 0, 0:2], ident_bf[:, :], ident_bf[:, 0:2], start=True, stop=True)
                if L.masked:
                    for c in range(2):
                        pe.matmul(ps[:, c, :], ident_bf[:, :], causal[:, :], start=True, stop=True)
                for b in range(2):
                    rb = slice(64 * b, 64 * b + 64)
                    for c in range(2):
                        rc = slice(64 * c, 64 * c + 64)
                        if L.kind == "self1":
                            mm = pe.matmul(ps[rb, c, :], qT[rc, slot, a_unit, rb], kbd[rc, slot, b * 512:(b + 1) * 512],
                                           start=True, stop=True)
                        elif L.kind == "latent":
                            for h in range(8):
                                mm = pe.matmul(ps[rb, c, h * 64:(h + 1) * 64], qts[rc, slot, h, rb], kT[rc, slot, 0, rb],
                                               start=True, stop=True)
                        else:
                            for a in range(2):
                                n = b if L.kind == "cross" else 2 * a + b
                                mm = pe.matmul(ps[rb, c, a * 256:(a + 1) * 256], qT[rc, slot, a, rb],
                                               kbd[rc, slot, n * 256:(n + 1) * 256], start=False, stop=True,
                                               skip_group_check=True)
                mm.then_inc(s.scored.sem, 1)

            def turn(i, k):
                u, us, p, slot, a = at(L, i, k)
                wait_done(pe, s.normed, u)
                for half, copied, full in ((0, s.ptc0, s.pt0), (1, s.ptc1, s.pt1)):
                    wait_freed(pe, copied, u, 1)
                    for n in range(4):
                        mm = pe.transpose(ps[:, 2 + half, n * P:(n + 1) * P], sd[:, us, (4 * half + n) * P:(4 * half + n + 1) * P],
                                          T.ident)
                    mm.then_inc(full.sem, 1)

            def values(i, k):
                u, us, p, slot, a_unit = at(L, i, k)
                wait_done(pe, s.ptc0, u)
                wait_done(pe, s.vbd, p)
                if L.kind == "latent":
                    if not (isinstance(u, int) and u < 1):
                        pe.wait_ge(c_low.sem, c_low.base + 2 * u - 1)
                else:
                    wait_freed(pe, s.avT, u, 1)
                chunks = pT[:, :, :].rearrange("p (c a g) t -> p c a g t", c=2, a=2)
                bank = ps[:, 4, 0:256].rearrange("p (a b t) -> p a b t", a=2, b=2)
                for c in range(2):
                    if c == 1:
                        wait_done(pe, s.ptc1, u)
                    if L.kind == "latent":
                        if c == 1:
                            wait_freed(pe, c_low, u, 1, 2)
                        wide = ps[:, 4 if c == 0 else 6, :].rearrange("p (n b t) -> p n b t", n=4, b=2)
                        for b in range(2):
                            mm = pe.matmul(wide[:, :, b, :], vbd[:, slot, b * P:(b + 1) * P], pT[:, 4 * c:4 * c + 4, 64 * b:64 * b + 64],
                                           start=True, stop=True)
                        mm.then_inc(s.av.sem, 1)
                        continue
                    for b in range(2):
                        rb = slice(64 * b, 64 * b + 64)
                        if L.kind == "self1":
                            for g in range(4):
                                mm = pe.matmul(bank[32 * g:32 * g + 32, c, b, :], vbd[:, slot, b * P + 32 * g:b * P + 32 * g + 32],
                                               pT[:, 4 * c + g, rb], start=True, stop=True)
                            continue
                        for g in range(2):
                            rows = slice(32 * (2 * c + g), 32 * (2 * c + g) + 32)
                            if L.kind == "cross":
                                mm = pe.matmul(bank[rows, :, b, :], vbd[:, slot, b * 64 + 32 * g:b * 64 + 32 * g + 32],
                                               chunks[:, c, :, g, rb], start=True, stop=True)
                            else:
                                for a in range(2):
                                    n = 4 * c + 2 * a + g
                                    mm = pe.matmul(bank[rows, a, b, :], vbd[:, slot, b * 256 + 32 * n:b * 256 + 32 * n + 32],
                                                   pT[:, n, rb], start=True, stop=True)
                if L.kind != "latent":
                    mm.then_inc(s.av.sem, 1)

            def project_out(i, k):
                u, us, p, slot, a_unit = at(L, i, k)
                if a_unit != L.upp - 1:
                    return
                if L.kind == "latent":
                    wait_done(pe, c_low, u, 2)
                    if isinstance(u, int) and u == 0:
                        pe.wait_ge(o_split.sem, o_split.base + 2)
                else:
                    wait_done(pe, s.avT, u)
                wait_freed(pe, s.y, p, 1)
                pairs = {"cross": [(avT[:, us, a], early.x_o, a) for a in range(2)],
                         "self0": [(avT[:, us, a], early.f_o, a) for a in range(2)],
                         "self1": [(avT[:, a, c], l1a_w.a_o, 2 * a + c) for a in range(2) for c in range(2)],
                         "latent": [(c_parts[:, a, n], None, (b, n)) for n in range(8) for a, b in PRODUCTS]}[L.kind]
                for n, (lhs, w, at0) in enumerate(pairs):
                    rhs = o_parts[:, at0[0], at0[1]] if w is None else w[:, at0 * D:(at0 + 1) * D]
                    mm = pe.matmul(ps[:, 7, 0:D], lhs, rhs, start=n == 0, stop=n == len(pairs) - 1)
                mm.then_inc(s.o.sem, 1)

            def turn_x(i, k):
                u, us, p, slot, a = at(L, i, k)
                if a == L.upp - 1:
                    pe_transpose_x(L, p, slot)

            def route(i, k):
                u, us, p, slot, a = at(L, i, k)
                wait_done(pe, s.xe, p)
                pe.wait_ge(s.vbd.sem, s.vbd.base + least(p + 2 + L.v_ahead, PAIRS))
                for kc in range(KC):
                    mm = pe.matmul(ps[:, 5, 0:E], xe[:, slot, kc], early.f_r[:, kc * E:(kc + 1) * E], start=kc == 0, stop=kc == 1)
                mm.then_inc(s.routed.sem, 1)

            g = L.lags
            stages = [(turn, g.turn), (scores, g.scores)] + ([(route, g.route)] if L.router else []) + [(project_out, g.out)]
            stages += ([(turn_x, g.turn_x)] if L.transposes else []) + [(project, g.project)]
            run(pe, L, stages + ([(project_values, g.values_in)] if L.kind in ("self0", "self1") else []) + [(values, g.turn)]
                + ([(ternary_pe, 0)] if L.kind == "latent" else []))

        def soft_act(L):
            s, act = L.s, nc.scalar

            def copy_xt(i, k):
                u, us, p, slot, a = at(L, i, k)
                if a == L.upp - 1:
                    act_copy_xt(L, p, slot)

            def copy_qkv(i, k):
                u, us, p, slot, a = at(L, i, k)
                if a:
                    return
                wait_done(act, s.qk_t if L.kind in ("cross", "latent") else s.qk_psum, p)
                wait_freed(act, s.scored, p, 2, L.upp)
                if L.kind == "cross":
                    act.activation(qT[:, slot], ps[:, 6, 0:256].rearrange("p (a t) -> p a t", a=2), ACT.Copy).then_inc(s.q.sem, 1)
                    act.activation(kT[:, slot, 0], ps[:, 6, 256:384], ACT.Copy).then_inc(s.k.sem, 1)
                elif L.kind == "latent":
                    act.activation(kT[:, slot, 0], ps[:, 5, 256:384], ACT.Copy).then_inc(s.k.sem, 1)
                elif L.kind == "self0":
                    act.activation(qT[:, slot], ps[:, 6, 0:256].rearrange("p (a t) -> p a t", a=2), ACT.Copy).then_inc(s.q.sem, 1)
                    wait_freed(act, s.kbd, p, 2)
                    act.activation(kT[:, slot], ps[:, 6, 256:512].rearrange("p (a t) -> p a t", a=2), ACT.Copy).then_inc(s.k.sem, 1)
                else:
                    for m in range(2):
                        ins = act.activation(qT[:, slot, m], ps[:, 6, m * P:(m + 1) * P], ACT.Identity, bias=SM.l1_qb[:, m:m + 1])
                    ins.then_inc(s.q.sem, 1)
                    wait_freed(act, s.kbd, p, 2)
                    act.activation(kT[:, slot, 0], ps[:, 6, 256:384], ACT.Identity, bias=SM.l1_kb).then_inc(s.k.sem, 1)

            def spread_v(i, k):
                u, us, p, slot, a = at(L, i, k)
                if L.kind == "self1":
                    return
                wait_freed(act, s.av, p, 2, 2 if L.kind == "latent" else 1)
                if L.kind == "self0":
                    wait_done(act, s.v_psum, p)
                act.wait_ge(s.zero.sem, s.zero.base + 1)
                for b in range(2):
                    rb = slice(64 * b, 64 * b + 64)
                    for x in range(2):
                        rx = slice(64 * x, 64 * x + 64)
                        if L.kind == "cross":
                            dst = vbd[rx, slot, 64 * b:64 * b + 64].rearrange("p (g x d) -> p g x d", g=2, x=2)[:, :, x, :]
                            src = ctx_tok[rb, p, :].rearrange("p (g x d) -> p g x d", g=2, x=2)[:, :, x, :]
                        elif L.kind == "latent":
                            dst = vbd[rx, slot, b * P + 64 * x:b * P + 64 * x + 64]
                            src = ctx_tok[rb, p, :]
                        else:
                            dst = vbd[rx, slot, 256 * b:256 * b + 256].rearrange("p (n x d) -> p n x d", n=8, x=2)
                            dst = dst.rearrange("p (c a g) x d -> p c a g x d", c=2, a=2)
                            src = ps[rb, 5, 256:512].rearrange("p (a c g x d) -> p a c g x d", a=2, c=2, g=2, x=2)
                            for c in range(2):
                                ins = act.activation(dst[:, c, :, :, x, :], src[:, :, c, :, x, :], ACT.Copy)
                            continue
                        ins = act.activation(dst, src, ACT.Copy)
                ins.then_inc(s.vbd.sem, 1)

            def exponent(i, k):
                u, us, p, slot, a = at(L, i, k)
                wait_done(act, s.subbed, u)
                act.activation(sd[:, us], sd[:, us], ACT.Exp, scale=L.scale).then_inc(s.exped.sem, 1)

            def square(i, k):
                u, us, p, slot, a = at(L, i, k)
                act_square(L, p, slot)

            def store_x(i, k):
                u, us, p, slot, a = at(L, i, k)
                wait_done(act, s.xn, p)
                act.activation(X[:, p, :], xn[:, slot], ACT.Copy).then_inc(s.x_stored.sem, 1)

            def copy_pt(i, k):
                u, us, p, slot, a = at(L, i, k)
                wait_done(act, s.pt0, u)
                wait_freed(act, s.av, u, 1, 2 if L.kind == "latent" else 1)
                act.activation(pT[:, 0:4], ps[:, 2, :].rearrange("p (n t) -> p n t", n=4), ACT.Copy).then_inc(s.ptc0.sem, 1)
                if L.kind in ("self1", "latent"):
                    wait_done(act, s.pt1, u)
                    act.activation(pT[:, 4:8], ps[:, 3, :].rearrange("p (n t) -> p n t", n=4), ACT.Copy).then_inc(s.ptc1.sem, 1)

            def copy_av(i, k):
                u, us, p, slot, a = at(L, i, k)
                if L.kind == "latent":
                    wait_freed(act, s.o, p, 1)
                    act.wait_ge(s.av.sem, s.av.base + 2 * u + 1)
                    act.activation(c_parts[:, 0, 0:4], ps[:, 4, :].rearrange("p (n t) -> p n t", n=4), ACT.Copy).then_inc(s.avT.sem, 1)
                    wait_done(act, s.av, u, 2)
                    act.activation(c_parts[:, 0, 4:8], ps[:, 6, :].rearrange("p (n t) -> p n t", n=4), ACT.Copy).then_inc(s.avT1.sem, 1)
                    return
                wait_done(act, s.av, u)
                if L.upp == 2:
                    wait_freed(act, s.o, p, 1)
                else:
                    wait_freed(act, s.o, p, 2)
                act.activation(avT[:, us], ps[:, 4, 0:256].rearrange("p (a t) -> p a t", a=2), ACT.Copy).then_inc(s.avT.sem, 1)

            def copy_logits(i, k):
                u, us, p, slot, a = at(L, i, k)
                wait_done(act, s.routed, p)
                act.activation(logits[:, p, :], ps[:, 5, 0:E], ACT.Copy).then_inc(s.lg.sem, 1)

            g = L.lags
            stages = [(copy_pt, g.turn)] + ([(copy_logits, g.route)] if L.router else []) + ([(square, g.out + 1)] if L.rms else [])
            stages += [(store_x, g.out + 1)] if L.kind == "cross" else []
            stages += [(copy_xt, g.turn_x)] if L.transposes else []
            stages += [(exponent, g.scores), (copy_qkv, g.project)]
            stages += [(copy_av, g.turn), (spread_v, g.values_in)]
            if L.kind == "latent":
                act.activation(o_parts[:, 0], fold_o, ACT.Copy).then_inc(o_split.sem, 1)
            run(act, L, stages)

        def soft_dve(L):
            s, dve = L.s, nc.vector

            def bank(us):
                return ps[:, 0:2, :].rearrange("p c (n t) -> p (c n) t", t=64)

            def top(i, k):
                u, us, p, slot, a = at(L, i, k)
                wait_done(dve, s.scored, u)
                dve.tensor_reduce(scores_max[:, us], bank(us), AX.X, ALU.max).then_inc(s.maxed.sem, 1)

            def below_top(i, k):
                u, us, p, slot, a = at(L, i, k)
                wait_done(dve, s.maxed, u)
                wait_freed(dve, s.pt1, u, 2)
                dve.tensor_tensor(sd[:, us].rearrange("p (n t) -> p n t", t=64), bank(us),
                                  scores_max[:, us, :, None].broadcast_to([P, 16, 64]), ALU.subtract).then_inc(s.subbed.sem, 1)

            def inverse_sum(i, k):
                u, us, p, slot, a = at(L, i, k)
                wait_done(dve, s.exped, u)
                dve.tensor_reduce(scores_sum[:, us], sd[:, us].rearrange("p (n t) -> p n t", t=64), AX.X,
                                  ALU.add).then_inc(s.summed.sem, 1)
                wait_done(dve, s.summed, u)
                wait_freed(dve, s.normed, u, 2)
                dve.reciprocal(scores_inv[:, us], scores_sum[:, us]).then_inc(s.inv.sem, 1)

            def copy_pt(i, k):
                u, us, p, slot, a = at(L, i, k)
                wait_done(dve, s.pt1, u)
                wait_freed(dve, s.av, u, 1, 2 if L.kind == "latent" else 1)
                dve.tensor_copy(pT[:, 4:8], ps[:, 3, :].rearrange("p (n t) -> p n t", n=4)).then_inc(s.ptc1.sem, 1)

            def spread_v(i, k):
                u, us, p, slot, a = at(L, i, k)
                if a:
                    return
                wait_done(dve, s.v_psum, p)
                dve.wait_ge(s.zero.sem, s.zero.base + 1)
                wait_freed(dve, s.av, p, 2, 2)
                for b in range(2):
                    rb = slice(64 * b, 64 * b + 64)
                    for x in range(2):
                        rx = slice(64 * x, 64 * x + 64)
                        dst = vbd[rx, slot, b * P:(b + 1) * P].rearrange("p (g n) -> p g n", g=4)[:, :, 8 * x:8 * x + 8]
                        src = ps[rb, 5, 256:320].rearrange("p (g x d) -> p g x d", g=4, x=2)[:, :, x, :]
                        bias = SM.l1_vb[rb].rearrange("p (g x d) -> p g x d", g=4, x=2)[:, :, x, :]
                        ins = dve.tensor_tensor(dst, src, bias, ALU.add)
                ins.then_inc(s.vbd.sem, 1)

            def post(step):
                def stage(i, k):
                    u, us, p, slot, a = at(L, i, k)
                    if a == L.upp - 1:
                        step(p, slot)
                return stage

            def add(p, slot):
                dve_add_residual(L, None, slot, p, p, ps[:, 7, 0:D], s.o)
                if L.norm:
                    dve_norm_stats(L, p, slot)

            def low_part(i, k):
                u, us, p, slot, a = at(L, i, k)
                for half, (copied, bank) in enumerate(((s.avT, 4), (s.avT1, 6))):
                    wait_done(dve, copied, u)
                    dve.tensor_tensor(c_parts[:, 1, 4 * half:4 * half + 4], ps[:, bank, :].rearrange("p (n t) -> p n t", n=4),
                                      c_parts[:, 0, 4 * half:4 * half + 4].bitcast(F32), ALU.subtract).then_inc(c_low.sem, 1)

            g = L.lags
            stages = ([(copy_pt, g.turn)] if L.kind in ("cross", "self0") else []) + ([(post(lambda p, slot: dve_scale_rms(L, p, slot)), g.out + 2)] if L.rms else [])
            if L.rms:
                stages += [(post(lambda p, slot: dve_mean_square(L, p, slot)), g.out + 1)]
            stages += [(top, g.scores), (below_top, g.scores), (post(add), g.out), (inverse_sum, g.scores)]
            if L.norm:
                stages += [(post(lambda p, slot: dve_norm(L, p, slot)), g.out)]
            if L.kind == "self1":
                stages += [(spread_v, g.values_in)]
            if L.kind == "latent":
                stages += [(low_part, g.turn), (ternary_dve, 0)]
                dve.wait_ge(o_split.sem, o_split.base + 1)
                dve.tensor_tensor(o_parts[:, 1], fold_o, o_parts[:, 0].bitcast(F32), ALU.subtract).then_inc(o_split.sem, 1)
            run(dve, L, stages)

        def soft_pool(L):
            s, pool = L.s, nc.gpsimd
            pool.memset(wk.vbd, 0.0).then_inc(s.zero.sem, 1)

            def load(i, k):
                u, us, p, slot, a = at(L, i, k)
                if a:
                    return
                if L.kind in ("cross", "latent"):
                    wait_freed(pool, s.qk_t, p, 2)
                    both = ctx_tok if L.kind == "latent" else k_rope
                    pool.tensor_copy(kst[:, slot].rearrange("p (x d) -> p x d", x=2),
                                     both[:, bass.ds(p, 1), :].broadcast_to([P, 2, 64])).then_inc(s.kst.sem, 1)
                    if L.kind == "latent":
                        return
                    xr, part2 = kbd[:, slot, 512:768], kbd[:, slot, 768:1024]
                    halves_of = lambda t: t.rearrange("p a (n x d) -> p a n x d", x=2, d=8)
                    two = lambda t: t.rearrange("p (a c) -> p a c", a=2)
                    x_of = XT[:, :, bass.ds(p * P, P)]
                    for x in range(2):
                        pool.tensor_tensor(halves_of(two(part2))[:, :, :, x], halves_of(x_of)[:, :, :, 1 - x],
                                           halves_of(two(rope_w[:, 1]))[:, :, :, x], ALU.mult).then_inc(s.rope.sem, 1)
                    pool.tensor_tensor(two(xr), x_of, two(rope_w[:, 0]), ALU.mult).then_inc(s.rope.sem, 1)
                    wait_done(pool, s.rope, p, 3)
                    by_tile = lambda t: t.rearrange("p (g c a d) -> p a c g d", g=4, c=2, a=2)
                    for m in range(2):
                        ins = pool.tensor_tensor(xq[:, slot, m * P:(m + 1) * P].rearrange("p (c g d) -> p c g d", c=2, g=4),
                                                 by_tile(xr)[:, m], by_tile(part2)[:, m], ALU.add)
                    ins.then_inc(s.xq.sem, 1)
                    return
                wait_freed(pool, s.v_psum, p, 2)
                pool.tensor_copy(xts[:, slot], XT[:, :, bass.ds(p * P, P)]).then_inc(s.xts.sem, 1)
                if L.bias_x:
                    pool.tensor_tensor(X[:, p, :], X[:, p, :], SM.l1_ob, ALU.add).then_inc(s.xb.sem, 1)

            def spread_k(i, k):
                u, us, p, slot, a = at(L, i, k)
                if a or L.kind == "latent":
                    return
                wait_done(pool, s.k, p)
                wait_freed(pool, s.scored, p, 2, L.upp)
                heads, mask = (8, T.mask_g8) if L.kind == "self1" else (4, T.mask_g4)
                for m in range(2 if L.kind == "self0" else 1):
                    n = 2 * heads * 64
                    dst = kbd[:, slot, m * n:(m + 1) * n].rearrange("p (b g t) -> p b g t", b=2, g=heads)
                    keys = kT[:, slot, m].rearrange("p (b t) -> p b t", b=2)[:, :, None, :].broadcast_to([P, 2, heads, 64])
                    ins = pool.tensor_tensor(dst, keys, mask[:, None, :, None].broadcast_to([P, 2, heads, 64]), ALU.mult)
                ins.then_inc(s.kbd.sem, 1)

            def divide(i, k):
                u, us, p, slot, a = at(L, i, k)
                wait_done(pool, s.inv, u)
                pr = sd[:, us].rearrange("p (n t) -> p n t", t=64)
                pool.tensor_tensor(pr, pr, scores_inv[:, us, :, None].broadcast_to([P, 16, 64]), ALU.mult).then_inc(s.normed.sem, 1)

            def post(step):
                def stage(i, k):
                    u, us, p, slot, a = at(L, i, k)
                    if a == L.upp - 1:
                        step(p, slot)
                return stage

            g = L.lags
            stages = [(load, g.scores if L.kind in ("self0", "self1") else 0)]
            if L.rms:
                stages += [(post(lambda p, slot: pool_rms(L, p, slot)), g.out + 1)]
            if L.norm:
                stages += [(post(lambda p, slot: pool_rstd(L, p, slot)), g.out)]
            stages += [(divide, g.scores)]
            if L.kind != "cross":
                stages += [(post(lambda p, slot: pool_store_x(L, p, slot, p)), g.out)]
            stages += [(spread_k, g.project)]
            if L.router:
                stages += [(post(lambda p, slot: pool_store_xt(L, p, slot, p)), g.turn_x)]
            run(pool, L, stages)

        def cross_keys_dve():
            s, dve = prep.s, nc.vector
            sq, kw, part2 = k_tmp[:, 0], k_tmp[:, 1], k_tmp[:, 2]
            dve.wait_ge(ld.ctx.sem, ld.ctx.base + 16)
            dve.wait_ge(ld.small.sem, ld.small.base + 16)
            dve.wait_ge(ld.tables.sem, ld.tables.base + 16)
            n = [0]

            def step(ins):
                n[0] += 1
                ins.then_inc(s.dve_keys.sem, 1)
                dve.wait_ge(s.dve_keys.sem, s.dve_keys.base + n[0])

            ss, r = scores_sum[:, 0, :], scores_sum[:, 1, :]
            step(dve.tensor_tensor(sq, ctx_tok[:, :, :], ctx_tok[:, :, :], ALU.mult))
            step(dve.tensor_reduce(ss, sq, AX.X, ALU.add))
            dve.tensor_scalar(ss, ss, 1.0 / DC, 1e-5, ALU.mult, ALU.add).then_inc(s.key_ms.sem, 1)
            dve.wait_ge(s.key_rms.sem, s.key_rms.base + 1)
            step(dve.tensor_tensor(kw, ctx_tok[:, :, :], r[:, :, None].broadcast_to([P, PAIRS, DC]), ALU.mult))
            step(dve.tensor_tensor(kw, kw, SM.x_knw[:, None, :].broadcast_to([P, PAIRS, DC]), ALU.mult))
            v = lambda t: t.rearrange("p t (n x d) -> p (t n) x d", x=2, d=8)
            for x in range(2):
                table = T.sin16[:, None, 8 * x:8 * x + 8].broadcast_to([P, 64, 8])
                step(dve.tensor_tensor(v(part2)[:, :, x], v(kw)[:, :, 1 - x], table, ALU.mult))
            w = lambda t: t.rearrange("p t (n d) -> p (t n) d", d=16)
            step(dve.tensor_tensor(w(sq), w(kw), T.cos16[:, None, :].broadcast_to([P, 64, 16]), ALU.mult))
            dve.tensor_tensor(k_rope, sq, part2, ALU.add).then_inc(s.keys.sem, 1)
            wn = SM.x_qnw.rearrange("p (n d) -> p n d", d=16)
            dve.tensor_tensor(rope_w[:, 0].rearrange("p (n d) -> p n d", d=16), wn, T.cos16[:, None, :].broadcast_to([P, 16, 16]),
                              ALU.mult).then_inc(s.rope_w.sem, 1)
            h = lambda t: t.rearrange("p (n x d) -> p n x d", x=2, d=8)
            for x in range(2):
                dve.tensor_tensor(h(rope_w[:, 1])[:, :, x], h(SM.x_qnw)[:, :, 1 - x],
                                  T.sin16[:, None, 8 * x:8 * x + 8].broadcast_to([P, 16, 8]), ALU.mult).then_inc(s.rope_w.sem, 1)

        def cross_keys_pool():
            nc.gpsimd.wait_ge(prep.s.key_ms.sem, prep.s.key_ms.base + 1)
            nc.gpsimd.tensor_tensor(scores_sum[:, 1, :], scores_sum[:, 0, :], T.negsq.broadcast_to([P, 16]), ALU.pow).then_inc(prep.s.key_rms.sem, 1)

        prep = named(s=sems("prep", "dve_keys key_ms key_rms keys rope_w"))

        moe = sems("moe", "top idx gap ex one p1 p2 idxf hot hot1 hot2 cw cwe gu silu h h_high h_low w_high w_low down acc")
        best = sbuf("best", [P, PAIRS, 8])
        best_at = sbuf("best_at", [P, PAIRS, 8], U32)
        best_f = sbuf("best_f", [P, PAIRS, 8])
        hot = sbuf("hot", [P, 2, PAIRS, E])
        share = sbuf("share", [P, 4, PAIRS])
        cw = sbuf("cw", [P, E, PAIRS])
        cwe = sbuf("cwe", [P, 2, PAIRS])
        raw = [mid[:, (1 - n) * 6144 + 3072:(1 - n) * 6144 + 6144] for n in range(2)]
        w_parts = [mid_r[:, (1 - n) * 6144:(1 - n) * 6144 + 6144].rearrange("p (n w) -> p n w", n=2) for n in range(2)]
        expert = [[part(w_parts[n][:, x], EXPERT) for x in range(2)] for n in range(2)]
        hidden = big_r[:, 0:8192].rearrange("p (b n m t) -> p b n m t", b=2, n=2, m=4)
        PRODUCTS = ((0, 0), (0, 1), (1, 0))
        h_full = wk.kbd[:, 0:1024].rearrange("p (b n) -> p b n", b=2)
        silu = wk.sd.rearrange("p (b n) -> p b n", b=2)[:, :, 0:512]
        CHUNKS, MT = TOK // GT, I // P

        def route_dve():
            dve = nc.vector
            for p in range(PAIRS):
                dve.max(best[:, p], logits[:, p]).then_inc(moe.top.sem, 1)
            for p in range(PAIRS):
                dve.wait_ge(moe.top.sem, p + 1)
                dve.max_index(best_at[:, p], best[:, p], logits[:, p]).then_inc(moe.idx.sem, 1)
            dve.tensor_tensor(share[:, 0], best[:, :, 1], best[:, :, 0], ALU.subtract).then_inc(moe.gap.sem, 1)
            dve.wait_ge(moe.idx.sem, PAIRS)
            dve.tensor_copy(best_f[:, :, :], best_at[:, :, :]).then_inc(moe.idxf.sem, 1)
            dve.wait_ge(moe.ex.sem, 1)
            dve.tensor_scalar(share[:, 1], share[:, 0], 1.0, None, ALU.add).then_inc(moe.one.sem, 1)
            dve.wait_ge(moe.one.sem, 1)
            dve.reciprocal(share[:, 2], share[:, 1]).then_inc(moe.p1.sem, 1)
            dve.wait_ge(moe.p1.sem, 1)
            dve.tensor_tensor(share[:, 3], share[:, 0], share[:, 2], ALU.mult).then_inc(moe.p2.sem, 1)
            dve.wait_ge(moe.idxf.sem, 1)
            dve.wait_ge(moe.p2.sem, 1)
            iota = T.iota8[:, None, :].broadcast_to([P, PAIRS, E])
            for n in range(2):
                dve.tensor_tensor(hot[:, n], iota, best_f[:, :, n:n + 1].broadcast_to([P, PAIRS, E]),
                                  ALU.is_equal).then_inc(moe.hot.sem, 1)
            for n in range(2):
                dve.wait_ge(moe.hot.sem, n + 1)
                dve.tensor_tensor(hot[:, n], hot[:, n], share[:, 2 + n, :, None].broadcast_to([P, PAIRS, E]),
                                  ALU.mult).then_inc(moe.hot1.sem, 1)
            dve.wait_ge(moe.hot1.sem, 2)
            dve.tensor_tensor(cw[:, :, :].rearrange("p e t -> p t e"), hot[:, 0], hot[:, 1], ALU.add).then_inc(moe.cw.sem, 1)

        def route_act():
            nc.scalar.wait_ge(moe.gap.sem, 1)
            nc.scalar.activation(share[:, 0], share[:, 0], ACT.Exp).then_inc(moe.ex.sem, 1)

        def moe_place(i, k):
            return 2 * CHUNKS * i + k, k % 2, 2 * i + k // CHUNKS, k // CHUNKS, k % CHUNKS

        def moe_pe():
            pe = nc.tensor

            def gate_up(i, k):
                u, us, e, slot, c = moe_place(i, k)
                if c == 0:
                    pe.wait_ge(moe.w_low.sem, e + 1)
                for m in range(MT):
                    j = MT * u + m
                    wait_freed(pe, moe.h, j, 2)
                    for n, name in enumerate(("gate", "up")):
                        for y, (a, b) in enumerate(PRODUCTS):
                            w = (expert[slot][a].gate, expert[slot][a].up)[n]
                            for kc in range(KC):
                                mm = pe.matmul(ps[:, 2 * n + m % 2, :], w[:, kc * I + m * P:kc * I + (m + 1) * P],
                                               x_parts[:, b, kc, c * GT:(c + 1) * GT], start=y + kc == 0, stop=y + kc == 3)
                    mm.then_inc(moe.gu.sem, 1)

            def down(i, k):
                u, us, e, slot, c = moe_place(i, k)
                for t in range(4):
                    j = 4 * u + t
                    wait_freed(pe, moe.acc, j, 4)
                    for m in range(MT):
                        if t == 0:
                            pe.wait_ge(moe.h_low.sem, MT * u + m + 1)
                        for y, (a, b) in enumerate(PRODUCTS):
                            mm = pe.matmul(ps[:, 4 + t, 0:D], hidden[:, us, a, m, t * P:(t + 1) * P],
                                           expert[slot][b].down[:, m * D:(m + 1) * D], start=m + y == 0, stop=m + y == MT + 1)
                    mm.then_inc(moe.down.sem, 1)

            pipelined(pe, E // 2, 2 * CHUNKS, [(gate_up, 0), (down, 1)])

        def moe_act():
            act = nc.scalar

            def gate(i, k):
                u, us, e, slot, c = moe_place(i, k)
                for m in range(MT + 1):
                    if m < MT:
                        j = MT * u + m
                        wait_done(act, moe.gu, j)
                        wait_freed(act, moe.h, j, 2)
                        act.activation(silu[:, m % 2], ps[:, m % 2, :], ACT.Silu).then_inc(moe.silu.sem, 1)
                    if m == 0:
                        wait_freed(act, moe.down, u, 2, 4)
                    else:
                        wait_done(act, moe.h, MT * u + m - 1)
                        act.activation(hidden[:, us, 0, m - 1], h_full[:, (m - 1) % 2], ACT.Copy).then_inc(moe.h_high.sem, 1)

            pipelined(act, E // 2, 2 * CHUNKS, [(gate, 0)])

        def moe_dve():
            dve = nc.vector

            def gated(i, k):
                u, us, e, slot, c = moe_place(i, k)
                wait_freed(dve, moe.down, u, 2, 4)
                for m in range(MT + 1):
                    if m < MT:
                        wait_done(dve, moe.silu, MT * u + m)
                        wait_freed(dve, moe.h_low, MT * u + m, 2)
                        dve.tensor_tensor(h_full[:, m % 2], silu[:, m % 2], ps[:, 2 + m % 2, :], ALU.mult).then_inc(moe.h.sem, 1)
                    if m:
                        wait_done(dve, moe.h_high, MT * u + m - 1)
                        dve.tensor_tensor(hidden[:, us, 1, m - 1], h_full[:, (m - 1) % 2], hidden[:, us, 0, m - 1].bitcast(F32),
                                          ALU.subtract).then_inc(moe.h_low.sem, 1)

            def accumulate(i, k):
                u, us, e, slot, c = moe_place(i, k)
                if c == 0:
                    dve.wait_ge(moe.cwe.sem, e + 1)
                for t in range(4):
                    wait_done(dve, moe.down, 4 * u + t)
                    if not (isinstance(u, int) and u < CHUNKS):
                        dve.wait_ge(moe.acc.sem, 4 * u + t + 1 - 4 * CHUNKS)
                    q = 4 * c + t
                    dve.scalar_tensor_tensor(out=X[:, q], in0=ps[:, 4 + t, 0:D], scalar=cwe[:, slot, q:q + 1], in1=X[:, q],
                                             op0=ALU.mult, op1=ALU.add).then_inc(moe.acc.sem, 1)

            pipelined(dve, E // 2, 2 * CHUNKS, [(gated, 0), (accumulate, 1)])

        def split_first_act():
            nc.scalar.wait_ge(ld.expert0.sem, 16)
            nc.scalar.activation(w_parts[0][:, 0], raw[0], ACT.Copy).then_inc(moe.w_high.sem, 1)

        def split_first_dve():
            nc.vector.wait_ge(moe.w_high.sem, 1)
            nc.vector.tensor_tensor(w_parts[0][:, 1], raw[0], w_parts[0][:, 0].bitcast(F32), ALU.subtract).then_inc(moe.w_low.sem, 1)

        def split_expert(e):
            pool = nc.gpsimd
            pool.wait_ge((ld.expert0, ld.expert1)[e % 2].sem, 16 * (e // 2) + 16)
            pool.tensor_copy(w_parts[e % 2][:, 0], raw[e % 2]).then_inc(moe.w_high.sem, 1)
            pool.wait_ge(moe.w_high.sem, e + 1)
            pool.tensor_tensor(w_parts[e % 2][:, 1], raw[e % 2], w_parts[e % 2][:, 0].bitcast(F32), ALU.subtract).then_inc(moe.w_low.sem, 1)

        def moe_pool():
            pool = nc.gpsimd
            pool.wait_ge(moe.cw.sem, 1)
            for e in range(E):
                if e >= 2:
                    pool.wait_ge(moe.acc.sem, 4 * CHUNKS * (e - 1))
                pool.tensor_copy(cwe[:, e % 2], cw[:, e]).then_inc(moe.cwe.sem, 1)
                if e + 1 < E:
                    split_expert(e + 1)

        norm = named(stats=Signal(moe.top.sem, PAIRS), aggr=Signal(moe.idx.sem, PAIRS), eps=Signal(moe.gap.sem, 1),
                     rstd=Signal(moe.ex.sem, 1), x=Signal(lin.s.an.sem, PAIRS), xtr=Signal(lin.s.atr.sem, PAIRS),
                     xe=Signal(lin.s.anT.sem, PAIRS))
        norm_stats = stat[:, 0:PAIRS * 6].rearrange("p (t n) -> p t n", t=PAIRS)
        norm_moments = stat[:, 96:96 + 2 * PAIRS].rearrange("p (t n) -> p t n", t=PAIRS)
        norm_rstd = stat[:, 128:128 + PAIRS]

        def norm_dve():
            dve = nc.vector
            for p in range(PAIRS):
                dve.bn_stats(norm_stats[:, p], X[:, p, :]).then_inc(norm.stats.sem, 1)
            for p in range(PAIRS):
                dve.wait_ge(norm.stats.sem, norm.stats.base + p + 1)
                dve.bn_aggr(norm_moments[:, p], norm_stats[:, p]).then_inc(norm.aggr.sem, 1)
            dve.wait_ge(norm.aggr.sem, norm.aggr.base + PAIRS)
            dve.tensor_scalar(norm_rstd, norm_moments[:, :, 1], LN_EPS, None, ALU.add).then_inc(norm.eps.sem, 1)
            dve.wait_ge(norm.rstd.sem, norm.rstd.base + 1)
            for p in range(PAIRS):
                dve.tensor_scalar(X[:, p, :], X[:, p, :], norm_moments[:, p, 0:1], norm_rstd[:, p:p + 1], ALU.subtract,
                                  ALU.mult).then_inc(norm.x.sem, 1)

        def norm_pool():
            nc.gpsimd.wait_ge(norm.eps.sem, norm.eps.base + 1)
            nc.gpsimd.tensor_tensor(norm_rstd, norm_rstd, T.negsq.broadcast_to([P, PAIRS]), ALU.pow).then_inc(norm.rstd.sem, 1)

        def norm_pe():
            for n in range(PAIRS // 2):
                for q in range(2):
                    nc.tensor.wait_ge(norm.x.sem, norm.x.base + 2 * n + q + 1)
                    for kc in range(KC):
                        at0 = kc * 2 * P + q * P
                        mm = nc.tensor.transpose(ps[:, n, at0:at0 + P], X[:, 2 * n + q, kc * P:(kc + 1) * P], T.ident)
                mm.then_inc(norm.xtr.sem, 1)

        def norm_act():
            for n in range(PAIRS // 2):
                nc.scalar.wait_ge(norm.xtr.sem, norm.xtr.base + n + 1)
                nc.scalar.activation(XT[:, :, 2 * n * P:2 * (n + 1) * P], ps[:, n, :].rearrange("p (k t) -> p k t", k=KC),
                                     ACT.Copy).then_inc(norm.xe.sem, 1)

        fold = named(**signals_of("fold", "psum act dve kv"), low=Signal(lin.s.low.sem, PAIRS),
                     x_high=Signal(lin.s.kb.sem, PAIRS), x_low=Signal(lin.s.vb.sem, PAIRS))
        lw = part(big, LATENT)
        fold_q = mid_r[:, :].rearrange("p (a k n) -> p a k n", a=2, k=KC)
        fold_s = [v.rearrange("p (g x n c) -> p g x n c", g=4, x=2, n=4)
                  for v in (big_r[:, 0:4096], big_r[:, 6144:10240])]
        fold_s_full = big[:, 6144:10240].rearrange("p (g x n c) -> p g x n c", g=4, x=2, n=4)
        TILE_PAIRS = [(0, 0), (1, 0), (1, 1), (2, 1)]
        steps = [("q", h, "dve") for h in range(H1)]
        steps += [("o", n, "act") for n in range(8)] + [("s", n, "dve") for n in range(8)]

        def copied_through(n):
            who = steps[n][2]
            return (fold.act, n + 1) if who == "act" else (fold.dve, sum(s[2] == who for s in steps[:n + 1]))

        def fold_pe():
            pe = nc.tensor
            pe.wait_ge(ld.latent.sem, 16)
            for n, (kind, at0, who) in enumerate(steps):
                if n >= 8:
                    sem, count = copied_through(n - 8)
                    pe.wait_ge(sem.sem, count)
                bank = ps[:, n % 8, :]
                if kind == "q":
                    for kc in range(KC):
                        mm = pe.matmul(bank[:, kc * QC:(kc + 1) * QC], lw.wq[:, at0 * D + kc * P:at0 * D + (kc + 1) * P],
                                       lw.wkcq[:, at0 * QC:(at0 + 1) * QC], start=True, stop=True)
                elif kind == "s":
                    g, x = at0 // 2, at0 % 2
                    for m, (t, pair) in enumerate(TILE_PAIRS):
                        row = x * H1 * QH + (3 * g + t) * P
                        mm = pe.matmul(bank[:, m * P:(m + 1) * P], lw.wqr[0:KV, row:row + P],
                                       lw.wkr[0:KV, (4 * g + 2 * pair) * KV:(4 * g + 2 * pair + 2) * KV], start=True, stop=True)
                else:
                    c, hp = at0 // 4, at0 % 4
                    for x in range(2):
                        h = 2 * (2 * hp + x) + c
                        mm = pe.matmul(bank[64 * x:64 * x + 64, 0:D], lw.wkckv[:, h * KV:(h + 1) * KV], lw.wo[:, h * D:(h + 1) * D],
                                       start=True, stop=True)
                mm.then_inc(fold.psum.sem, 1)

        def fold_copies_act():
            act = nc.scalar
            for n, (kind, at0, by) in enumerate(steps):
                bank = ps[:, n % 8, :]
                if kind == "q":
                    act.wait_ge(fold.psum.sem, n + 1)
                    dst = mid_r[:, 0:6144].rearrange("p (k x n) -> p k x n", k=KC, x=2)[:, :, :, at0 * QH:(at0 + 1) * QH]
                    act.activation(dst, bank[:, 0:KC * QC].rearrange("p (k x n) -> p k x n", k=KC, x=2), ACT.Copy).then_inc(fold.act.sem, 1)
                elif kind == "s":
                    act.wait_ge(fold.dve.sem, H1 + at0 + 1)
                    act.activation(fold_s[0][:, at0 // 2, at0 % 2], fold_s_full[:, at0 // 2, at0 % 2], ACT.Copy).then_inc(fold.act.sem, 1)
                else:
                    act.wait_ge(fold.psum.sem, n + 1)
                    act.activation(fold_o[:, at0], bank[:, 0:D], ACT.Copy).then_inc(fold.act.sem, 1)

        def fold_copies_dve():
            dve = nc.vector
            for n, (kind, at0, by) in enumerate(steps):
                bank = ps[:, n % 8, :]
                if kind == "q":
                    dve.wait_ge(fold.act.sem, n + 1)
                    parts = [mid_r[:, a * 6144:(a + 1) * 6144].rearrange("p (k x n) -> p k x n", k=KC, x=2)[:, :, :, at0 * QH:(at0 + 1) * QH]
                             for a in range(2)]
                    dve.tensor_tensor(parts[1], bank[:, 0:KC * QC].rearrange("p (k x n) -> p k x n", k=KC, x=2),
                                      parts[0].bitcast(F32), ALU.subtract).then_inc(fold.dve.sem, 1)
                elif kind == "s":
                    dve.wait_ge(fold.psum.sem, n + 1)
                    dve.tensor_tensor(fold_s_full[:, at0 // 2, at0 % 2].rearrange("p n (x c) -> p (n x) c", x=2),
                                      bank.rearrange("p (m c) -> p m c", m=8), T.mask_fold[:, :, None].broadcast_to([P, 8, KV]),
                                      ALU.mult).then_inc(fold.dve.sem, 1)

        def fold_low_pool():
            for at0 in range(8):
                nc.gpsimd.wait_ge(fold.act.sem, H1 + 8 + at0 + 1)
                nc.gpsimd.tensor_tensor(fold_s[1][:, at0 // 2, at0 % 2], fold_s_full[:, at0 // 2, at0 % 2],
                                        fold_s[0][:, at0 // 2, at0 % 2].bitcast(F32), ALU.subtract).then_inc(fold.low.sem, 1)

        def chunk(n):
            return slice(n * GT, (n + 1) * GT)

        def split_x_act():
            for n in range(TOK // GT):
                nc.scalar.activation(x_high[:, :, chunk(n)], XT[:, :, chunk(n)], ACT.Copy).then_inc(fold.x_high.sem, 1)

        def split_x_pool():
            for n in range(TOK // GT):
                nc.gpsimd.wait_ge(fold.x_high.sem, fold.x_high.base + n + 1)
                nc.gpsimd.tensor_tensor(XT_r[:, :, chunk(n)], XT[:, :, chunk(n)], x_high[:, :, chunk(n)].bitcast(F32),
                                        ALU.subtract).then_inc(fold.x_low.sem, 1)

        def rotate_kv_dve():
            dve = nc.vector
            t1 = work[:, 0:1024].rearrange("p (t n) -> p t n", t=PAIRS)
            t2 = work[:, 1024:2048].rearrange("p (t n) -> p t n", t=PAIRS)
            dve.tensor_tensor(t1, ctx_tok[:, :, :], T.cos64[:, None, :].broadcast_to([P, PAIRS, KV]), ALU.mult).then_inc(fold.kv.sem, 1)
            for x in range(2):
                dst, src = slice(32 * x, 32 * x + 32), slice(32 - 32 * x, 64 - 32 * x)
                dve.tensor_tensor(t2[:, :, dst], ctx_tok[:, :, src], T.sin64[:, None, dst].broadcast_to([P, PAIRS, 32]),
                                  ALU.mult).then_inc(fold.kv.sem, 1)
            dve.wait_ge(fold.kv.sem, 3)
            dve.tensor_tensor(ctx_tok[:, :, :], t1, t2, ALU.add).then_inc(fold.kv.sem, 1)

        turned = work[:, 0:4096].rearrange("p (b n t) -> p b n t", b=2, n=4)
        x_high = work_r[:, 4096:8192].rearrange("p (k t) -> p k t", k=KC)
        outgoing = work[:, 8704:9728].rearrange("p (b t) -> p b t", b=2)
        rotated = big_r[:, 10240:16384].rearrange("p (a n x t) -> p a n x t", a=2, n=3, x=2)
        rope_q = T.rope_q.rearrange("p (n t s) -> p n t s", n=4, t=3)

        def query_pe():
            pe = nc.tensor

            def make(i, k):
                u = 4 * i + k
                if k == 0:
                    pe.wait_ge(fold.x_low.sem, fold.x_low.base + i + 1)
                for t in range(3):
                    j = 3 * u + t
                    wait_freed(pe, qry.mult, j, 3)
                    for x in range(2):
                        for y, (a, b) in enumerate(PRODUCTS):
                            for kc in range(KC):
                                at0 = x * H1 * QH + (3 * k + t) * P
                                mm = pe.matmul(ps[:, 2 * t + x, :], fold_q[:, a, kc, at0:at0 + P],
                                               (x_high, XT_r)[b][:, kc, bass.ds(i * GT, GT)], start=y + kc == 0, stop=y + kc == 3)
                    mm.then_inc(qry.q.sem, 1)

            def to_keys(i, k):
                u = 4 * i + k
                wait_freed(pe, qry.out, u, 1, 2)
                for pair in range(2):
                    pe.wait_ge(qry.low.sem, qry.low.base + 3 * u + 2 + pair)
                    terms = [(x, m, t) for m, (t, q) in enumerate(TILE_PAIRS) if q == pair for x in range(2)]
                    for n, (x, m, t) in enumerate(terms):
                        for y, (a, b) in enumerate(PRODUCTS):
                            mm = pe.matmul(ps[:, 6 + pair, :], fold_s[a][:, k, x, m], rotated[:, b, t, x], start=n + y == 0,
                                           stop=n + y == 5)
                    mm.then_inc(qry.t.sem, 1)

            pipelined(pe, TOK // GT, 4, [(make, 0), (to_keys, 1)])

        def wait_rotated_freed(eng, u, t):
            if not (isinstance(u, int) and u < 1):
                eng.wait_ge(qry.t.sem, 2 * u - (1 if t == 0 else 0))

        def query_dve():
            dve = nc.vector

            def low(u, t, b):
                wait_rotated_freed(dve, u, t)
                wait_done(dve, qry.high, 3 * u + t)
                dve.tensor_tensor(rotated[:, 1, t], turned[:, b, 0::2], rotated[:, 0, t].bitcast(F32), ALU.subtract).then_inc(qry.low.sem, 1)

            def mult(i, k):
                u = 4 * i + k
                for t in range(3):
                    j = 3 * u + t
                    b = (3 * k + t) % 2
                    wait_done(dve, qry.q, j)
                    wait_freed(dve, qry.low, j, 2)
                    for n, x in enumerate((0, 1, 1, 0)):
                        table = rope_q[:, (0, 1, 2, 3)[n], t, None, :].broadcast_to([P, GT // S, S])
                        ins = dve.tensor_tensor(turned[:, b, n].rearrange("p (b s) -> p b s", s=S),
                                                ps[:, 2 * t + x, :].rearrange("p (b s) -> p b s", s=S), table, ALU.mult)
                    ins.then_inc(qry.mult.sem, 1)
                    if t:
                        low(u, t - 1, 1 - b)
                    elif not (isinstance(u, int) and u < 1):
                        low(u - 1, 2, 1 - b)

            pipelined(dve, TOK // GT, 4, [(mult, 0)])
            low(4 * (TOK // GT) - 1, 2, (3 * 3 + 2) % 2)

        def query_pool():
            pool = nc.gpsimd

            def combine(i, k):
                u = 4 * i + k
                for t in range(3):
                    j = 3 * u + t
                    b = (3 * k + t) % 2
                    wait_done(pool, qry.mult, j)
                    pool.tensor_tensor(turned[:, b, 0], turned[:, b, 0], turned[:, b, 1], ALU.subtract)
                    pool.tensor_tensor(turned[:, b, 2], turned[:, b, 2], turned[:, b, 3], ALU.add).then_inc(qry.add.sem, 1)

            pipelined(pool, TOK // GT, 4, [(combine, 0)])

        def query_act():
            act = nc.scalar

            def high(i, k):
                u = 4 * i + k
                for t in range(3):
                    b = (3 * k + t) % 2
                    wait_rotated_freed(act, u, t)
                    wait_done(act, qry.add, 3 * u + t)
                    act.activation(rotated[:, 0, t], turned[:, b, 0::2], ACT.Copy).then_inc(qry.high.sem, 1)

            def copy(i, k):
                u = 4 * i + k
                for pair in range(2):
                    wait_done(act, qry.t, 2 * u + pair)
                    wait_freed(act, qry.sent[pair], u, 1, 16)
                    act.activation(outgoing[:, pair], ps[:, 6 + pair, :], ACT.Copy).then_inc(qry.out.sem, 1)

            pipelined(act, TOK // GT, 4, [(copy, 1), (high, 0)])

        def query_sync():
            sp = nc.sync
            for u in range(4 * (TOK // GT)):
                for pair in range(2):
                    sp.wait_ge(qry.out.sem, 2 * u + pair + 1)
                    at0 = u // 4 * GT
                    sp.dma_start(q_lat[:, 2 * (u % 4) + pair, at0:at0 + GT], outgoing[:, pair]).then_inc(qry.sent[pair].sem, 16)
            for n in range(2):
                wait_done(sp, qry.sent[n], 4 * (TOK // GT) - 1, 16)
            for p in range(PAIRS):
                wait_freed(sp, latent.s.scored, p, 2)
                sp.dma_start(qts[:, p % 2], q_lat[:, :, p * P:(p + 1) * P]).then_inc(qry.back[p % 2].sem, 16)
                if p == 1:
                    sp.dma_start(mid[:, 0:4096], dram["ffn"]).then_inc(ld.ffn.sem, 16)

        SUMS_AT = 2
        tern = sems("tern", "sums total mean inv scaled rounded up down gs")
        fw = part(mid, FFN)
        up_q = XT[:, 0, 0:KC * HID // 2].bitcast(BF16)
        tst = sbuf("tst", [P, 8])
        xq_t = sbuf("xq_t", [P, 2, KC, P], BF16)
        gs = small[:, pieces(SMALL)[0]["f_gamma"][0]:pieces(SMALL)[0]["f_gamma"][1]]

        def ternary_dve(i, k):
            u, dve = 2 * i + k, nc.vector
            if not isinstance(u, int):
                return

            def divide(n):
                w = (fw.up, fw.down)[n]
                dve.tensor_scalar(w, w, tst[:, 4 + n:5 + n], ROUND, ALU.mult, ALU.add).then_inc(tern.scaled.sem, 1)

            def clip(n):
                w = (fw.up, fw.down)[n]
                dve.wait_ge(tern.scaled.sem, n + 1)
                dve.tensor_scalar(w, w, ROUND, 1.0, ALU.subtract, ALU.min).then_inc(tern.rounded.sem, 1)
                dve.wait_ge(tern.rounded.sem, n + 1)
                dve.tensor_scalar((up_q, down_q)[n], w, -1.0, None, ALU.max).then_inc((tern.up, tern.down)[n].sem, 1)

            if u == SUMS_AT:
                dve.wait_ge(ld.ffn.sem, 16)
                for n, w in enumerate((fw.up, fw.down)):
                    dve.tensor_reduce(tst[:, n:n + 1], w, AX.X, ALU.add, apply_absolute_value=True).then_inc(tern.sums.sem, 1)
            if u == SUMS_AT + 1:
                dve.wait_ge(tern.total.sem, 1)
                dve.tensor_scalar(tst[:, 2:4], ps[:, 5, 0:2], 1.0 / (D * HID), 1e-8, ALU.mult, ALU.max).then_inc(tern.mean.sem, 1)
                dve.wait_ge(tern.mean.sem, 1)
                dve.reciprocal(tst[:, 4:6], tst[:, 2:4]).then_inc(tern.inv.sem, 1)
                dve.tensor_scalar(gs, SM.f_gamma, tst[:, 3:4], None, ALU.mult).then_inc(tern.gs.sem, 1)
                dve.wait_ge(tern.inv.sem, 1)
                divide(0)
            if u == SUMS_AT + 2:
                clip(0)
                divide(1)
            if u == SUMS_AT + 3:
                clip(1)

        def ternary_pe(i, k):
            u, pe = 2 * i + k, nc.tensor
            if isinstance(u, int) and u == SUMS_AT + 1:
                pe.wait_ge(tern.sums.sem, 2)
                wait_done(pe, latent.s.k, u)
                pe.matmul(ps[:, 5, 0:2], ones[:, :], tst[:, 0:2], start=True, stop=True).then_inc(tern.total.sem, 1)

        ffn_pT = big_r[:, 0:4096].rearrange("p (b x n t) -> p b x n t", b=2, x=2, n=8)
        down_q = mid_r[:, KC * HID:KC * HID + HID // P * D]

        def run_ffn(eng, stages):
            pipelined(eng, PAIRS // 4, 4, [((lambda i, k, f=f: f(4 * i + k, k % 2, k)), lag) for f, lag in stages], margin=4)

        def ffn_act():
            s, act = ffn.s, nc.scalar

            def square(p, slot, quad):
                wait_freed(act, s.xo, p, 2)
                act.activation(xo[:, slot], X[:, p, :], ACT.Square, accum_out=stat_cols(slot, 12)).then_inc(s.ss.sem, 1)

            def copy_x(p, slot, quad):
                wait_done(act, s.xtr, p)
                wait_freed(act, s.scored, p, 2)
                act.activation(xq_t[:, slot], ps[:, 5, 0:256].rearrange("p (k t) -> p k t", k=KC), ACT.Copy).then_inc(s.xe.sem, 1)

            def gate(p, slot, quad):
                wait_done(act, s.scored, p)
                wait_done(act, s.part, p)
                wait_freed(act, s.pt1, p, 2)
                for n in range(2):
                    ins = act.activation(sd[:, slot, n * 512:(n + 1) * 512], ps[:, n, :], ACT.Silu, scale=stat_cols(quad, 20))
                ins.then_inc(s.exped.sem, 1)

            def high_part(p, slot, quad):
                wait_freed(act, s.o, p, 2)
                for half, full in enumerate((s.pt0, s.pt1)):
                    wait_done(act, full, p)
                    act.activation(ffn_pT[:, slot, 0, 4 * half:4 * half + 4], ps[:, 2 + half, :].rearrange("p (n t) -> p n t", n=4),
                                   ACT.Copy).then_inc(s.ptc0.sem, 1)

            run_ffn(act, [(gate, 3), (copy_x, 2), (high_part, 4), (square, 0)])

        def ffn_pool():
            run_ffn(nc.gpsimd, [(lambda p, slot, quad: pool_rstd(ffn, p, slot), 6),
                                (lambda p, slot, quad: pool_rms(ffn, p, slot), 0),
                                (lambda p, slot, quad: pool_store_x(ffn, p, slot, p), 6)])

        def ffn_dve():
            s, dve = ffn.s, nc.vector
            xw = wk.xe.rearrange("p (b n) -> p b n", b=2)

            def mean_square(p, slot, quad):
                dve_mean_square(named(s=s, rms=1e-6), p, slot)

            def quantize(p, slot, quad):
                wait_done(dve, s.rr, p)
                wait_freed(dve, s.q1, p, 2)
                dve.scalar_tensor_tensor(out=xw[:, slot], in0=X[:, p, :], scalar=stat_cols(slot, 14), in1=SM.f_nw, op0=ALU.mult,
                                         op1=ALU.mult).then_inc(s.xw.sem, 1)
                wait_done(dve, s.xw, p)
                dve.tensor_reduce(stat_cols(slot, 16), xw[:, slot], AX.X, ALU.max, apply_absolute_value=True).then_inc(s.amax.sem, 1)
                wait_done(dve, s.amax, p)
                dve.tensor_scalar(stat_cols(slot, 17), stat_cols(slot, 16), 1e-8, None, ALU.max).then_inc(s.gam.sem, 1)
                wait_done(dve, s.gam, p)
                wait_freed(dve, s.exped, p, 4)
                dve.reciprocal(stat_cols(slot, 18), stat_cols(slot, 17)).then_inc(s.inv_gam.sem, 1)
                dve.tensor_scalar(stat_cols(quad, 20), stat_cols(slot, 17), 1.0 / 127.0, tst[:, 2:3], ALU.mult,
                                  ALU.mult).then_inc(s.part.sem, 1)
                wait_done(dve, s.inv_gam, p)
                dve.tensor_scalar(xw[:, slot], xw[:, slot], 127.0, stat_cols(slot, 18), ALU.mult, ALU.mult).then_inc(s.q1.sem, 1)
                wait_done(dve, s.q1, p)
                dve.tensor_scalar(xw[:, slot], xw[:, slot], ROUND, ROUND, ALU.add, ALU.subtract).then_inc(s.q2.sem, 1)
                wait_done(dve, s.q2, p)
                wait_freed(dve, s.xtr, p, 2)
                dve.tensor_scalar(xo[:, slot], xw[:, slot], 127.0, -127.0, ALU.min, ALU.max).then_inc(s.xo.sem, 1)

            def low_part(p, slot, quad):
                for half in range(2):
                    dve.wait_ge(s.ptc0.sem, s.ptc0.base + 2 * p + half + 1)
                    high = ffn_pT[:, slot, 0, 4 * half:4 * half + 4]
                    dve.tensor_tensor(ffn_pT[:, slot, 1, 4 * half:4 * half + 4], ps[:, 2 + half, :].rearrange("p (n t) -> p n t", n=4),
                                      high.bitcast(F32), ALU.subtract).then_inc(s.ptc1.sem, 1)

            def add(p, slot, quad):
                wait_done(dve, s.o, p)
                wait_freed(dve, s.x_stored, p, 2)
                dve.tensor_tensor(xn[:, slot], ps[:, 7, 0:D], gs, ALU.mult).then_inc(s.down.sem, 1)
                wait_done(dve, s.down, p)
                dve.scalar_tensor_tensor(out=xn[:, slot], in0=X[:, p, :], scalar=2.0, in1=xn[:, slot], op0=ALU.mult,
                                         op1=ALU.add).then_inc(s.y.sem, 1)
                dve_norm_stats(ffn, p, slot)

            run_ffn(dve, [(add, 6), (quantize, 1), (low_part, 4), (lambda p, slot, quad: dve_norm(ffn, p, slot), 6), (mean_square, 0)])

        def ffn_pe():
            s, pe = ffn.s, nc.tensor
            pe.wait_ge(tern.up.sem, 1)
            pe.wait_ge(tern.down.sem, 1)

            def turn_x(p, slot, quad):
                wait_done(pe, s.xo, p)
                wait_freed(pe, s.xe, p, 1)
                for kc in range(KC):
                    mm = pe.transpose(ps[:, 5, kc * P:(kc + 1) * P], xo[:, slot, kc * P:(kc + 1) * P], T.ident)
                mm.then_inc(s.xtr.sem, 1)

            def up(p, slot, quad):
                wait_done(pe, s.xe, p)
                wait_freed(pe, s.exped, p, 1)
                for n in range(2):
                    for kc in range(KC):
                        mm = pe.matmul(ps[:, n, :], xq_t[:, slot, kc], up_q[:, kc * HID + n * 512:kc * HID + (n + 1) * 512],
                                       start=kc == 0, stop=kc == 1)
                mm.then_inc(s.scored.sem, 1)

            def turn(p, slot, quad):
                wait_done(pe, s.exped, p)
                for half, full in ((0, s.pt0), (1, s.pt1)):
                    if not (isinstance(p, int) and p < 1):
                        pe.wait_ge(s.ptc1.sem, s.ptc1.base + 2 * p - 1 + half)
                    for n in range(4):
                        mm = pe.transpose(ps[:, 2 + half, n * P:(n + 1) * P], sd[:, slot, (4 * half + n) * P:(4 * half + n + 1) * P],
                                          T.ident)
                    mm.then_inc(full.sem, 1)

            def down(p, slot, quad):
                wait_done(pe, s.ptc1, p, 2)
                wait_freed(pe, s.y, p, 1)
                for n in range(8):
                    for x in range(2):
                        mm = pe.matmul(ps[:, 7, 0:D], ffn_pT[:, slot, x, n], down_q[:, n * D:(n + 1) * D],
                                       start=n + x == 0, stop=n + x == 8)
                mm.then_inc(s.o.sem, 1)

            run_ffn(pe, [(up, 3), (turn_x, 2), (turn, 4), (down, 5)])

        block = ctx.enter_context(nc.Block())

        @block.sync
        def _(sp):
            x_rows, x_cols = dram["x"].rearrange("(t p) c -> p t c", p=P), dram["x_t"].rearrange("p (k t) -> p k t", k=KC)
            sp.dma_start(ctx_tok[:, :, :], dram["ctx"].rearrange("(t p) c -> p t c", p=P)).then_inc(ld.ctx.sem, 16)
            sp.dma_start(tables[:, :], dram["tables"]).then_inc(ld.tables.sem, 16)
            sp.dma_start(small[:, :], dram["small"]).then_inc(ld.small.sem, 16)
            sp.dma_start(XT[:, :, 0:FIRST * P], x_cols[:, :, 0:FIRST * P]).then_inc(ld.xt0.sem, 16)
            sp.dma_start(big[:, 0:2048], dram["early"][:, 0:2048]).then_inc(ld.early0.sem, 16)
            sp.dma_start(X[:, 0:FIRST], x_rows[:, 0:FIRST]).then_inc(ld.x0.sem, 16)
            sp.dma_start(XT[:, :, FIRST * P:], x_cols[:, :, FIRST * P:]).then_inc(ld.xt.sem, 16)
            sp.dma_start(X[:, FIRST:], x_rows[:, FIRST:]).then_inc(ld.x.sem, 16)
            sp.dma_start(big[:, 2048:4624], dram["early"][:, 2048:]).then_inc(ld.early.sem, 16)
            sp.dma_start(big[:, 12288:12800], dram["causal"]).then_inc(ld.causal.sem, 16)
            sp.dma_start(raw[0], dram["experts"][0]).then_inc(ld.expert0.sem, 16)
            wait_sublayer(sp, cross)
            for e in range(1, E):
                if e >= 2:
                    sp.wait_ge(moe.down.sem, 4 * CHUNKS * (e - 1))
                sp.dma_start(raw[e % 2], dram["experts"][e]).then_inc((ld.expert0, ld.expert1)[e % 2].sem, 16)
            sp.wait_ge(moe.down.sem, 4 * CHUNKS * E)
            sp.dma_start(mid[:, 0:1920], dram["l1a"]).then_inc(ld.l1a.sem, 16)
            sp.dma_start(big[:, :], dram["latent"]).then_inc(ld.latent.sem, 16)
            query_sync()
            y = out.rearrange("(t p) c -> p t c", p=P)
            for q in range(4):
                wait_done(sp, ffn.s.x_stored, 4 * q + 3)
                sp.dma_start(y[:, 4 * q:4 * q + 4], X[:, 4 * q:4 * q + 4, :]).then_inc(stored.y.sem, 16)
            sp.wait_ge(stored.y.sem, 64)

        @block.gpsimd
        def _(pool):
            pool.memset(ones[:, :], 1.0).then_inc(setup.ones.sem, 1)
            lin_pool()
            wait_sublayer(pool, lin)
            pool.wait_ge(prep.s.keys.sem, 1)
            pool.wait_ge(prep.s.rope_w.sem, 3)
            soft_pool(cross)
            wait_sublayer(pool, cross)
            soft_pool(causal_self)
            wait_sublayer(pool, causal_self)
            moe_pool()
            pool.wait_ge(moe.acc.sem, 16 * E)
            norm_pool()
            pool.wait_ge(norm.xe.sem, norm.xe.base + PAIRS // 2)
            soft_pool(grouped)
            wait_sublayer(pool, grouped)
            split_x_pool()
            fold_low_pool()
            pool.wait_ge(fold.kv.sem, 4)
            query_pool()
            pool.wait_ge(qry.out.sem, TOK // GT * 8)
            soft_pool(latent)
            wait_sublayer(pool, latent)
            ffn_pool()

        @block.tensor
        def _(pe):
            lin_pe()
            wait_sublayer(pe, lin)
            pe.wait_ge(ld.early.sem, 16)
            pe.wait_ge(setup.causal.sem, 1)
            pe.wait_ge(setup.ident.sem, 1)
            soft_pe(cross)
            wait_sublayer(pe, cross)
            soft_pe(causal_self)
            wait_sublayer(pe, causal_self)
            moe_pe()
            pe.wait_ge(moe.acc.sem, 16 * E)
            norm_pe()
            pe.wait_ge(norm.xe.sem, norm.xe.base + PAIRS // 2)
            pe.wait_ge(ld.l1a.sem, 16)
            soft_pe(grouped)
            wait_sublayer(pe, grouped)
            fold_pe()
            pe.wait_ge(fold.act.sem, H1 + 16)
            pe.wait_ge(fold.dve.sem, H1 + 8)
            pe.wait_ge(fold.low.sem, fold.low.base + 8)
            query_pe()
            pe.wait_ge(qry.out.sem, TOK // GT * 8)
            pe.wait_ge(setup.ones.sem, 1)
            soft_pe(latent)
            wait_sublayer(pe, latent)
            ffn_pe()

        @block.scalar
        def _(act):
            lin_act()
            wait_sublayer(act, lin)
            act.wait_ge(ld.causal.sem, ld.causal.base + 16)
            act.activation(causal[:, :], big[:, 12288:12800], ACT.Copy).then_inc(setup.causal.sem, 1)
            split_first_act()
            soft_act(cross)
            wait_sublayer(act, cross)
            soft_act(causal_self)
            wait_sublayer(act, causal_self)
            route_act()
            moe_act()
            act.wait_ge(moe.acc.sem, 16 * E)
            norm_act()
            soft_act(grouped)
            wait_sublayer(act, grouped)
            split_x_act()
            fold_copies_act()
            query_act()
            act.wait_ge(fold.kv.sem, 4)
            soft_act(latent)
            wait_sublayer(act, latent)
            ffn_act()

        @block.vector
        def _(dve):
            cross_keys_dve()
            lin_dve()
            wait_sublayer(dve, lin)
            split_first_dve()
            soft_dve(cross)
            wait_sublayer(dve, cross)
            soft_dve(causal_self)
            wait_sublayer(dve, causal_self)
            route_dve()
            dve.wait_ge(moe.cw.sem, 1)
            moe_dve()
            dve.wait_ge(moe.acc.sem, 16 * E)
            norm_dve()
            dve.wait_ge(norm.xe.sem, norm.xe.base + PAIRS // 2)
            soft_dve(grouped)
            wait_sublayer(dve, grouped)
            rotate_kv_dve()
            fold_copies_dve()
            dve.wait_ge(fold.kv.sem, 4)
            query_dve()
            dve.wait_ge(qry.out.sem, TOK // GT * 8)
            soft_dve(latent)
            wait_sublayer(dve, latent)
            dve.wait_ge(tern.gs.sem, 1)
            ffn_dve()



def halves(w):
    return w.reshape(-1, P, w.shape[1]).transpose(1, 0, 2).reshape(P, -1)


def columns(v):
    return v.reshape(-1, P).T


def rows(v):
    return np.broadcast_to(v[None, :], (P, v.shape[0]))


def pack(parts, widths):
    return np.ascontiguousarray(np.concatenate([parts[n].reshape(P, w) for n, w in widths], 1))


def top64(a):
    return np.concatenate([a, np.zeros_like(a)], 0)


def layouts(i):
    x = i["x"].reshape(TOK, D)
    small = {
        "l0_qb": columns(i["L0_attn_q_b"]), "l0_kvb": rows(np.concatenate([i["L0_attn_k_b"], i["L0_attn_v_b"]])),
        "l0_ob": rows(i["L0_attn_o_b"]), "x_qnw": rows(i["L0_xattn_q_norm_w"]), "x_knw": rows(i["L0_xattn_k_norm_w"]),
        "ln1": columns(i["L0_ffn_w_ln1"]), "ln2": columns(i["L0_ffn_w_ln2"]),
        "l1_ob": rows(i["L1_attn_b_out"]), "f_nw": rows(i["L1_ffn_norm_weight"]), "f_gamma": rows(i["L1_ffn_gamma"]),
    }
    w_qkv, b_qkv = i["L1_attn_w_qkv"], i["L1_attn_b_qkv"]
    acgd = np.arange(D).reshape(8, 2, 2, 8).transpose(1, 2, 0, 3).reshape(-1)
    small["l1_qb"] = columns(b_qkv[:D][acgd])
    small["l1_kb"] = np.concatenate([b_qkv[D:D + 64]] * 2)[:, None]
    small["l1_vb"] = rows(b_qkv[D + 64:])
    xo = i["L0_xattn_w_out"].T.reshape(4, 2, 2, 16, D).transpose(2, 1, 0, 3, 4).reshape(D, D)
    early = {
        "l0_q": halves(i["L0_attn_q_w"].T), "l0_kv": halves(np.concatenate([i["L0_attn_k_w"].T, i["L0_attn_v_w"].T], 1)),
        "l0_o": halves(i["L0_attn_o_w"].T), "x_o": halves(xo), "f_q": halves(i["L0_ffn_Wq"].T), "f_k": halves(i["L0_ffn_Wk"].T),
        "f_v": halves(i["L0_ffn_Wv"].T), "f_o": halves(i["L0_ffn_Wo"].T), "f_r": halves(i["L0_ffn_Wr"].T),
    }
    wo = i["L1_attn_w_out"].T.reshape(4, 2, 2, 2, 8, D).transpose(2, 3, 0, 1, 4, 5)
    wo = np.concatenate([wo.reshape(4, 4, 16, D), np.zeros((4, 4, 16, D), wo.dtype)], 2).reshape(4 * P, D)
    l1a = {"a_q": halves(w_qkv[:D][acgd].T), "a_k": halves(np.concatenate([w_qkv[D:D + 64]] * 2, 0).T),
           "a_v": halves(w_qkv[D + 64:].T), "a_o": halves(wo)}
    wqr = i["L1_xattn_W_qr"].reshape(H1, 2, QH, KV).transpose(3, 1, 0, 2).reshape(KV, -1)
    latent = {"wq": i["L1_xattn_Wq"].reshape(H1, P, D).transpose(1, 0, 2), "wkcq": i["L1_xattn_w_kc_q"].transpose(1, 0, 2),
              "wqr": top64(wqr), "wkr": top64(i["L1_xattn_W_kr"].transpose(2, 0, 1).reshape(KV, -1)),
              "wkckv": i["L1_xattn_w_kc_kv"].transpose(1, 0, 2), "wo": halves(i["L1_xattn_Wo"].T)}
    ffn = {"up": halves(i["L1_ffn_weight_up"].T), "down": halves(i["L1_ffn_weight_down"].T)}
    experts = [pack({"gate": halves(i["L0_ffn_Wg"][e].T), "up": halves(i["L0_ffn_Wu"][e].T),
                     "down": halves(i["L0_ffn_Wd"][e].T)}, EXPERT) for e in range(E)]
    return {
        "x": np.ascontiguousarray(x), "x_t": halves(np.ascontiguousarray(x.T)), "ctx": i["ctx_512"].reshape(TOK, DC),
        "tables": shape_tables(), "causal": causal_table(), "small": pack(small, SMALL), "early": pack(early, EARLY),
        "l1a": pack(l1a, L1A), "latent": pack(latent, LATENT), "ffn": pack(ffn, FFN), "experts": np.stack(experts, 0),
    }


def kernel(**inputs):
    import concourse.bacc as _bacc
    from concourse.bass_utils import run_bass_kernel_spmd as _run

    nc = _bacc.Bacc("TRN2", target_bir_lowering=False, num_devices=1)
    arrays = layouts({n: np.asarray(a) for n, a in inputs.items()})
    arrays = {n: np.ascontiguousarray(a) for n, a in arrays.items()}
    dram = {n: nc.dram_tensor(f"in_{n}", a.shape, mybir.dt.from_np(a.dtype), kind="ExternalInput").ap() for n, a in arrays.items()}
    out = nc.dram_tensor("out_x", (TOK, D), F32, kind="ExternalOutput").ap()
    decoder(nc, dram, out)
    r = _run(nc, [{f"in_{n}": a for n, a in arrays.items()}], core_ids=[0])
    return r.results[0]["out_x"].reshape(B, S, D)
```
